# Optimizing a Trainium2 kernel written in Bass

```python
import numpy as np
import jax
import jax.numpy as jnp

def _softmax(x, axis=-1):
    return jax.nn.softmax(x, axis=axis)

def _gelu(x):
    return jax.nn.gelu(x, approximate=True)

def _silu(x):
    return jax.nn.silu(x)

def _sigmoid(x):
    return jax.nn.sigmoid(x)

def _layernorm(x, axis=-1, eps=1e-05):
    m = jnp.mean(x, axis=axis, keepdims=True)
    v = jnp.var(x, axis=axis, keepdims=True)
    return (x - m) / jnp.sqrt(v + eps)

def _scatter_add(tgt, idx, src, axis=0):
    return tgt.at[idx].add(src)

def _segment_sum(src, seg, n):
    return jax.ops.segment_sum(src, seg, n)
kernel_name = 'mk_seq_preln_d2_jaxref_r8_f2e1db'

def setup_inputs(seed: int=0):
    np.random.seed(seed)
    _w = jnp.asarray

    def _L0_attn_setup():
        import jax, jax.numpy as jnp
        import numpy as np
        B, T, C = (32, 128, 128)
        N_LAYER, LAYER_ID, FIRST_SA = (12, 3, 1)
        RWKV_K_CLAMP = 60.0
        RWKV_K_EPS = 1e-16

        def _init_params():
            f1 = 3.0 + (LAYER_ID - FIRST_SA) / (N_LAYER - 1 - FIRST_SA) * (1.2 - 3.0)
            f2 = 0.65 + (LAYER_ID - FIRST_SA) / (N_LAYER - 1 - FIRST_SA) * (0.4 - 0.65)
            h = np.arange(C, dtype=np.float64)
            decay_speed = np.power(f2, h / (C - 1) * 7) * f1
            time_decay = np.log(decay_speed).astype(np.float32)
            time_first = np.full((C,), np.log(0.3), dtype=np.float32)
            tm = np.ones((C,), dtype=np.float32)
            tm[:C // 2] = 0.0
            return (jnp.asarray(time_decay), jnp.asarray(time_first), jnp.asarray(tm))

        def _wkv(decay, first_w, y, eps):
            a = jnp.broadcast_to(decay, y.shape)

            def comb(l, r):
                a1, b1 = l
                a2, b2 = r
                return (a1 * a2, a2 * b1 + b2)
            _, S = jax.lax.associative_scan(comb, (a, y), axis=1)
            S_prev = jnp.pad(S, ((0, 0), (1, 0), (0, 0)))[:, :-1]
            return eps + first_w * y + S_prev
        key = jax.random.key(seed)
        ks = jax.random.split(key, 5)
        x = jax.random.normal(ks[0], (B, T, C), dtype=jnp.float32)
        scale = 0.02
        Wk = jax.random.normal(ks[1], (C, C), dtype=jnp.float32) * scale
        Wv = jax.random.normal(ks[2], (C, C), dtype=jnp.float32) * scale
        Wr = jax.random.normal(ks[3], (C, C), dtype=jnp.float32) * scale
        Wo = jax.random.normal(ks[4], (C, C), dtype=jnp.float32) * scale
        time_decay, time_first, time_mix = _init_params()
        return {'x': x, 'time_decay': time_decay, 'time_first': time_first, 'time_mix': time_mix, 'Wk': Wk, 'Wv': Wv, 'Wr': Wr, 'Wo': Wo}
    _L0_attn_in = _L0_attn_setup()

    def _L0_ffn_setup():
        import jax, jax.numpy as jnp
        import numpy as np
        D = 128
        I = 64
        E = 32
        K = 4
        T = 2 * 256
        C = 2 * T * K // E
        key = jax.random.key(seed)
        ks = jax.random.split(key, 9)
        bf = jnp.bfloat16
        std = 0.02
        x = jax.random.normal(ks[0], (2, 256, D), dtype=jnp.float32).astype(bf)
        gate_w = (std * jax.random.normal(ks[1], (E, D), dtype=jnp.float32)).astype(bf)
        bias = jnp.zeros((E,), jnp.float32)
        W1 = (std * jax.random.normal(ks[2], (E, D, I), dtype=jnp.float32)).astype(bf)
        W3 = (std * jax.random.normal(ks[3], (E, D, I), dtype=jnp.float32)).astype(bf)
        W2 = (std * jax.random.normal(ks[4], (E, I, D), dtype=jnp.float32)).astype(bf)
        sw1 = (std * jax.random.normal(ks[5], (I, D), dtype=jnp.float32)).astype(bf)
        sw3 = (std * jax.random.normal(ks[6], (I, D), dtype=jnp.float32)).astype(bf)
        sw2 = (std * jax.random.normal(ks[7], (D, I), dtype=jnp.float32)).astype(bf)
        return {'x': x, 'gate_w': gate_w, 'bias': bias, 'W1': W1, 'W3': W3, 'W2': W2, 'sw1': sw1, 'sw3': sw3, 'sw2': sw2}
    _L0_ffn_in = _L0_ffn_setup()

    def _L1_attn_setup():
        import jax, jax.numpy as jnp
        import numpy as np
        EPS = 1e-12
        HEADS = 16
        DIM_KEYS = 16
        DIM_VALUES = 64

        def l2norm(t):
            n = jnp.linalg.norm(t, axis=-1, keepdims=True)
            return t / jnp.maximum(n, EPS)

        def tanh_norm(t):
            n = jnp.linalg.norm(t, axis=-1, keepdims=True)
            return jnp.tanh(n) * (t / jnp.maximum(n, EPS))

        def split_heads(x, h):
            b, n, hd = x.shape
            return x.reshape(b, n, h, hd // h).transpose(0, 2, 1, 3)
        key = jax.random.key(seed)
        k1, k2, k3, k4 = jax.random.split(key, 4)
        b, n, dim = (4, 256, 128)
        dim_inner = (DIM_KEYS + DIM_VALUES) * HEADS
        tokens = jax.random.normal(k1, (b, n, dim), dtype=jnp.float32)
        Wqg = jax.random.normal(k2, (dim, dim_inner), dtype=jnp.float32) * dim ** (-0.5)
        Wkv = jax.random.normal(k3, (dim, dim_inner), dtype=jnp.float32) * dim ** (-0.5)
        Wout = jax.random.normal(k4, (DIM_VALUES * HEADS, dim), dtype=jnp.float32) * (DIM_VALUES * HEADS) ** (-0.5)
        return {'tokens': tokens, 'Wqg': Wqg, 'Wkv': Wkv, 'Wout': Wout}
    _L1_attn_in = _L1_attn_setup()

    def _L1_ffn_setup():
        import jax, jax.numpy as jnp
        import numpy as np
        B, S, H, NH, E, F = (4, 128, 128, 16, 8, 512)
        D = H // NH
        EPS = 1e-05

        def _layernorm(x, g, b):
            mu = jnp.mean(x, axis=-1, keepdims=True)
            var = jnp.var(x, axis=-1, keepdims=True)
            return (x - mu) * jax.lax.rsqrt(var + EPS) * g + b
        key = jax.random.key(seed)
        ks = jax.random.split(key, 16)
        s = 0.02
        return {'x': jax.random.normal(ks[0], (B, S, H), jnp.float32), 'ln1_g': jnp.ones((H,), jnp.float32), 'ln1_b': jnp.zeros((H,), jnp.float32), 'ln2_g': jnp.ones((H,), jnp.float32), 'ln2_b': jnp.zeros((H,), jnp.float32), 'wq': jax.random.normal(ks[1], (H, H), jnp.float32) * s, 'bq': jnp.zeros((H,), jnp.float32), 'wk': jax.random.normal(ks[2], (H, H), jnp.float32) * s, 'bk': jnp.zeros((H,), jnp.float32), 'wv': jax.random.normal(ks[3], (H, H), jnp.float32) * s, 'bv': jnp.zeros((H,), jnp.float32), 'wo': jax.random.normal(ks[4], (H, H), jnp.float32) * s, 'bo': jnp.zeros((H,), jnp.float32), 'gate_w': jax.random.normal(ks[5], (H, E), jnp.float32) * s, 'gate_b': jnp.zeros((E,), jnp.float32), 'w1': jax.random.normal(ks[6], (E, H, F), jnp.float32) * s, 'b1': jnp.zeros((E, F), jnp.float32), 'w2': jax.random.normal(ks[7], (E, F, H), jnp.float32) * s, 'b2': jnp.zeros((E, H), jnp.float32)}
    _L1_ffn_in = _L1_ffn_setup()
    _d = {'L0_attn_x': _L0_attn_in['x'], 'L0_attn_time_decay': _L0_attn_in['time_decay'], 'L0_attn_time_first': _L0_attn_in['time_first'], 'L0_attn_time_mix': _L0_attn_in['time_mix'], 'L0_attn_Wk': _L0_attn_in['Wk'], 'L0_attn_Wv': _L0_attn_in['Wv'], 'L0_attn_Wr': _L0_attn_in['Wr'], 'L0_attn_Wo': _L0_attn_in['Wo'], 'L0_ffn_gate_w': _L0_ffn_in['gate_w'], 'L0_ffn_bias': _L0_ffn_in['bias'], 'L0_ffn_W1': _L0_ffn_in['W1'], 'L0_ffn_W3': _L0_ffn_in['W3'], 'L0_ffn_W2': _L0_ffn_in['W2'], 'L0_ffn_sw1': _L0_ffn_in['sw1'], 'L0_ffn_sw3': _L0_ffn_in['sw3'], 'L0_ffn_sw2': _L0_ffn_in['sw2'], 'L1_attn_Wqg': _L1_attn_in['Wqg'], 'L1_attn_Wkv': _L1_attn_in['Wkv'], 'L1_attn_Wout': _L1_attn_in['Wout'], 'L1_ffn_ln1_g': _L1_ffn_in['ln1_g'], 'L1_ffn_ln1_b': _L1_ffn_in['ln1_b'], 'L1_ffn_ln2_g': _L1_ffn_in['ln2_g'], 'L1_ffn_ln2_b': _L1_ffn_in['ln2_b'], 'L1_ffn_wq': _L1_ffn_in['wq'], 'L1_ffn_bq': _L1_ffn_in['bq'], 'L1_ffn_wk': _L1_ffn_in['wk'], 'L1_ffn_bk': _L1_ffn_in['bk'], 'L1_ffn_wv': _L1_ffn_in['wv'], 'L1_ffn_bv': _L1_ffn_in['bv'], 'L1_ffn_wo': _L1_ffn_in['wo'], 'L1_ffn_bo': _L1_ffn_in['bo'], 'L1_ffn_gate_w': _L1_ffn_in['gate_w'], 'L1_ffn_gate_b': _L1_ffn_in['gate_b'], 'L1_ffn_w1': _L1_ffn_in['w1'], 'L1_ffn_b1': _L1_ffn_in['b1'], 'L1_ffn_w2': _L1_ffn_in['w2'], 'L1_ffn_b2': _L1_ffn_in['b2']}
    _x0 = _d['L0_attn_x']
    _d['L0_attn_x'] = jax.random.normal(jax.random.fold_in(jax.random.key(seed), 1), (16, 256, 128), dtype=_x0.dtype)
    del _x0
    return _d

def reference(L0_attn_x, L0_attn_time_decay, L0_attn_time_first, L0_attn_time_mix, L0_attn_Wk, L0_attn_Wv, L0_attn_Wr, L0_attn_Wo, L0_ffn_gate_w, L0_ffn_bias, L0_ffn_W1, L0_ffn_W3, L0_ffn_W2, L0_ffn_sw1, L0_ffn_sw3, L0_ffn_sw2, L1_attn_Wqg, L1_attn_Wkv, L1_attn_Wout, L1_ffn_ln1_g, L1_ffn_ln1_b, L1_ffn_ln2_g, L1_ffn_ln2_b, L1_ffn_wq, L1_ffn_bq, L1_ffn_wk, L1_ffn_bk, L1_ffn_wv, L1_ffn_bv, L1_ffn_wo, L1_ffn_bo, L1_ffn_gate_w, L1_ffn_gate_b, L1_ffn_w1, L1_ffn_b1, L1_ffn_w2, L1_ffn_b2):

    def _L0_attn_ref(x, time_decay, time_first, time_mix, Wk, Wv, Wr, Wo):
        import jax, jax.numpy as jnp
        import numpy as np
        B, T, C = (32, 128, 128)
        N_LAYER, LAYER_ID, FIRST_SA = (12, 3, 1)
        RWKV_K_CLAMP = 60.0
        RWKV_K_EPS = 1e-16

        def _init_params():
            f1 = 3.0 + (LAYER_ID - FIRST_SA) / (N_LAYER - 1 - FIRST_SA) * (1.2 - 3.0)
            f2 = 0.65 + (LAYER_ID - FIRST_SA) / (N_LAYER - 1 - FIRST_SA) * (0.4 - 0.65)
            h = np.arange(C, dtype=np.float64)
            decay_speed = np.power(f2, h / (C - 1) * 7) * f1
            time_decay = np.log(decay_speed).astype(np.float32)
            time_first = np.full((C,), np.log(0.3), dtype=np.float32)
            tm = np.ones((C,), dtype=np.float32)
            tm[:C // 2] = 0.0
            return (jnp.asarray(time_decay), jnp.asarray(time_first), jnp.asarray(tm))

        def _wkv(decay, first_w, y, eps):
            a = jnp.broadcast_to(decay, y.shape)

            def comb(l, r):
                a1, b1 = l
                a2, b2 = r
                return (a1 * a2, a2 * b1 + b2)
            _, S = jax.lax.associative_scan(comb, (a, y), axis=1)
            S_prev = jnp.pad(S, ((0, 0), (1, 0), (0, 0)))[:, :-1]
            return eps + first_w * y + S_prev
        Bn, Tn, Cn = x.shape
        xs = jnp.pad(x, ((0, 0), (1, 0), (0, 0)))[:, :-1]
        xm = x * time_mix + xs * (1.0 - time_mix)
        k = xm @ Wk.T
        v = xm @ Wv.T
        r = xm @ Wr.T
        k = jnp.exp(jnp.minimum(k, RWKV_K_CLAMP))
        kv = k * v
        decay = jnp.exp(-jnp.exp(time_decay))
        first_w = jnp.exp(time_first)
        wkv = _wkv(decay, first_w, kv, 0.0)
        wk = _wkv(decay, first_w, k, RWKV_K_EPS)
        rwkv = jax.nn.sigmoid(r) * (wkv / wk)
        return rwkv @ Wo.T

    def _L0_ffn_ref(x, gate_w, bias, W1, W3, W2, sw1, sw3, sw2):
        import jax, jax.numpy as jnp
        import numpy as np
        D = 128
        I = 64
        E = 32
        K = 4
        T = 2 * 256
        C = 2 * T * K // E
        X = x.reshape(-1, D)
        logits = (X @ gate_w.T).astype(jnp.float32)
        scores = jax.nn.sigmoid(logits)
        _, idx = jax.lax.top_k(scores + bias[None, :], K)
        w = jnp.take_along_axis(scores, idx, axis=-1)
        w = w / jnp.clip(jnp.sum(w, axis=-1, keepdims=True), 1e-12, None)
        w = w.astype(x.dtype)
        eid = idx.reshape(-1)
        onehot = (eid[:, None] == jnp.arange(E)[None, :]).astype(jnp.int32)
        pos = jnp.take_along_axis(jnp.cumsum(onehot, axis=0) - 1, eid[:, None], axis=1)[:, 0]
        valid = pos < C
        posc = jnp.minimum(pos, C - 1)
        Xrep = jnp.repeat(X, K, axis=0)
        xe = jnp.zeros((E, C, D), x.dtype).at[eid, posc].add(jnp.where(valid[:, None], Xrep, jnp.zeros((), x.dtype)))
        h = jax.nn.silu(jnp.einsum('ecd,edi->eci', xe, W1)) * jnp.einsum('ecd,edi->eci', xe, W3)
        ye = jnp.einsum('eci,eid->ecd', h, W2)
        gflat = jnp.where(valid, w.reshape(-1), jnp.zeros((), x.dtype))
        yrows = ye[eid, posc] * gflat[:, None]
        out = yrows.reshape(-1, K, D).sum(axis=1)
        out = out + jax.nn.silu(X @ sw1.T) * (X @ sw3.T) @ sw2.T
        return out.reshape(x.shape)

    def _L1_attn_ref(tokens, Wqg, Wkv, Wout):
        import jax, jax.numpy as jnp
        import numpy as np
        EPS = 1e-12
        HEADS = 16
        DIM_KEYS = 16
        DIM_VALUES = 64

        def l2norm(t):
            n = jnp.linalg.norm(t, axis=-1, keepdims=True)
            return t / jnp.maximum(n, EPS)

        def tanh_norm(t):
            n = jnp.linalg.norm(t, axis=-1, keepdims=True)
            return jnp.tanh(n) * (t / jnp.maximum(n, EPS))

        def split_heads(x, h):
            b, n, hd = x.shape
            return x.reshape(b, n, h, hd // h).transpose(0, 2, 1, 3)
        qg = split_heads(tokens @ Wqg, HEADS)
        kv = split_heads(tokens @ Wkv, HEADS)
        queries, gates = (qg[..., :DIM_KEYS], qg[..., DIM_KEYS:])
        keys, values = (kv[..., :DIM_KEYS], kv[..., DIM_KEYS:])
        queries, keys, values = (l2norm(queries), l2norm(keys), l2norm(values))
        sim = jnp.einsum('bhid,bhjd->bhij', queries, keys)
        attn = jnp.square(jax.nn.relu(sim))
        aggr = jnp.einsum('bhij,bhjd->bhid', attn, values)
        out = tanh_norm(aggr) * jnp.tanh(jax.nn.silu(gates))
        b, h, n, d = out.shape
        out = out.transpose(0, 2, 1, 3).reshape(b, n, h * d)
        return out @ Wout

    def _L1_ffn_ref(x, ln1_g, ln1_b, ln2_g, ln2_b, wq, bq, wk, bk, wv, bv, wo, bo, gate_w, gate_b, w1, b1, w2, b2):
        import jax, jax.numpy as jnp
        import numpy as np
        B, S, H, NH, E, F = (4, 128, 128, 16, 8, 512)
        D = H // NH
        EPS = 1e-05

        def _layernorm(x, g, b):
            mu = jnp.mean(x, axis=-1, keepdims=True)
            var = jnp.var(x, axis=-1, keepdims=True)
            return (x - mu) * jax.lax.rsqrt(var + EPS) * g + b
        b, s, h = x.shape
        hn = _layernorm(x, ln1_g, ln1_b)
        q = (hn @ wq + bq).reshape(b, s, NH, D).transpose(0, 2, 1, 3)
        k = (hn @ wk + bk).reshape(b, s, NH, D).transpose(0, 2, 1, 3)
        v = (hn @ wv + bv).reshape(b, s, NH, D).transpose(0, 2, 1, 3)
        scores = jnp.einsum('bhqd,bhkd->bhqk', q, k) / jnp.sqrt(jnp.float32(D))
        attn = jax.nn.softmax(scores, axis=-1)
        o = jnp.einsum('bhqk,bhkd->bhqd', attn, v)
        o = o.transpose(0, 2, 1, 3).reshape(b, s, h)
        x = x + (o @ wo + bo)
        hn2 = _layernorm(x, ln2_g, ln2_b).reshape(-1, h)
        logits = hn2 @ gate_w + gate_b
        idx = jnp.argmax(logits, axis=-1)
        mid = jax.nn.relu(jnp.einsum('th,ehf->etf', hn2, w1) + b1[:, None, :])
        y = jnp.einsum('etf,efh->eth', mid, w2) + b2[:, None, :]
        moe = y[idx, jnp.arange(hn2.shape[0])]
        return x + moe.reshape(b, s, h)
    x = L0_attn_x
    x = x + _L0_attn_ref(_layernorm(x, axis=-1), L0_attn_time_decay, L0_attn_time_first, L0_attn_time_mix, L0_attn_Wk, L0_attn_Wv, L0_attn_Wr, L0_attn_Wo)
    x = x + _L0_ffn_ref(_layernorm(x, axis=-1), L0_ffn_gate_w, L0_ffn_bias, L0_ffn_W1, L0_ffn_W3, L0_ffn_W2, L0_ffn_sw1, L0_ffn_sw3, L0_ffn_sw2)
    x = x + _L1_attn_ref(_layernorm(x, axis=-1), L1_attn_Wqg, L1_attn_Wkv, L1_attn_Wout)
    x = x + _L1_ffn_ref(_layernorm(x, axis=-1), L1_ffn_ln1_g, L1_ffn_ln1_b, L1_ffn_ln2_g, L1_ffn_ln2_b, L1_ffn_wq, L1_ffn_bq, L1_ffn_wk, L1_ffn_bk, L1_ffn_wv, L1_ffn_bv, L1_ffn_wo, L1_ffn_bo, L1_ffn_gate_w, L1_ffn_gate_b, L1_ffn_w1, L1_ffn_b1, L1_ffn_w2, L1_ffn_b2)
    return x

_drawn_inputs = setup_inputs


def setup_inputs(seed=0):
    import zlib

    import numpy as np

    out = dict(_drawn_inputs(seed))
    spreads = {'L0_attn_time_first': (-1.2039728164672852, 0.6),
     'L0_ffn_bias': (0.0, 0.8),
     'L1_ffn_ln1_g': (1.0, 0.6),
     'L1_ffn_ln1_b': (0.0, 0.8),
     'L1_ffn_ln2_g': (1.0, 0.6),
     'L1_ffn_ln2_b': (0.0, 1.25),
     'L1_ffn_bq': (0.0, 0.8),
     'L1_ffn_bk': (0.0, 2.0),
     'L1_ffn_bv': (0.0, 0.454),
     'L1_ffn_bo': (0.0, 0.433),
     'L1_ffn_gate_b': (0.0, 0.337),
     'L1_ffn_b1': (0.0, 1.462),
     'L1_ffn_b2': (0.0, 0.442)}
    factors = {'L0_attn_time_decay': 5.7,
     'L0_attn_time_mix': 6.121,
     'L0_attn_Wk': 8.0,
     'L0_attn_Wv': 3.683,
     'L0_attn_Wr': 8.0,
     'L0_attn_Wo': 3.78,
     'L0_ffn_gate_w': 8.0,
     'L0_ffn_W1': 8.0,
     'L0_ffn_W3': 8.0,
     'L0_ffn_W2': 8.0,
     'L0_ffn_sw1': 8.0,
     'L0_ffn_sw3': 8.0,
     'L0_ffn_sw2': 8.0,
     'L1_ffn_wq': 8.0,
     'L1_ffn_wk': 8.0,
     'L1_ffn_wv': 8.0,
     'L1_ffn_wo': 3.713,
     'L1_attn_Wqg': 3.469,
     'L1_attn_Wkv': 3.371,
     'L1_attn_Wout': 3.345,
     'L1_ffn_w1': 4.163}
    for name, (base, spread) in spreads.items():
        noise = np.random.default_rng([zlib.crc32(name.encode()), seed]).standard_normal(out[name].shape)
        drawn = base * np.exp(spread * noise) if base else spread * noise
        out[name] = jnp.asarray(drawn.astype(out[name].dtype))
    for name, factor in factors.items():
        out[name] = (out[name] * factor).astype(out[name].dtype)
    return out
```

```python
from contextlib import ExitStack

import concourse.bass as bass
from concourse import mybir

F32 = mybir.dt.float32
BF16 = mybir.dt.bfloat16
F16 = mybir.dt.float16
U32 = mybir.dt.uint32
I32 = mybir.dt.int32
ALU = mybir.AluOpType
ACT = mybir.ActivationFunctionType
AX = mybir.AxisListType.X

P = 128
D = 128
BATCH, SEQ = 16, 256
TOK = BATCH * SEQ
LN_EPS = 1e-5

HEADS, DK, DV = 16, 16, 64
HALF = HEADS // 2
PAIRS = HEADS // 2
TERMS = 4

DH = 8
TERMS1 = 8
SCALE = float(DH) ** -0.5
E1, F1 = 8, 512
CHUNKS = F1 // P
BLOCKS = TOK // P + E1
NO_ROWS = E1 * TOK

E0, K0, CAP, I0 = 32, 4, 128, 64
SLOTS0 = E0 * CAP


class Chain:

    def __init__(self, engine, semaphore):
        self.engine, self.semaphore, self.count = engine, semaphore, 0

    def step(self, instruction):
        self.count += 1
        instruction.then_inc(self.semaphore, 1)
        return self.count

    def need(self, count):
        self.engine.wait_ge(self.semaphore, count)

    def restart(self):
        self.engine.wait_ge(self.semaphore, self.count)
        self.engine.sem_clear(self.semaphore)
        self.count = 0


class Seq:

    def __init__(self, turn, place):
        self.n, self.p, self.k = 2 * turn + place + 1, place % 2, turn + place // 2 + 1


def pipeline(eng, half, stages=4):
    def step(turn, at):
        work = [Seq(turn, at - lag) if not isinstance(turn, int) or 0 <= at - lag < BATCH else None
                for lag in range(stages)]
        half(*work)

    lead = stages - 1
    turns = (BATCH - lead) // 2
    for at in range(lead + 2):
        step(0, at)
    with eng.Fori(1, turns) as turn:
        step(turn, lead)
        step(turn, lead + 1)
    for at in range(lead + 2 * turns, BATCH + lead):
        step(0, at)


def repeat(eng, turns, turn):
    turn(0)
    with eng.Fori(1, turns) as i:
        turn(i)


def wait(eng, semaphore, value):
    if not isinstance(value, int) or value > 0:
        eng.wait_ge(semaphore, value)


def rows(ap, first, n, tiles):
    return ap[bass.ds(first, n)].rearrange("(j q) d -> q j d", q=P)


def build_program(nc, a, out):
    with ExitStack() as ctx:
        scope = [ctx]

        def sb(name, shape, dt=F32):
            return scope[-1].enter_context(nc.sbuf_tensor(name, shape, dt))

        def two(name, shape, dt=F32):
            return [sb(f"{name}{p}", shape, dt) for p in range(2)]

        sem_scope = [ctx]

        def sem(name):
            return sem_scope[-1].enter_context(nc.semaphore(name))

        def sems(name):
            return [sem(f"{name}{p}") for p in range(2)]

        def dram(name, shape, dt=F32):
            return nc.dram_tensor(name, shape, dt, kind="Internal").ap()

        psum = ctx.enter_context(nc.psum_tensor("psum", [P, 8, 512], F32))
        bank = [psum[:, n, :] for n in range(8)]

        x1_dram = dram("x1_dram", (TOK, D))
        route_dram = dram("route_dram", (TOK, 2 * K0))
        xe_dram = dram("xe_dram", (SLOTS0, D))
        ye_dram = dram("ye_dram", (SLOTS0, D))
        x3_dram = dram("x3_dram", (TOK, D))
        x4n_dram = dram("x4n_dram", (TOK, 2 * D))
        token_dram = dram("token_dram", (NO_ROWS + P, 1), U32)

        ident = sb("ident", [P, P])
        before = sb("before", [P, P], BF16)
        ones = sb("ones", [P, P], BF16)
        expert_id = sb("expert_id", [P, E0])
        zero_rows = sb("zero_rows", [P, 4, D])
        minus_half = sb("minus_half", [P, 4])
        w_rkvo = sb("w_rkvo", [P, 4, D])
        decay_in = sb("decay_in", [P, 1])
        decay_exp = sb("decay_exp", [P, 1])
        decay = sb("decay", [P, 1])
        first_in = sb("first_in", [P, 1])
        first_w = sb("first_w", [P, 1])
        mix = sb("mix", [P, 1])
        one_less_mix = sb("one_less_mix", [P, 1])
        gate0_w = sb("gate0_w", [P, E0])
        bias0 = sb("bias0", [P, E0])
        sw13 = sb("sw13", [P, 2, I0])
        sw2 = sb("sw2", [P, D])

        consts_in = sem("consts_in")
        casts_in = sem("casts_in")
        made = sem("made")
        weights_in = sem("weights_in")
        decay_ready = sem("decay_ready")
        xe_zeroed = sem("xe_zeroed")
        N_CONST_DMA, N_CAST_DMA, N_MADE, N_WEIGHT_DMA = 7, 8, 9, 16

        def constants_ready(eng):
            eng.wait_ge(consts_in, 16 * N_CONST_DMA)
            eng.wait_ge(casts_in, 16 * N_CAST_DMA)
            eng.wait_ge(made, N_MADE)
            eng.wait_ge(decay_ready, 3)

        ident16 = sb("ident16", [P, P], F16)
        ident_b = sb("ident_b", [P, P], BF16)
        w_qk = sb("w_qk", [P, 2 * HEADS * DK])
        w_v = sb("w_v", [P, HEADS * DV])
        w_g = sb("w_g", [P, HEADS * DV])
        w_out = sb("w_out", [P, PAIRS, D])
        w_qkv = sb("w_qkv", [P, 3 * D])
        b_qkv = sb("b_qkv", [P, 3 * D])
        w_o = sb("w_o", [P, D])
        b_o = sb("b_o", [P, D])
        gate1_w = sb("gate1_w", [P, E1])
        gate1_b = sb("gate1_b", [P, E1])
        norms = sb("norms", [P, 4])
        head_mask = sb("head_mask", [P, 4])
        token_start = sb("token_start", [P, 2])
        steps_of = sb("steps_of", [P, TOK // P])
        block_id = sb("block_id", [P, BLOCKS])
        ones_row = sb("ones_row", [1, P])

        scope.append(ctx.enter_context(ExitStack()))
        U1 = 512
        J1 = U1 // P
        x_in = two("x_in", [P, J1, D])
        stats = two("stats", [P, J1, 6])
        meanvar = two("meanvar", [P, J1, 2])
        veps = two("veps", [P, J1])
        rstd = two("rstd", [P, J1])
        xn = two("xn", [P, J1, D])
        xT = two("xT", [P, 2, SEQ + 1])
        shifted = two("shifted", [P, 2, SEQ])
        xm = two("xm", [P, 2, SEQ])
        ek = two("ek", [P, 2, SEQ])
        kv = two("kv", [P, 2, SEQ])
        tanh_r = two("tanh_r", [P, U1])
        sum_kv = two("sum_kv", [P, 2, SEQ + 1])
        sum_k = two("sum_k", [P, 2, SEQ + 1])
        num = two("num", [P, 2, SEQ])
        den = two("den", [P, 2, SEQ])
        rden = two("rden", [P, 2, SEQ])
        rw = two("rw", [P, U1])
        x1 = two("x1", [P, J1, D])
        x1s = two("x1s", [P, J1, D])
        xn2 = two("xn2", [P, J1, D])
        x2T = two("x2T", [P, U1])
        tanh_l = two("tanh_l", [P, J1, E0])
        score = two("score", [P, J1, E0])
        biased = two("biased", [P, J1, E0])
        top = two("top", [P, J1, 8])
        top_at = two("top_at", [P, J1, 8], U32)
        chosen = two("chosen", [P, J1 * K0])
        onehot = two("onehot", [P, J1, K0, E0])
        taken = two("taken", [P, J1, E0], BF16)
        prior = sb("prior", [P, 2 * J1 + 1, E0], BF16)
        picked = two("picked", [P, J1, K0, E0])
        pos = two("pos", [P, J1 * K0])
        weight = two("weight", [P, J1, K0])
        wsum = two("wsum", [P, J1])
        fits = two("fits", [P, J1 * K0])
        slot = two("slot", [P, J1 * K0])
        route = two("route", [P, J1, 2 * K0])
        tanh_a = two("tanh_a", [P, 2 * P])
        half_h = two("half_h", [P, 2 * P])
        hid = two("hid", [P, 2 * P])

        s = {}
        sem_scope.append(ctx.enter_context(ExitStack()))
        for name in "x_landed x1_stored route_stored scattered xe_landed w_landed ye_stored".split():
            s[name] = sems(name)
        for name in ("var1 rstd1 xn_made xnT_ps xT_made xm_made k_ps v_ps r_ps kmin ek_made tanh_r_made "
                     "rw_made y_ps x1_made var2 rstd2 xn2_made x2T_ps x2T_made logit_ps ab_ps tanh_l_made tanh_a_made "
                     "taken_made prior_made pos_ps slots_read route_made hid_made ysh_ps x1s_made "
                     "xeT_ps xeT_made e_ab_ps e_tanh_made e_hid_made ye_ps ye_made").split():
            s[name] = sem(name)
        early = [x for value in s.values() for x in (value if isinstance(value, list) else [value])]
        sem_scope.pop().close()
        dve_chain = sem("dve_chain")
        act_chain = sem("act_chain")
        pool_chain = sem("pool_chain")
        pool_turn = sem("pool_turn")
        sp_turn = sem("sp_turn")
        phase1_units = TOK // U1
        T1 = phase1_units // 2

        pairs = E0 // 2
        T2 = pairs // 2
        xe = two("xe", [P, 2, D])
        w13 = two("w13", [P, 2, 2, I0])
        w2 = two("w2", [P, D])
        xeT = two("xeT", [P, 2 * P])
        e_tanh = two("e_tanh", [P, P])
        e_half = two("e_half", [P, P])
        e_hid = two("e_hid", [P, P])
        ye = two("ye", [P, 2, D])

        scope.pop().close()
        scope.append(ctx.enter_context(ExitStack()))
        x1l = two("x1l", [P, 2, D])
        routel = two("routel", [P, 2, 2 * K0])
        yg = two("yg", [P, 2, K0, D])
        x2 = sb("x2", [P, 2, D])
        x2_kept = two("x2_kept", [P, 2, D])
        stats3 = sb("stats3", [P, 2, 6])
        meanvar3 = sb("meanvar3", [P, 2, 2])
        veps3 = sb("veps3", [P, 2])
        rstd3 = sb("rstd3", [P, 2])
        xn3 = sb("xn3", [P, 2, D])
        x3T = sb("x3T", [P, SEQ])
        qk = sb("qk", [P, 2, 2 * HEADS, DK])
        squares = two("squares", [P, 512])
        qk_norm = sb("qk_norm", [P, 2, 2 * HEADS])
        v_norm = sb("v_norm", [P, 2, HEADS])
        o_norm = sb("o_norm", [P, 2, HALF])
        o_len = sb("o_len", [P, 2, HALF])
        o_tanh = sb("o_tanh", [P, 2, HALF])
        o_factor = sb("o_factor", [P, 2, HALF])
        guess = sb("guess", [P, 2 * 2 * HEADS])
        newton = sb("newton", [P, 2 * 2 * HEADS])
        qk_inv = sb("qk_inv", [P, 2, 2 * HEADS])
        v_inv = sb("v_inv", [P, 2, HEADS])
        o_inv = sb("o_inv", [P, 2, HALF])
        terms = sb("terms", [P, 2, 2 * HEADS, TERMS, DK], F16)
        qT = two("qT", [P, PAIRS, SEQ], F16)
        kT = two("kT", [P, PAIRS, SEQ], F16)
        v = two("v", [P, 2, HEADS * DV])
        tanh_g = two("tanh_g", [P, 512])
        silu_g = sb("silu_g", [P, HEADS * DV])
        gate = two("gate", [P, 2, HEADS * DV])
        RING = 4
        attn = [sb(f"attn{n}", [P, 2, 512]) for n in range(RING)]
        aggr = sb("aggr", [P, 2, 512])
        aggr_sq = sb("aggr_sq", [P, 2, 512])
        o = sb("o", [P, 2, 512])
        oT = sb("oT", [P, 2, PAIRS, P])
        x3 = two("x3", [P, 2, D])
        for name in ("x1l_landed", "routel_landed", "yg_landed", "x3_stored"):
            s[name] = sems(name)
        for name in ("x2_made var3 rstd3 xn3_made x3T_ps x3T_made qk_ps v_ps3 g_ps qk_squared qk_copied v_squared v_copied "
                     "sq_reduced g_tanh silu_made gate_made qk_scaled high_made terms_made terms_ps qkT_act qkT_dve v_inv_made v_made "
                     "score_ps relu_made attn_made attn_made_pool attn_read aggr_out aggr_sq_made o_len_made o_tanh_made "
                     "o_factor_made gated o_made oT_ps oT_act oT_dve y3_ps x3_made yg_cleared phases").split():
            s[name] = sem(name)
        ring = [bank[6], bank[7]]
        OT_BANK = ((0, 1), (1, 0))
        G_BANK = ((1, 0), (1, 0))
        POOL_PAIRS = (3, 6)

        scope.pop().close()
        x3l = two("x3l", [P, 2, D])
        x3_kept = two("x3_kept", [P, 2, D])
        stats4 = sb("stats4", [P, 2, 6])
        meanvar4 = sb("meanvar4", [P, 2, 2])
        veps4 = sb("veps4", [P, 2])
        rstd4 = sb("rstd4", [P, 2])
        rstd4_in = sb("rstd4_in", [P, 2])
        rstd4_norm = sb("rstd4_norm", [P, 2])
        x3n = two("x3n", [P, 2, D])
        xn4 = sb("xn4", [P, 2, D])
        h4T = sb("h4T", [P, SEQ])
        qk4 = sb("qk4", [P, 2, 2, D])
        v4 = two("v4", [P, 2, HEADS, DH + 1])
        terms4 = sb("terms4", [P, 2, 2, HEADS, TERMS1, DH], BF16)
        high4 = sb("high4", [P, 2, 2, D], BF16)
        k_highT = sb("k_highT", [P, SEQ], BF16)
        q_highT = sb("q_highT", [P, 4, SEQ], BF16)
        qT4 = two("qT4", [P, PAIRS, SEQ], BF16)
        kT4 = two("kT4", [P, PAIRS, SEQ], BF16)
        prob = [sb(f"prob{n}", [P, 2 * SEQ]) for n in range(4)]
        rsum = sb("rsum", [P, 2, HEADS])
        o4 = sb("o4", [P, 2, D])
        o4T = sb("o4T", [P, SEQ])
        stats5 = sb("stats5", [P, 2, 6])
        meanvar5 = sb("meanvar5", [P, 2, 2])
        veps5 = sb("veps5", [P, 2])
        rstd5 = sb("rstd5", [P, 2])
        x3_plain = two("x3_plain", [P, 2, D])
        x4 = two("x4", [P, 2, D])
        x4n = two("x4n", [P, 2, 2 * D])
        h5T = sb("h5T", [P, SEQ])
        logit = sb("logit", [P, 2, E1])
        top_b = sb("top_b", [P, 2, 8])
        top_at_b = sb("top_at_b", [P, 2, 8], U32)
        chosen_b = sb("chosen_b", [P, 2])
        onehot_b = sb("onehot_b", [P, 2, E1], BF16)
        prior_b = sb("prior_b", [P, 3, E1], BF16)
        picked_b = sb("picked_b", [P, 2, E1])
        pos_b = sb("pos_b", [P, 2])
        slot_b = two("slot_b", [P, 2], U32)
        token = two("token", [P, 2], U32)
        token_f = sb("token_f", [P, 2])
        no_token = sb("no_token", [P, E1 * TOK // P + 1], U32)
        for name in ("x3l_landed", "x4_stored", "token_sent"):
            s[name] = sems(name)
        for name in ("kept_made var4 rstd4 xn4_made x4T_ps h4T_made qkv_ps qkv_out high4_made rest4_made mid4_made terms4_made "
                     "high_ps high_out max_ps max_made k4_ps k4_out q4_ps q4_out score4_ps exp_made pv_made o4_made o4T_ps "
                     "o4T_made y4_ps rstd4_in x3n_made x4_made sum_made plain_made var5 rstd5 x4n_made x5T_ps h5T_made logit1_ps logit1_sum logit1_out onehot1_made prior1_made pos1_ps pos1_out "
                     "slot1_made set4 x3_all table_cleared").split():
            s[name] = sem(name)
        count = sb("count", [P, E1])
        steps = sb("steps", [P, E1, TOK // P])
        blocks_of = sb("blocks_of", [P, E1])
        blocks_to = sb("blocks_to", [P, E1])
        passed = sb("passed", [P, BLOCKS, E1])
        passed_blocks = sb("passed_blocks", [P, BLOCKS, E1])
        block_expert = sb("block_expert", [P, BLOCKS])
        block_start = sb("block_start", [P, BLOCKS])
        block_row = sb("block_row", [P, BLOCKS])
        block_row_i = sb("block_row_i", [P, BLOCKS], I32)
        block_expert_i = sb("block_expert_i", [P, BLOCKS], I32)
        rows_of = two("rows_of", [P, 1], U32)
        got = two("got", [P, 2 * D])
        wa = two("wa", [P, F1])
        wb = two("wb", [P, CHUNKS, D])
        ba = two("ba", [P, CHUNKS])
        bb = two("bb", [1, D])
        g5T = two("g5T", [P, P])
        mid = two("mid", [P, CHUNKS, P])
        res = two("res", [P, D])
        for name in ("rows_landed", "got_landed", "wa_landed", "res_sent"):
            s[name] = sems(name)
        for name in ("all_counted count_ps plan_made g5T_ps g5T_made mid_ps mid_act mid_dve res_ps res_made cleared").split():
            s[name] = sem(name)

        block = ctx.enter_context(nc.Block())

        @block.sync
        def _(sp):
            for dst, src in ((ident[:], a["eye"]), (w_rkvo[:], a["w_rkvo"]), (decay_in[:], a["time_decay"]),
                             (first_in[:], a["time_first"]), (mix[:], a["time_mix"]), (expert_id[:], a["ids"]),
                             (bias0[:], a["bias0"].partition_broadcast(P))):
                sp.dma_start(dst, src).then_inc(consts_in, 16)
            sp.wait_ge(made, N_MADE)
            for n in range(SLOTS0 // U1):
                sp.dma_start(rows(xe_dram, n * U1, U1, J1), zero_rows[:]).then_inc(xe_zeroed, 16)

            for dst, src in ((w_qk[:], a["w_qk"]), (w_v[:], a["w_v"]), (w_g[:], a["w_g"]), (w_out[:], a["w_out"]),
                             (w_qkv[:], a["w_qkv"]), (b_qkv[:], a["b_qkv"].partition_broadcast(P)), (w_o[:], a["w_o"]),
                             (b_o[:], a["b_o"].partition_broadcast(P)), (gate1_w[:], a["gate1_w"]),
                             (gate1_b[:], a["gate1_b"].partition_broadcast(P)), (norms[:], a["norms"]), (head_mask[:], a["head_mask"]),
                             (token_start[:], a["token_start"]), (steps_of[:], a["steps_of"].partition_broadcast(P)),
                             (block_id[:], a["block_id"].partition_broadcast(P)), (ones_row[:], a["ones"][0:1, :])):
                sp.dma_start(dst, src).then_inc(weights_in, 16)

            def turn(i):
                for p in range(2):
                    wait(sp, s["x1_made"], 2 * i)
                    sp.dma_start(x_in[p][:], rows(a["x"], (2 * i + p) * U1, U1, J1)).then_inc(s["x_landed"][p], 16)
                for p in range(2):
                    sp.wait_ge(s["route_made"], 2 * i + p + 1)
                    sp.dma_start(rows(route_dram, (2 * i + p) * U1, U1, J1), route[p][:]).then_inc(s["route_stored"][p], 16)
                    sp.wait_ge(s["x1s_made"], 2 * i + p + 1)
                    sp.dma_start(rows(x1_dram, (2 * i + p) * U1, U1, J1), x1s[p][:]).then_inc(s["x1_stored"][p], 16)

            repeat(sp, T1, turn)

            for p in range(2):
                sp.wait_ge(s["scattered"][p], 16 * J1 * K0 * T1)
            def turn(i):
                for p in range(2):
                    wait(sp, s["xeT_ps"], 2 * i)
                    sp.dma_start(xe[p][:], rows(xe_dram, (2 * i + p) * 2 * CAP, 2 * CAP, 2)).then_inc(s["xe_landed"][p], 16)
                for p in range(2):
                    sp.wait_ge(s["ye_made"], 2 * i + p + 1)
                    sp.dma_start(rows(ye_dram, (2 * i + p) * 2 * CAP, 2 * CAP, 2), ye[p][:]).then_inc(s["ye_stored"][p], 16)

            repeat(sp, T2, turn)

            for p in range(2):
                sp.wait_ge(s["x1_stored"][p], 16 * T1)
                sp.wait_ge(s["route_stored"][p], 16 * T1)
                sp.wait_ge(s["ye_stored"][p], 16 * T2)
            sp.sem_inc(s["phases"], 1)
            sp.wait_ge(s["phases"], 5)
            for semaphore in early:
                sp.sem_clear(semaphore)
            sp.sem_inc(s["cleared"], 1)

            def half(fetch, front, att, tail):
                if fetch:
                    wait(sp, s["x2_made"], fetch.n - 2)
                    sp.dma_start(x1l[fetch.p][:], rows(x1_dram, (fetch.n - 1) * SEQ, SEQ, 2)).then_inc(s["x1l_landed"][fetch.p], 16)
                    sp.dma_start(routel[fetch.p][:], rows(route_dram, (fetch.n - 1) * SEQ, SEQ, 2)).then_inc(s["routel_landed"][fetch.p], 16)
                if tail:
                    sp.wait_ge(s["x3_made"], tail.n)
                    sp.dma_start(rows(x3_dram, (tail.n - 1) * SEQ, SEQ, 2), x3[tail.p][:]).then_inc(s["x3_stored"][tail.p], 16)

            pipeline(sp, half)
            for p in range(2):
                sp.wait_ge(s["x3_stored"][p], 16 * BATCH // 2)
            sp.sem_inc(s["phases"], 1)
            sp.wait_ge(s["phases"], 10)
            sp.wait_ge(s["set4"], 1)
            sp.dma_start(token_dram.rearrange("(q n) a -> q (n a)", q=P), no_token[:]).then_inc(s["table_cleared"], 16)

            def half(fetch, front, att, tail, end):
                if fetch:
                    wait(sp, s["kept_made"], fetch.n - 2)
                    sp.dma_start(x3l[fetch.p][:], rows(x3_dram, (fetch.n - 1) * SEQ, SEQ, 2)).then_inc(s["x3l_landed"][fetch.p], 16)
                if tail:
                    sp.wait_ge(s["x4n_made"], tail.n)
                    sp.wait_ge(s["sum_made"], tail.n)
                    sp.dma_start(rows(x4n_dram, (tail.n - 1) * SEQ, SEQ, 2), x4n[tail.p][:]).then_inc(s["x4_stored"][tail.p], 16)

            pipeline(sp, half, 5)
            for p in range(2):
                sp.wait_ge(s["x4_stored"][p], 16 * BATCH // 2)
                sp.wait_ge(s["token_sent"][p], 32 * BATCH // 2)
            sp.wait_ge(s["plan_made"], 1)
            def turn(i):
                for p in range(2):
                    block_n = 2 * i + p
                    wait(sp, s["res_sent"][p], 16 * i)
                    sp.sem_inc(sp_turn, 1)
                    first = sp.value_load(block_row_i[0:1, bass.ds(block_n, 1)], min_val=0, max_val=NO_ROWS)
                    sp.dma_start(rows_of[p][:], token_dram[bass.ds(first, P)]).then_inc(s["rows_landed"][p], 16)
                    wait(sp, s["res_ps"], 2 * i)
                    sp.sem_inc(sp_turn, 1)
                    expert = sp.value_load(block_expert_i[0:1, bass.ds(block_n, 1)], min_val=0, max_val=E1 - 1)
                    sp.dma_start(wa[p][:], a["wa"][bass.ds(expert, 1)].rearrange("e q f -> (e q) f")).then_inc(s["wa_landed"][p], 16)
                    sp.dma_start(wb[p][:], a["wb"][bass.ds(expert, 1)].rearrange("e (c q) d -> q (e c) d", q=P)).then_inc(s["wa_landed"][p], 16)
                    sp.dma_start(ba[p][:], a["ba"][bass.ds(expert, 1)].rearrange("e q c -> (e q) c")).then_inc(s["wa_landed"][p], 16)
                    sp.dma_start(bb[p][:], a["bb"][bass.ds(expert, 1)]).then_inc(s["wa_landed"][p], 16)

            repeat(sp, BLOCKS // 2, turn)
            for p in range(2):
                sp.wait_ge(s["res_sent"][p], 16 * BLOCKS // 2)

        @block.gpsimd
        def _(pool):
            def hold(semaphore, value):
                if not isinstance(value, int) or value > 0:
                    pool.wait_ge(semaphore, value)
                    pool.sem_inc(pool_turn, 1)

            chain = Chain(pool, pool_chain)
            for dst, src in ((before[:], a["upper"]), (gate0_w[:], a["gate0_w"]), (sw13[:], a["sw13"]),
                             (sw2[0:I0, :], a["sw2"]), (sw2[I0:P, :], a["sw2"]), (ones[:], a["ones"]),
                             (ident16[:], a["eye"]), (ident_b[:], a["eye"])):
                pool.dma_start(dst, src).then_inc(casts_in, 16)
            pool.memset(zero_rows[:], 0.0).then_inc(made, 1)
            pool.memset(minus_half[:], -0.5).then_inc(made, 1)
            for p in range(2):
                pool.memset(xT[p][:, :, 0:1], 0.0).then_inc(made, 1)
                pool.memset(sum_kv[p][:, :, 0:1], 0.0).then_inc(made, 1)
                pool.memset(sum_k[p][:, :, 0:1], 0.0).then_inc(made, 1)
                if p == 0:
                    pool.memset(prior[:, 0:1, :], 0.0).then_inc(made, 1)
            last_slot = pool.to_reg(SLOTS0 - 1)
            pool.wait_ge(made, N_MADE)
            pool.wait_ge(xe_zeroed, 16 * (SLOTS0 // U1))
            def turn(i):
                for var, ready in (("var1", "rstd1"), ("var2", "rstd2")):
                    for p in range(2):
                        hold(s[var], 2 * i + p + 1)
                        n = chain.step(pool.tensor_scalar(veps[p][:], meanvar[p][:, :, 1], 1.0, LN_EPS, ALU.mult, ALU.add))
                        chain.need(n)
                        pool.tensor_tensor(rstd[p][:], veps[p][:], minus_half[:, 0:J1], ALU.pow).then_inc(s[ready], 1)
                for p in range(2):
                    hold(s["route_made"], 2 * i + p + 1)
                    where = route[p][:].bitcast(U32)
                    for j in range(J1):
                        for k in range(K0):
                            pool.indirect_dma_start(
                                xe_dram, bass.IndirectOffsetOnAxis(ap=where[:, j, K0 + k:K0 + k + 1], axis=0),
                                xn2[p][:, j, :], None, bounds_check=last_slot, oob_is_err=False,
                            ).then_inc(s["scattered"][p], 16)
                chain.restart()

            repeat(pool, T1, turn)
            def turn(i):
                for p in range(2):
                    hold(s["ye_ps"], 2 * i)
                    pool.dma_start(w13[p][:, 0, :, :], a["w1"][:, bass.ds((2 * i + p) * 2, 2), :]).then_inc(s["w_landed"][p], 16)
                    pool.dma_start(w13[p][:, 1, :, :], a["w3"][:, bass.ds((2 * i + p) * 2, 2), :]).then_inc(s["w_landed"][p], 16)
                    pool.dma_start(w2[p][:], a["w2"][bass.ds((2 * i + p) * P, P)]).then_inc(s["w_landed"][p], 16)

            repeat(pool, T2, turn)
            pool.drain().then_inc(s["phases"], 1)
            pool.wait_ge(s["phases"], 5)
            for p in range(2):
                pool.memset(yg[p][:], 0.0).then_inc(s["yg_cleared"], 1)
            pool.wait_ge(s["yg_cleared"], 2)

            def square(att, g):
                hold(s["relu_made"], PAIRS * (att.n - 1) + g + 1)
                r = attn[g % RING]
                pool.tensor_tensor(r[:], r[:], r[:], ALU.mult).then_inc(s["attn_made_pool"], 1)

            def scale_gate(q, hf):
                hold(s["gate_made"], 2 * q.n)
                hold(s["o_factor_made"], 2 * (q.n - 1) + hf + 1)
                for j in range(2):
                    part = gate[q.p][:, j, 512 * hf:512 * hf + 512].rearrange("q (h d) -> q h d", d=DV)
                    ins = pool.tensor_tensor(part, part, o_factor[:, j, :].unsqueeze(2).to_broadcast([P, HALF, DV]), ALU.mult)
                    ins.then_inc(s["gated"], 1)

            def half(fetch, front, att, tail):
                if front:
                    hold(s["var3"], front.n)
                    n = chain.step(pool.tensor_scalar(veps3[:], meanvar3[:, :, 1], 1.0, LN_EPS, ALU.mult, ALU.add))
                    chain.need(n)
                    pool.tensor_tensor(rstd3[:], veps3[:], minus_half[:, 0:2], ALU.pow).then_inc(s["rstd3"], 1)
                if fetch:
                    if not isinstance(fetch.n, int) or fetch.n > 2:
                        hold(s["x2_made"], fetch.n - 2)
                    hold(s["routel_landed"][fetch.p], 16 * fetch.k)
                    where = routel[fetch.p][:].bitcast(U32)
                    for j in range(2):
                        for k in range(K0):
                            pool.indirect_dma_start(
                                yg[fetch.p][:, j, k, :], None, ye_dram,
                                bass.IndirectOffsetOnAxis(ap=where[:, j, K0 + k:K0 + k + 1], axis=0),
                                bounds_check=last_slot, oob_is_err=False,
                            ).then_inc(s["yg_landed"][fetch.p], 16)
                if tail:
                    scale_gate(tail, 1)
                if att:
                    square(att, POOL_PAIRS[0])
                if front:
                    hold(s["v_inv_made"], front.n)
                    hold(s["v_copied"], 4 * front.n)
                    vv = v[front.p][:].rearrange("q j (h d) -> q (j h) d", d=DV)
                    pool.tensor_tensor(vv, vv, v_inv[:].rearrange("q j h -> q (j h)").unsqueeze(2).to_broadcast([P, 2 * HEADS, DV]), ALU.mult).then_inc(s["v_made"], 1)
                if att:
                    scale_gate(att, 0)
                    square(att, POOL_PAIRS[1])
                if front:
                    chain.restart()

            pipeline(pool, half)
            pool.drain().then_inc(s["phases"], 1)
            pool.wait_ge(s["phases"], 10)
            no_more = pool.to_reg(NO_ROWS - 1)
            last_token = pool.to_reg(TOK - 1)
            pool.memset(no_token[:], TOK).then_inc(s["set4"], 1)
            pool.memset(terms4[:], 0.0).then_inc(s["set4"], 1)
            for p in range(2):
                pool.memset(v4[p][:, :, :, DH:DH + 1], 1.0).then_inc(s["set4"], 1)
                pool.memset(got[p][:], 0.0).then_inc(s["set4"], 1)
            pool.memset(prior_b[:, 0:1, :], 0.0).then_inc(s["set4"], 1)
            pool.wait_ge(s["set4"], 7)
            pool.memset(terms4[:, 1, :, :, 6, 0:1].rearrange("q j h a -> q (j h) a"), 1.0).then_inc(s["set4"], 1)
            pool.wait_ge(s["set4"], 8)

            def inverse_deviation(var, meanvar_x, veps_x, rstd_x, done, count):
                hold(s[var], count)
                n = chain.step(pool.tensor_scalar(veps_x[:], meanvar_x[:, :, 1], 1.0, LN_EPS, ALU.mult, ALU.add))
                chain.need(n)
                pool.tensor_tensor(rstd_x[:], veps_x[:], minus_half[:, 0:2], ALU.pow).then_inc(s[done], 1)

            def half(fetch, front, att, tail, end):
                if front:
                    inverse_deviation("var4", meanvar4, veps4, rstd4_in, "rstd4_in", front.n)
                    hold(s["rstd4_in"], front.n)
                    n = chain.step(pool.tensor_tensor(veps4[:], rstd4_in[:], rstd4_in[:], ALU.mult))
                    chain.need(n)
                    n = chain.step(pool.tensor_tensor(veps4[:], veps4[:], meanvar4[:, :, 1], ALU.mult))
                    chain.need(n)
                    n = chain.step(pool.tensor_scalar(veps4[:], veps4[:], 1.0, LN_EPS, ALU.mult, ALU.add))
                    chain.need(n)
                    n = chain.step(pool.tensor_tensor(rstd4_norm[:], veps4[:], minus_half[:, 0:2], ALU.pow))
                    chain.need(n)
                    pool.tensor_tensor(rstd4[:], rstd4_norm[:], rstd4_in[:], ALU.mult).then_inc(s["rstd4"], 1)
                    chain.step(pool.tensor_scalar(x3n[front.p][:, 0, :], x3l[front.p][:, 0, :], meanvar4[:, 0, 0:1], rstd4_in[:, 0:1], ALU.subtract, ALU.mult))
                    pool.tensor_scalar(x3n[front.p][:, 1, :], x3l[front.p][:, 1, :], meanvar4[:, 1, 0:1], rstd4_in[:, 1:2], ALU.subtract, ALU.mult).then_inc(s["x3n_made"], 1)
                if att:
                    if not isinstance(att.n, int) or att.n > 2:
                        hold(s["x4_made"], att.n - 2)
                    if not isinstance(att.n, int) or att.n > 2:
                        hold(s["sum_made"], att.n - 2)
                    pool.tensor_copy(x3_plain[att.p][:], x3l[att.p][:]).then_inc(s["plain_made"], 1)
                    hold(s["x3n_made"], att.n)
                    pool.tensor_tensor(x3_kept[att.p][:], x3n[att.p][:], b_o[:].unsqueeze(1).to_broadcast([P, 2, D]), ALU.add).then_inc(s["kept_made"], 1)
                if tail:
                    inverse_deviation("var5", meanvar5, veps5, rstd5, "rstd5", tail.n)
                    if not isinstance(tail.k, int) or tail.k > 1:
                        hold(s["x4_stored"][tail.p], 16 * (tail.k - 1))
                    hold(s["plain_made"], tail.n)
                    pool.tensor_tensor(x4n[tail.p][:, :, 0:D], x4[tail.p][:], x3_plain[tail.p][:], ALU.add).then_inc(s["sum_made"], 1)
                if end:
                    hold(s["slot1_made"], end.n)
                    pool.wait_ge(s["table_cleared"], 16)
                    for j in range(2):
                        pool.indirect_dma_start(
                            token_dram, bass.IndirectOffsetOnAxis(ap=slot_b[end.p][:, j:j + 1], axis=0),
                            token[end.p][:, j:j + 1], None, bounds_check=no_more, oob_is_err=False,
                        ).then_inc(s["token_sent"][end.p], 16)
                if front or tail:
                    chain.restart()

            pipeline(pool, half, 5)
            for p in range(2):
                pool.wait_ge(s["x4_stored"][p], 16 * BATCH // 2)

            def gather(turn, p, passed_by):
                if passed_by is not None:
                    hold(s["res_made"], passed_by)
                hold(s["rows_landed"][p], 16 * (turn + 1))
                pool.indirect_dma_start(
                    got[p][:], None, x4n_dram, bass.IndirectOffsetOnAxis(ap=rows_of[p][:], axis=0),
                    bounds_check=last_token, oob_is_err=False).then_inc(s["got_landed"][p], 16)

            def turn(i):
                for p in range(2):
                    gather(i, p, 2 * i)
                for p in range(2):
                    hold(s["res_made"], 2 * i + p + 1)
                    pool.indirect_dma_start(
                        out, bass.IndirectOffsetOnAxis(ap=rows_of[p][:], axis=0), res[p][:], None,
                        bounds_check=last_token, oob_is_err=False).then_inc(s["res_sent"][p], 16)

            repeat(pool, BLOCKS // 2, turn)
            for p in range(2):
                pool.wait_ge(s["res_sent"][p], 16 * BLOCKS // 2)

        @block.scalar
        def _(act):
            act.wait_ge(consts_in, 16 * N_CONST_DMA)
            act.activation(decay_exp[:], decay_in[:], ACT.Exp).then_inc(decay_ready, 1)
            act.wait_ge(decay_ready, 1)
            act.activation(decay[:], decay_exp[:], ACT.Exp, scale=-1.0).then_inc(decay_ready, 1)
            act.activation(first_w[:], first_in[:], ACT.Exp).then_inc(decay_ready, 1)
            constants_ready(act)
            def turn(i):
                for p in range(2):
                    act.wait_ge(s["xnT_ps"], 2 * i + p + 1)
                    act.activation(xT[p][:, :, 1:], bank[4 * p][:].rearrange("q (a t) -> q a t", a=2), ACT.Copy).then_inc(s["xT_made"], 1)
                for p in range(2):
                    act.wait_ge(s["kmin"], 2 * i + p + 1)
                    act.activation(ek[p][:], ek[p][:], ACT.Exp).then_inc(s["ek_made"], 1)
                    act.wait_ge(s["r_ps"], 2 * i + p + 1)
                    act.activation(tanh_r[p][:], bank[4 * p + 3][:], ACT.Tanh, scale=0.5).then_inc(s["tanh_r_made"], 1)
                for p in range(2):
                    act.wait_ge(s["x2T_ps"], 2 * i + p + 1)
                    act.activation(x2T[p][:], bank[4 * p + 1][:], ACT.Copy).then_inc(s["x2T_made"], 1)
                for p in range(2):
                    act.wait_ge(s["logit_ps"], 2 * i + p + 1)
                    act.activation(tanh_l[p][:], bank[4 * p][:, 0:J1 * E0].rearrange("q (j e) -> q j e", j=J1), ACT.Tanh, scale=0.5).then_inc(s["tanh_l_made"], 1)
                    act.wait_ge(s["ab_ps"], 2 * i + p + 1)
                    act.activation(tanh_a[p][:], bank[4 * p + 2][:, 0:256], ACT.Tanh, scale=0.5).then_inc(s["tanh_a_made"], 1)

            repeat(act, T1, turn)
            def turn(i):
                for p in range(2):
                    act.wait_ge(s["xeT_ps"], 2 * i + p + 1)
                    act.activation(xeT[p][:], bank[4 * p][:, 0:256], ACT.Copy).then_inc(s["xeT_made"], 1)
                for p in range(2):
                    act.wait_ge(s["e_ab_ps"], 2 * i + p + 1)
                    act.activation(e_tanh[p][:], bank[4 * p + 1][:, 0:P], ACT.Tanh, scale=0.5).then_inc(s["e_tanh_made"], 1)
                for p in range(2):
                    wait(act, s["ye_stored"][p], 16 * i)
                    act.wait_ge(s["ye_ps"], 2 * i + p + 1)
                    act.activation(ye[p][:, 0, :], bank[4 * p + 2][:, 0:D], ACT.Copy)
                    act.activation(ye[p][:, 1, :], bank[4 * p + 3][:, 0:D], ACT.Copy).then_inc(s["ye_made"], 1)

            repeat(act, T2, turn)

            act.drain().then_inc(s["phases"], 1)
            act.wait_ge(s["phases"], 5)

            def relu(att, g):
                r = attn[g % RING]
                wait(act, s["attn_read"], PAIRS * (att.n - 1) + g + 1 - RING)
                act.wait_ge(s["score_ps"], PAIRS * (att.n - 1) + g + 1)
                act.activation(r[:], psum[:, 2 * (g % 2):2 * (g % 2) + 2, :], ACT.Relu).then_inc(s["relu_made"], 1)

            def square_of(front, k, src):
                wait(act, s["sq_reduced"], 6 * (front.n - 1) + k - 1)
                act.activation(squares[k % 2][:], src, ACT.Square).then_inc(s["qk_squared"] if k < 2 else s["v_squared"], 1)

            def gate_tanh(front, j):
                wait(act, s["o_made"], 2 * (front.n - 2))
                act.wait_ge(s["silu_made"], 4 * (front.n - 1) + 2 * j + 2)
                act.activation(gate[front.p][:, j, :], silu_g[:], ACT.Tanh, scale=0.5).then_inc(s["gate_made"], 1)

            def take_aggregate(q, hf):
                wait(act, s["o_made"], 2 * (q.n - 1) + hf)
                act.wait_ge(s["attn_read"], PAIRS * (q.n - 1) + 4 * hf + 4)
                act.activation(aggr[:], psum[:, 4:6, :], ACT.Copy).then_inc(s["aggr_out"], 1)
                act.wait_ge(s["aggr_out"], 2 * (q.n - 1) + hf + 1)
                act.activation(aggr_sq[:], aggr[:], ACT.Square).then_inc(s["aggr_sq_made"], 1)

            def tanh_of_norm(q, hf):
                wait(act, s["o_factor_made"], 2 * (q.n - 1) + hf)
                act.wait_ge(s["o_len_made"], 2 * (q.n - 1) + hf + 1)
                act.activation(o_tanh[:], o_len[:], ACT.Tanh).then_inc(s["o_tanh_made"], 1)

            def take_oT(q, hf):
                act.wait_ge(s["oT_ps"], 4 * (q.n - 1) + 2 * hf + 1)
                act.activation(oT[:, 0, 4 * hf:4 * hf + 4, :], ring[OT_BANK[hf][0]][:].rearrange("q (c t) -> q c t", c=4), ACT.Copy).then_inc(s["oT_act"], 1)

            def half(fetch, front, att, tail):
                for g in range(PAIRS):
                    if att:
                        relu(att, g)
                    if front and g == 0:
                        act.wait_ge(s["x3T_ps"], front.n)
                        act.activation(x3T[:], ring[0][:, 0:SEQ], ACT.Copy).then_inc(s["x3T_made"], 1)
                    if tail and g == 1:
                        take_aggregate(tail, 1)
                    if front and g == 1:
                        for j in range(2):
                            act.wait_ge(s["qk_copied"], 2 * (front.n - 1) + j + 1)
                            square_of(front, j, qk[:, j, :, :].rearrange("q h d -> q (h d)"))
                    if tail and g == 2:
                        tanh_of_norm(tail, 1)
                    if front and g in (2, 3):
                        for h in range(2):
                            act.wait_ge(s["v_copied"], 4 * (front.n - 1) + 2 * (g - 2) + h + 1)
                            square_of(front, 2 + 2 * (g - 2) + h, v[front.p][:, g - 2, 512 * h:512 * h + 512])
                    if front and g == 5:
                        gate_tanh(front, 0)
                    if front and g in (4, 5):
                        for h in range(2):
                            m = 4 * (front.n - 1) + 2 * (g - 4) + h + 1
                            act.wait_ge(s["g_ps"], m)
                            wait(act, s["silu_made"], m - 2)
                            act.activation(tanh_g[h][:], ring[G_BANK[g - 4][h]][:], ACT.Tanh, scale=0.5).then_inc(s["g_tanh"], 1)
                    if tail and g == 4:
                        take_oT(tail, 1)
                    if att and g == 5:
                        take_aggregate(att, 0)
                    if front and g == 4:
                        wait(act, s["terms_ps"], 4 * (front.n - 1))
                        act.wait_ge(s["qk_scaled"], front.n)
                        act.activation(terms[:, :, :, 0, :].rearrange("q j h d -> q (j h) d"), qk[:].rearrange("q j h d -> q (j h) d"), ACT.Copy).then_inc(s["high_made"], 1)
                    if front and g == 6:
                        gate_tanh(front, 1)
                    if att and g == 6:
                        tanh_of_norm(att, 0)
                    if front and g in (6, 7):
                        c = g - 6
                        act.wait_ge(s["terms_ps"], 4 * (front.n - 1) + 2 * c + 1)
                        act.activation(qT[front.p][:, 4 * c:4 * c + 4, :].rearrange("q a (j t) -> q a j t", j=2),
                                       ring[0].bitcast(F16).rearrange("q (a j t) -> q a j t", a=4, j=2), ACT.Copy).then_inc(s["qkT_act"], 1)
                    if att and g == 7:
                        take_oT(att, 0)

            pipeline(act, half)
            act.drain().then_inc(s["phases"], 1)
            act.wait_ge(s["phases"], 10)
            act.wait_ge(s["cleared"], 1)
            act.wait_ge(weights_in, 16 * N_WEIGHT_DMA)
            act.wait_ge(s["set4"], 8)

            def exp(att, head):
                wait(act, s["pv_made"], HEADS * (att.n - 1) + head + 1 - 4)
                act.wait_ge(s["score4_ps"], HEADS * (att.n - 1) + head + 1)
                act.activation(prob[head % 4][:], bank[head % 3][:], ACT.Exp, scale=SCALE).then_inc(s["exp_made"], 1)

            def take_terms(front, what, c, x):
                dst = (kT4 if what == "k4" else qT4)[front.p]
                act.wait_ge(s[what + "_ps"], 2 * (front.n - 1) + c + 1)
                act.activation(dst[:, 4 * c:4 * c + 4, :].rearrange("q a t -> q (a t)"), ring[x].bitcast(BF16), ACT.Copy).then_inc(s[what + "_out"], 1)

            def half(fetch, front, att, tail, end):
                flat = terms4[:].rearrange("q w j h m d -> q (w j h) m d")
                qk_flat = qk4[:].rearrange("q w j (h d) -> q (w j h) d", d=DH)
                for g in range(PAIRS):
                    if att:
                        exp(att, 2 * g)
                        exp(att, 2 * g + 1)
                    if front and g == 0:
                        act.wait_ge(s["x4T_ps"], front.n)
                        act.activation(h4T[:], ring[0][:, 0:SEQ], ACT.Identity, bias=norms[:, 1:2], scale=norms[:, 0:1]).then_inc(s["h4T_made"], 1)
                    if front and g == 1:
                        wait(act, s["q4_ps"], 2 * (front.n - 1))
                        act.wait_ge(s["qkv_out"], 2 * front.n)
                        act.activation(high4[:], qk4[:], ACT.Copy).then_inc(s["high4_made"], 1)
                        act.wait_ge(s["high4_made"], front.n)
                        act.activation(flat[:, :, 0, :], high4[:].rearrange("q w j (h d) -> q (w j h) d", d=DH), ACT.Copy)
                        act.wait_ge(s["rest4_made"], front.n)
                        act.activation(flat[:, :, 4, :], qk_flat, ACT.Copy).then_inc(s["mid4_made"], 1)
                    if front and g == 2:
                        take_terms(front, "k4", 0, 1)
                    if tail and g == 2:
                        act.wait_ge(s["o4T_ps"], tail.n)
                        act.activation(o4T[:], ring[0][:, 0:SEQ], ACT.Copy).then_inc(s["o4T_made"], 1)
                    if front and g == 3:
                        take_terms(front, "k4", 1, 0)
                    if front and g == 5:
                        take_terms(front, "q4", 0, 0)
                    if tail and g == 6:
                        act.wait_ge(s["x5T_ps"], tail.n)
                        act.activation(h5T[:], ring[1][:, 0:SEQ], ACT.Identity, bias=norms[:, 3:4], scale=norms[:, 2:3]).then_inc(s["h5T_made"], 1)
                    if front and g == 7:
                        take_terms(front, "q4", 1, 0)

            pipeline(act, half, 5)
            def turn(i):
                for p in range(2):
                    act.wait_ge(s["g5T_ps"], 2 * i + p + 1)
                    act.activation(g5T[p][:], bank[4 * p][:, 0:P], ACT.Identity, bias=norms[:, 3:4], scale=norms[:, 2:3]).then_inc(s["g5T_made"], 1)
                for p in range(2):
                    act.wait_ge(s["mid_ps"], 4 * i + 2 * p + 1)
                    for c in range(2):
                        ins = act.activation(mid[p][:, c, :], bank[4 * p + 1][:, c * P:(c + 1) * P], ACT.Relu, bias=ba[p][:, c:c + 1])
                    ins.then_inc(s["mid_act"], 1)

            repeat(act, BLOCKS // 2, turn)

        @block.tensor
        def _(pe):
            constants_ready(pe)
            def turn(i):
                for p in range(2):
                    b = bank[4 * p:4 * p + 4]
                    wait(pe, s["slots_read"], 2 * i)
                    pe.wait_ge(s["xn_made"], 2 * i + p + 1)
                    for j in range(J1):
                        mm = pe.transpose(b[0][:, j * P:(j + 1) * P], xn[p][:, j, :], ident[:])
                    mm.then_inc(s["xnT_ps"], 1)
                for p in range(2):
                    b = bank[4 * p:4 * p + 4]
                    wait(pe, s["x1s_made"], 2 * i)
                    pe.wait_ge(s["xm_made"], 2 * i + p + 1)
                    for n, name in ((0, "k_ps"), (1, "v_ps"), (2, "r_ps")):
                        pe.matmul(b[1 + n][:], w_rkvo[:, n, :], xm[p][:].rearrange("q a t -> q (a t)"), start=True, stop=True).then_inc(s[name], 1)
                for p in range(2):
                    pe.wait_ge(s["rw_made"], 2 * i + p + 1)
                    for j in range(J1):
                        mm = pe.matmul(bank[4 * p][:, j * P:(j + 1) * P], rw[p][:, j * P:(j + 1) * P], w_rkvo[:, 3, :], start=True, stop=True)
                    mm.then_inc(s["y_ps"], 1)
                for p in range(2):
                    pe.wait_ge(s["xn2_made"], 2 * i + p + 1)
                    for j in range(J1):
                        mm = pe.transpose(bank[4 * p + 1][:, j * P:(j + 1) * P], xn2[p][:, j, :], ident[:])
                    mm.then_inc(s["x2T_ps"], 1)
                for p in range(2):
                    b = bank[4 * p:4 * p + 4]
                    pe.wait_ge(s["x2T_made"], 2 * i + p + 1)
                    for j in range(J1):
                        mm = pe.matmul(b[0][:, j * E0:(j + 1) * E0], x2T[p][:, j * P:(j + 1) * P], gate0_w[:], start=True, stop=True)
                    mm.then_inc(s["logit_ps"], 1)
                    for n in range(2):
                        for h in range(2):
                            mm = pe.matmul(b[2][I0 * h:I0 * h + I0, 256 * n:256 * n + 256], sw13[:, n, :], x2T[p][:, 256 * h:256 * h + 256], start=True, stop=True)
                    mm.then_inc(s["ab_ps"], 1)
                for p in range(2):
                    b = bank[4 * p:4 * p + 4]
                    pe.wait_ge(s["hid_made"], 2 * i + p + 1)
                    for j in range(J1):
                        h = I0 * (j // 2)
                        mm = pe.matmul(b[3 - j // 2 * 2][:, j * P:(j + 1) * P], hid[p][h:h + I0, (j % 2) * P:(j % 2) * P + P], sw2[h:h + I0, :], start=True, stop=True)
                    mm.then_inc(s["ysh_ps"], 1)
                for p in range(2):
                    b = bank[4 * p:4 * p + 4]
                    here = b[0][:, 256:256 + J1 * E0]
                    pe.wait_ge(s["tanh_l_made"], 2 * i + p + 1)
                    pe.wait_ge(s["prior_made"], 2 * i + p + 1)
                    pe.matmul(here, before[:], taken[p][:].rearrange("q j e -> q (j e)"), start=True, stop=False)
                    pe.matmul(here, ones[:], prior[:, J1 * p:J1 * p + J1, :].rearrange("q j e -> q (j e)"), start=False, stop=True).then_inc(s["pos_ps"], 1)

            repeat(pe, T1, turn)
            def turn(i):
                for p in range(2):
                    pe.wait_ge(s["xe_landed"][p], 16 * (i + 1))
                    for e in range(2):
                        mm = pe.transpose(bank[4 * p][:, e * P:(e + 1) * P], xe[p][:, e, :], ident[:])
                    mm.then_inc(s["xeT_ps"], 1)
                for p in range(2):
                    pe.wait_ge(s["w_landed"][p], 48 * (i + 1))
                    pe.wait_ge(s["xeT_made"], 2 * i + p + 1)
                    for n in range(2):
                        for e in range(2):
                            mm = pe.matmul(bank[4 * p + 1][I0 * e:I0 * e + I0, n * P:(n + 1) * P], w13[p][:, n, e, :], xeT[p][:, e * P:(e + 1) * P], start=True, stop=True)
                    mm.then_inc(s["e_ab_ps"], 1)
                for p in range(2):
                    wait(pe, s["ye_made"], 2 * i)
                    pe.wait_ge(s["e_hid_made"], 2 * i + p + 1)
                    for e in range(2):
                        mm = pe.matmul(bank[4 * p + 2 + e][:, 0:D], e_hid[p][I0 * e:I0 * e + I0, :], w2[p][I0 * e:I0 * e + I0, :], start=True, stop=True)
                    mm.then_inc(s["ye_ps"], 1)

            repeat(pe, T2, turn)

            pe.drain().then_inc(s["phases"], 1)
            pe.wait_ge(s["phases"], 5)
            pe.wait_ge(weights_in, 16 * N_WEIGHT_DMA)
            readers = [[], []]

            def fill(x, after, now):
                for semaphore, value in readers[x]:
                    pe.wait_ge(semaphore, value)
                for semaphore, value in now:
                    pe.wait_ge(semaphore, value)
                readers[x] = after
                return ring[x]

            def scores(att, g):
                wait(pe, s["relu_made"], PAIRS * (att.n - 1) + g - 1)
                if g == 0:
                    pe.wait_ge(s["qkT_act"], 2 * att.n)
                    pe.wait_ge(s["qkT_dve"], 2 * att.n)
                for c in range(2):
                    for h in range(2):
                        part = slice(64 * h, 64 * h + 64)
                        mm = pe.matmul(psum[:, 2 * (g % 2) + h, c * SEQ:(c + 1) * SEQ], kT[att.p][part, g, c * P:(c + 1) * P], qT[att.p][part, g, :], start=True, stop=True)
                mm.then_inc(s["score_ps"], 1)

            def aggregate(q, g):
                hf = g // 4
                if g % 4 == 0:
                    wait(pe, s["aggr_out"], 2 * (q.n - 1) + hf)
                if g == 0:
                    pe.wait_ge(s["v_made"], q.n)
                if g in POOL_PAIRS:
                    pe.wait_ge(s["attn_made_pool"], 2 * (q.n - 1) + POOL_PAIRS.index(g) + 1)
                else:
                    pe.wait_ge(s["attn_made"], (PAIRS - 2) * (q.n - 1) + g - sum(x < g for x in POOL_PAIRS) + 1)
                for j in range(2):
                    for h in range(2):
                        head = 2 * g + h
                        for c in range(2):
                            mm = pe.matmul(psum[:, 4 + j, (head % HALF) * DV:(head % HALF + 1) * DV], attn[g % RING][:, h, c * SEQ + j * P:c * SEQ + (j + 1) * P],
                                           v[q.p][:, c, head * DV:(head + 1) * DV], start=(c == 0), stop=(c == 1))
                mm.then_inc(s["attn_read"], 1)

            def turn_oT(q, hf):
                for j in range(2):
                    x = OT_BANK[hf][j]
                    b = fill(x, [(s["oT_dve" if j else "oT_act"], 2 * (q.n - 1) + hf + 1)], [(s["o_made"], 2 * (q.n - 1) + hf + 1)])
                    for c in range(4):
                        mm = pe.transpose(b[:, c * P:(c + 1) * P], o[:, j, c * P:(c + 1) * P], ident[:])
                    mm.then_inc(s["oT_ps"], 1)

            def half(fetch, front, att, tail):
                if tail:
                    readers[0] = [(s["oT_act"], 2 * (tail.n - 1) + 1)]
                    readers[1] = [(s["oT_dve"], 2 * (tail.n - 1) + 1)]
                for g in range(PAIRS):
                    if att:
                        scores(att, g)
                    if tail and g < 2:
                        aggregate(tail, 6 + g)
                    if att and g >= 2:
                        aggregate(att, g - 2)
                    if front and g == 0:
                        b = fill(0, [(s["x3T_made"], front.n)], [(s["xn3_made"], front.n)])
                        for j in range(2):
                            mm = pe.transpose(b[:, j * P:(j + 1) * P], xn3[:, j, :], ident[:])
                        mm.then_inc(s["x3T_ps"], 1)
                    if front and g == 1:
                        for j in range(2):
                            m = 2 * (front.n - 1) + j + 1
                            b = fill(1 - j, [(s["qk_copied"], m)], [(s["x3T_made"], front.n)] if j == 0 else [])
                            pe.matmul(b[:], x3T[:, j * P:(j + 1) * P], w_qk[:], start=True, stop=True).then_inc(s["qk_ps"], 1)
                    if front and g in (2, 3):
                        for h in range(2):
                            m = 4 * (front.n - 1) + 2 * (g - 2) + h + 1
                            b = fill(1 - h, [(s["v_copied"], m)], [])
                            pe.matmul(b[:], x3T[:, (g - 2) * P:(g - 1) * P], w_v[:, 512 * h:512 * h + 512], start=True, stop=True).then_inc(s["v_ps3"], 1)
                    if front and g in (4, 5):
                        for h in range(2):
                            m = 4 * (front.n - 1) + 2 * (g - 4) + h + 1
                            b = fill(G_BANK[g - 4][h], [(s["silu_made"], m)], [])
                            pe.matmul(b[:], x3T[:, (g - 4) * P:(g - 3) * P], w_g[:, 512 * h:512 * h + 512], start=True, stop=True).then_inc(s["g_ps"], 1)
                    if tail and g == 4:
                        turn_oT(tail, 1)
                    if tail and g == 5:
                        b = fill(1, [(s["x3_made"], tail.n)], [(s["oT_act"], 2 * tail.n), (s["oT_dve"], 2 * tail.n)])
                        for j in range(2):
                            for c in range(PAIRS):
                                mm = pe.matmul(b[:, j * D:(j + 1) * D], oT[:, j, c, :], w_out[:, c, :], start=(c == 0), stop=(c == PAIRS - 1))
                        mm.then_inc(s["y3_ps"], 1)
                    if front and g in (6, 7):
                        for t in range(2):
                            m = 2 * (front.n - 1) + (g - 6) + 1
                            b = fill(t, [(s["qkT_dve" if t else "qkT_act"], m)], [(s["terms_made"], front.n)] if g == 6 and t == 0 else [])
                            b16 = b.bitcast(F16)
                            for a4 in range(4):
                                for j in range(2):
                                    head = HEADS * t + 2 * (4 * (g - 6) + a4)
                                    at = (2 * a4 + j) * P
                                    mm = pe.transpose(b16[:, at:at + P], terms[:, j, head:head + 2, :, :].rearrange("q h m d -> q (h m d)"), ident16[:])
                            mm.then_inc(s["terms_ps"], 1)
                    if att and g == 7:
                        turn_oT(att, 0)

            pipeline(pe, half)
            pe.drain().then_inc(s["phases"], 1)
            pe.wait_ge(s["phases"], 10)
            pe.wait_ge(s["cleared"], 1)
            pe.wait_ge(s["set4"], 8)
            readers = [[], []]
            LAST_USER = (15, 13, 14)

            def fill4(x, after, now):
                for semaphore, value in readers[x] + now:
                    pe.wait_ge(semaphore, value)
                readers[x] = after
                return ring[x]

            def scores4(att, head):
                before_it = head - 3 if head >= 3 else LAST_USER[head] - HEADS
                wait(pe, s["exp_made"], HEADS * (att.n - 1) + before_it + 1)
                if head % 8 == 0:
                    pe.wait_ge(s["k4_out"], 2 * (att.n - 1) + head // 8 + 1)
                    pe.wait_ge(s["q4_out"], 2 * (att.n - 1) + head // 8 + 1)
                part = slice(64 * (head % 2), 64 * (head % 2) + 64)
                for c in range(2):
                    mm = pe.matmul(bank[head % 3][:, c * SEQ:(c + 1) * SEQ], kT4[att.p][part, head // 2, c * P:(c + 1) * P], qT4[att.p][part, head // 2, :], start=True, stop=True)
                mm.then_inc(s["score4_ps"], 1)

            def values4(q, head):
                if head == 0:
                    wait(pe, s["o4_made"], q.n - 1)
                pe.wait_ge(s["exp_made"], HEADS * (q.n - 1) + head + 1)
                for j in range(2):
                    at = (HEADS * j + head) * (DH + 1)
                    for c in range(2):
                        mm = pe.matmul(bank[3][:, at:at + DH + 1], prob[head % 4][:, c * SEQ + j * P:c * SEQ + (j + 1) * P], v4[q.p][:, c, head, :], start=(c == 0), stop=(c == 1))
                mm.then_inc(s["pv_made"], 1)

            def maxima(front, r):
                gp, jp, j = r // 4, r // 2 % 2, r % 2
                wait(pe, s["max_made"], 8 * (front.n - 1) + r)
                if r == 0:
                    pe.wait_ge(s["high_out"], front.n)
                for a2 in range(2):
                    part = slice(32 * (2 * gp + a2), 32 * (2 * gp + a2) + 32)
                    for b2 in range(2):
                        mm = pe.matmul(bank[4 + a2][:, b2 * SEQ:(b2 + 1) * SEQ], q_highT[part, 2 * jp + b2, j * P:(j + 1) * P], k_highT[part, :], start=True, stop=True)
                mm.then_inc(s["max_ps"], 1)

            def turn_terms(front, what, c, x, after):
                b16 = fill4(x, [(s[what + "_out"], 2 * (front.n - 1) + c + 1)], after).bitcast(BF16)
                for a4 in range(4):
                    for j in range(2):
                        head = 2 * (4 * c + a4)
                        at = (2 * a4 + j) * P
                        mm = pe.transpose(b16[:, at:at + P], terms4[:, 1 if what == "k4" else 0, j, head:head + 2, :, :].rearrange("q h m d -> q (h m d)"), ident_b[:])
                mm.then_inc(s[what + "_ps"], 1)

            def half(fetch, front, att, tail, end):
                if att:
                    readers[0] = [(s["q4_out"], 2 * att.n)]
                if end:
                    readers[1] = [(s["h5T_made"], end.n)]
                for g in range(PAIRS):
                    if att:
                        scores4(att, 2 * g)
                        scores4(att, 2 * g + 1)
                    if tail and g == 0:
                        values4(tail, HEADS - 2)
                        values4(tail, HEADS - 1)
                    if att and g >= 1:
                        values4(att, 2 * g - 2)
                        values4(att, 2 * g - 1)
                    if front and g == 0:
                        b = fill4(0, [(s["h4T_made"], front.n)], [(s["xn4_made"], front.n)])
                        for j in range(2):
                            mm = pe.transpose(b[:, j * P:(j + 1) * P], xn4[:, j, :], ident[:])
                        mm.then_inc(s["x4T_ps"], 1)
                        for j in range(2):
                            b = fill4(1 - j, [(s["qkv_out"], 2 * (front.n - 1) + j + 1)], [(s["h4T_made"], front.n)] if j == 0 else [])
                            pe.matmul(b[:, 0:3 * D], h4T[:, j * P:(j + 1) * P], w_qkv[:], start=True, stop=True).then_inc(s["qkv_ps"], 1)
                    if end and g == 1:
                        b = fill4(1, [(s["logit1_out"], end.n)], [(s["h5T_made"], end.n)])
                        for j in range(2):
                            mm = pe.matmul(b[:, j * E1:(j + 1) * E1], h5T[:, j * P:(j + 1) * P], gate1_w[:], start=True, stop=True)
                        mm.then_inc(s["logit1_ps"], 1)
                    if front and g == 1:
                        b16 = fill4(0, [(s["high_out"], front.n)], [(s["high4_made"], front.n)]).bitcast(BF16)
                        for w in range(2):
                            for j in range(2):
                                mm = pe.transpose(b16[:, (2 * w + j) * P:(2 * w + j + 1) * P], high4[:, w, j, :], ident_b[:])
                        mm.then_inc(s["high_ps"], 1)
                    if front and g == 2:
                        turn_terms(front, "k4", 0, 1, [(s["terms4_made"], front.n)])
                    if tail and g == 2:
                        b = fill4(0, [(s["o4T_made"], tail.n)], [(s["o4_made"], tail.n)])
                        for j in range(2):
                            mm = pe.transpose(b[:, j * P:(j + 1) * P], o4[:, j, :], ident[:])
                        mm.then_inc(s["o4T_ps"], 1)
                    if end and g == 2:
                        b = fill4(1, [(s["pos1_out"], end.n)], [(s["onehot1_made"], end.n), (s["prior1_made"], end.n)])
                        pe.matmul(b[:, 0:2 * E1], before[:], onehot_b[:].rearrange("q j e -> q (j e)"), start=True, stop=False)
                        pe.matmul(b[:, 0:2 * E1], ones[:], prior_b[:, 0:2, :].rearrange("q j e -> q (j e)"), start=False, stop=True).then_inc(s["pos1_ps"], 1)
                    if front and g in (2, 3):
                        maxima(front, 2 * (g - 2))
                        maxima(front, 2 * (g - 2) + 1)
                    if front and g == 3:
                        turn_terms(front, "k4", 1, 0, [])
                    if tail and g == 3:
                        b = fill4(1, [(s["x4_made"], tail.n)], [(s["o4T_made"], tail.n)])
                        for j in range(2):
                            mm = pe.matmul(b[:, j * D:(j + 1) * D], o4T[:, j * P:(j + 1) * P], w_o[:], start=True, stop=True)
                        mm.then_inc(s["y4_ps"], 1)
                    if front and g in (5, 6):
                        if g == 5:
                            turn_terms(front, "q4", 0, 0, [(s["max_made"], 8 * (front.n - 1) + 4)])
                        maxima(front, 2 * (g - 3))
                        maxima(front, 2 * (g - 3) + 1)
                    if tail and g == 6:
                        b = fill4(1, [(s["h5T_made"], tail.n)], [(s["x4n_made"], tail.n)])
                        for j in range(2):
                            mm = pe.transpose(b[:, j * P:(j + 1) * P], x4n[tail.p][:, j, D:2 * D], ident[:])
                        mm.then_inc(s["x5T_ps"], 1)
                    if front and g == 7:
                        turn_terms(front, "q4", 1, 0, [(s["max_made"], 8 * front.n)])

            pipeline(pe, half, 5)
            pe.wait_ge(s["all_counted"], 1)
            pe.matmul(bank[7][:, 0:E1], ones[:], prior_b[:, 0, :], start=True, stop=True).then_inc(s["count_ps"], 1)
            def turn(i):
                for p in range(2):
                    wait(pe, s["res_made"], 2 * i)
                    pe.wait_ge(s["got_landed"][p], 16 * (i + 1))
                    pe.transpose(bank[4 * p][:, 0:P], got[p][:, D:2 * D], ident[:]).then_inc(s["g5T_ps"], 1)
                for p in range(2):
                    pe.wait_ge(s["wa_landed"][p], 64 * (i + 1))
                    pe.wait_ge(s["g5T_made"], 2 * i + p + 1)
                    for c in range(CHUNKS):
                        mm = pe.matmul(bank[4 * p + 1 + c // 2][:, (c % 2) * P:(c % 2 + 1) * P] if c < 2 else bank[4 * p + 2][:, (c % 2) * P:(c % 2 + 1) * P],
                                       wa[p][:, c * P:(c + 1) * P], g5T[p][:], start=True, stop=True)
                        if c % 2 == 1:
                            mm.then_inc(s["mid_ps"], 1)
                for p in range(2):
                    pe.wait_ge(s["mid_act"], 2 * i + p + 1)
                    pe.wait_ge(s["mid_dve"], 2 * i + p + 1)
                    pe.matmul(bank[4 * p + 3][:, 0:D], ones_row[:], bb[p][:], start=True, stop=False)
                    for c in range(CHUNKS):
                        mm = pe.matmul(bank[4 * p + 3][:, 0:D], mid[p][:, c, :], wb[p][:, c, :], start=False, stop=(c == CHUNKS - 1))
                    mm.then_inc(s["res_ps"], 1)

            repeat(pe, BLOCKS // 2, turn)

        @block.vector
        def _(dve):
            chain = Chain(dve, dve_chain)
            constants_ready(dve)
            n = chain.step(dve.tensor_scalar(one_less_mix[:], mix[:], -1.0, 1.0, ALU.mult, ALU.add))
            chain.need(n)
            chain.restart()

            def statistics(x, p, signal):
                for j in range(J1):
                    n = chain.step(dve.bn_stats(stats[p][:, j, :], x[:, j, :]))
                chain.need(n)
                for j in range(J1):
                    ins = dve.bn_aggr(meanvar[p][:, j, :], stats[p][:, j, :])
                    if j < J1 - 1:
                        chain.step(ins)
                ins.then_inc(signal, 1)

            def normalise(x, y, p, signal):
                for j in range(J1):
                    ins = dve.tensor_scalar(y[:, j, :], x[:, j, :], meanvar[p][:, j, 0:1], rstd[p][:, j:j + 1], ALU.subtract, ALU.mult)
                    if j < J1 - 1:
                        chain.step(ins)
                ins.then_inc(signal, 1)

            def turn(i):
                for p in range(2):
                    dve.wait_ge(s["x_landed"][p], 16 * (i + 1))
                    statistics(x_in[p], p, s["var1"])
                for p in range(2):
                    dve.wait_ge(s["var1"], 2 * i + p + 1)
                    dve.wait_ge(s["rstd1"], 2 * i + p + 1)
                    normalise(x_in[p], xn[p], p, s["xn_made"])
                for p in range(2):
                    dve.wait_ge(s["xT_made"], 2 * i + p + 1)
                    n = chain.step(dve.tensor_scalar(shifted[p][:], xT[p][:, :, 0:SEQ], one_less_mix[:], None, ALU.mult))
                    chain.need(n)
                    dve.scalar_tensor_tensor(xm[p][:], xT[p][:, :, 1:], mix[:], shifted[p][:], ALU.mult, ALU.add).then_inc(s["xm_made"], 1)
                for p in range(2):
                    dve.wait_ge(s["k_ps"], 2 * i + p + 1)
                    dve.tensor_scalar(ek[p][:], bank[4 * p + 1][:].rearrange("q (a t) -> q a t", a=2), 60.0, None, ALU.min).then_inc(s["kmin"], 1)
                for p in range(2):
                    dve.wait_ge(s["v_ps"], 2 * i + p + 1)
                    dve.wait_ge(s["ek_made"], 2 * i + p + 1)
                    n = chain.step(dve.tensor_tensor(kv[p][:], ek[p][:], bank[4 * p + 2][:].rearrange("q (a t) -> q a t", a=2), ALU.mult))
                    for a2 in range(2):
                        chain.step(dve.tensor_tensor_scan(sum_k[p][:, a2, 1:], decay[:].to_broadcast([P, SEQ]), ek[p][:, a2, :], 0.0, ALU.mult, ALU.add))
                    chain.need(n)
                    for a2 in range(2):
                        n = chain.step(dve.tensor_tensor_scan(sum_kv[p][:, a2, 1:], decay[:].to_broadcast([P, SEQ]), kv[p][:, a2, :], 0.0, ALU.mult, ALU.add))
                    chain.need(n)
                    n1 = chain.step(dve.scalar_tensor_tensor(den[p][:], ek[p][:], first_w[:], sum_k[p][:, :, 0:SEQ], ALU.mult, ALU.add))
                    n2 = chain.step(dve.scalar_tensor_tensor(num[p][:], kv[p][:], first_w[:], sum_kv[p][:, :, 0:SEQ], ALU.mult, ALU.add))
                    chain.need(n1)
                    n = chain.step(dve.tensor_scalar(den[p][:], den[p][:], 1e-16, None, ALU.add))
                    chain.need(n)
                    n = chain.step(dve.reciprocal(rden[p][:], den[p][:]))
                    chain.need(n)
                    n = chain.step(dve.scalar_tensor_tensor(num[p][:], num[p][:], 0.5, rden[p][:], ALU.mult, ALU.mult))
                    chain.need(n)
                    dve.wait_ge(s["tanh_r_made"], 2 * i + p + 1)
                    dve.scalar_tensor_tensor(rw[p][:], tanh_r[p][:], 1.0, num[p][:].rearrange("q a t -> q (a t)"), ALU.add, ALU.mult).then_inc(s["rw_made"], 1)
                for p in range(2):
                    dve.wait_ge(s["y_ps"], 2 * i + p + 1)
                    dve.tensor_tensor(x1[p][:], x_in[p][:], bank[4 * p][:].rearrange("q (j d) -> q j d", j=J1), ALU.add).then_inc(s["x1_made"], 1)
                    dve.wait_ge(s["x1_made"], 2 * i + p + 1)
                    statistics(x1[p], p, s["var2"])
                for p in range(2):
                    wait(dve, s["scattered"][p], 16 * J1 * K0 * i)
                    dve.wait_ge(s["var2"], 2 * i + p + 1)
                    dve.wait_ge(s["rstd2"], 2 * i + p + 1)
                    normalise(x1[p], xn2[p], p, s["xn2_made"])
                for p in range(2):
                    dve.wait_ge(s["tanh_l_made"], 2 * i + p + 1)
                    n = chain.step(dve.tensor_scalar(score[p][:], tanh_l[p][:], 0.5, 0.5, ALU.mult, ALU.add))
                    chain.need(n)
                    n = chain.step(dve.tensor_tensor(biased[p][:], score[p][:], bias0[:].unsqueeze(1).to_broadcast([P, J1, E0]), ALU.add))
                    chain.need(n)
                    for j in range(J1):
                        n = chain.step(dve.max(top[p][:, j, :], biased[p][:, j, :]))
                    chain.need(n)
                    for j in range(J1):
                        n = chain.step(dve.max_index(top_at[p][:, j, :], top[p][:, j, :], biased[p][:, j, :]))
                    chain.need(n)
                    n = chain.step(dve.tensor_copy(chosen[p][:].rearrange("q (j k) -> q j k", j=J1), top_at[p][:, :, 0:K0]))
                    chain.need(n)
                    n = chain.step(dve.tensor_tensor(
                        onehot[p][:].rearrange("q j k e -> q (j k) e"), expert_id[:].unsqueeze(1).to_broadcast([P, J1 * K0, E0]),
                        chosen[p][:].unsqueeze(2).to_broadcast([P, J1 * K0, E0]), ALU.is_equal))
                    chain.need(n)
                    with nc.allow_low_precision(reason="ones and zeros, exact in bfloat16"):
                        dve.tensor_reduce(taken[p][:], onehot[p][:].rearrange("q j k e -> q j e k"), AX, ALU.add).then_inc(s["taken_made"], 1)
                    dve.wait_ge(s["taken_made"], 2 * i + p + 1)
                    if p == 0:
                        wait(dve, s["pos_ps"], 2 * i)
                    for j in range(J1):
                        ins = dve.tensor_tensor(prior[:, J1 * p + j + 1, :], prior[:, J1 * p + j, :], taken[p][:, j, :], ALU.add)
                        if j < J1 - 1:
                            n = chain.step(ins)
                            chain.need(n)
                    ins.then_inc(s["prior_made"], 1)
                    dve.wait_ge(s["prior_made"], 2 * i + p + 1)
                    n = chain.step(dve.tensor_tensor(picked[p][:], onehot[p][:], score[p][:].unsqueeze(2).to_broadcast([P, J1, K0, E0]), ALU.mult))
                    chain.need(n)
                    n = chain.step(dve.tensor_reduce(weight[p][:], picked[p][:], AX, ALU.add))
                    chain.need(n)
                    n = chain.step(dve.tensor_reduce(wsum[p][:], weight[p][:], AX, ALU.add))
                    chain.need(n)
                    n = chain.step(dve.tensor_scalar(wsum[p][:], wsum[p][:], 1e-12, None, ALU.max))
                    chain.need(n)
                    n = chain.step(dve.reciprocal(wsum[p][:], wsum[p][:]))
                    chain.need(n)
                    n = chain.step(dve.tensor_tensor(weight[p][:], weight[p][:], wsum[p][:].unsqueeze(2).to_broadcast([P, J1, K0]), ALU.mult))
                    chain.need(n)
                for p in range(2):
                    dve.wait_ge(s["ab_ps"], 2 * i + p + 1)
                    dve.wait_ge(s["tanh_a_made"], 2 * i + p + 1)
                    n = chain.step(dve.scalar_tensor_tensor(half_h[p][:], tanh_a[p][:], 1.0, bank[4 * p + 2][:, 0:256], ALU.add, ALU.mult))
                    chain.need(n)
                    dve.scalar_tensor_tensor(hid[p][:], half_h[p][:], 0.5, bank[4 * p + 2][:, 256:512], ALU.mult, ALU.mult).then_inc(s["hid_made"], 1)
                for p in range(2):
                    dve.wait_ge(s["pos_ps"], 2 * i + p + 1)
                    n = chain.step(dve.tensor_tensor(
                        picked[p][:], onehot[p][:],
                        bank[4 * p][:, 256:256 + J1 * E0].rearrange("q (j e) -> q j e", j=J1).unsqueeze(2).to_broadcast([P, J1, K0, E0]), ALU.mult))
                    chain.need(n)
                    dve.tensor_reduce(pos[p][:].rearrange("q (j k) -> q j k", j=J1), picked[p][:], AX, ALU.add).then_inc(s["slots_read"], 1)
                    dve.wait_ge(s["slots_read"], 2 * i + p + 1)
                    n = chain.step(dve.tensor_scalar(fits[p][:], pos[p][:], float(CAP), None, ALU.is_lt))
                    n = chain.step(dve.scalar_tensor_tensor(slot[p][:], chosen[p][:], float(CAP), pos[p][:], ALU.mult, ALU.add))
                    chain.need(n)
                    wait(dve, s["route_stored"][p], 16 * i)
                    chain.step(dve.tensor_tensor(route[p][:, :, 0:K0], weight[p][:], fits[p][:].rearrange("q (j k) -> q j k", j=J1), ALU.mult))
                    n = chain.step(dve.scalar_tensor_tensor(slot[p][:], slot[p][:], -float(SLOTS0), fits[p][:], ALU.add, ALU.mult))
                    chain.need(n)
                    dve.tensor_scalar(route[p][:].bitcast(U32)[:, :, K0:2 * K0], slot[p][:].rearrange("q (j k) -> q j k", j=J1), float(SLOTS0), None, ALU.add).then_inc(s["route_made"], 1)
                for p in range(2):
                    dve.wait_ge(s["ysh_ps"], 2 * i + p + 1)
                    wait(dve, s["x1_stored"][p], 16 * i)
                    for h, b in ((0, bank[4 * p + 3]), (1, bank[4 * p + 1])):
                        half = slice(2 * h, 2 * h + 2)
                        ins = dve.tensor_tensor(x1s[p][:, half, :], x1[p][:, half, :], b[:, 256 * h:256 * h + 256].rearrange("q (j d) -> q j d", j=2), ALU.add)
                        if h == 0:
                            chain.step(ins)
                    ins.then_inc(s["x1s_made"], 1)
                for p in range(2):
                    dve.wait_ge(s["pos_ps"], 2 * i + p + 1)
                chain.step(dve.tensor_copy(prior[:, 0, :], prior[:, 2 * J1, :]))
                chain.restart()

            repeat(dve, T1, turn)
            def turn(i):
                for p in range(2):
                    b = bank[4 * p + 1]
                    dve.wait_ge(s["e_ab_ps"], 2 * i + p + 1)
                    dve.wait_ge(s["e_tanh_made"], 2 * i + p + 1)
                    n = chain.step(dve.scalar_tensor_tensor(e_half[p][:], e_tanh[p][:], 1.0, b[:, 0:P], ALU.add, ALU.mult))
                    chain.need(n)
                    dve.scalar_tensor_tensor(e_hid[p][:], e_half[p][:], 0.5, b[:, P:2 * P], ALU.mult, ALU.mult).then_inc(s["e_hid_made"], 1)
                chain.restart()

            repeat(dve, T2, turn)
            dve.drain().then_inc(s["phases"], 1)
            dve.wait_ge(s["phases"], 5)

            def inverse_root(dst, squared, columns, signal=None):
                y, t = dst, newton[:, 0:columns]
                n = chain.step(dve.tensor_scalar(squared, squared, 1e-24, None, ALU.max))
                chain.need(n)
                n = chain.step(dve.tensor_scalar(guess[:, 0:columns].bitcast(U32), squared.bitcast(U32), 1, None, ALU.logical_shift_right))
                chain.need(n)
                n = chain.step(dve.tensor_scalar(y.bitcast(U32), guess[:, 0:columns].bitcast(U32), -1.0, float(0x5F3759DF), ALU.mult, ALU.add))
                chain.need(n)
                for turn in range(3):
                    n = chain.step(dve.tensor_tensor(t, y, y, ALU.mult))
                    chain.need(n)
                    n = chain.step(dve.scalar_tensor_tensor(t, t, -0.5, squared, ALU.mult, ALU.mult))
                    chain.need(n)
                    ins = dve.scalar_tensor_tensor(y, t, 1.5, y, ALU.add, ALU.mult)
                    if turn == 2 and signal:
                        ins.then_inc(signal, 1)
                    else:
                        n = chain.step(ins)
                        chain.need(n)

            def square(q, g):
                dve.wait_ge(s["relu_made"], PAIRS * (q.n - 1) + g + 1)
                r = attn[g % RING]
                dve.tensor_tensor(r[:], r[:], r[:], ALU.mult).then_inc(s["attn_made"], 1)

            def length_of(q, hf):
                dve.wait_ge(s["aggr_sq_made"], 2 * (q.n - 1) + hf + 1)
                n = chain.step(dve.tensor_reduce(o_norm[:].rearrange("q j h -> q (j h)"), aggr_sq[:].rearrange("q j (h d) -> q (j h) d", d=DV), AX, ALU.add))
                chain.need(n)
                inverse_root(o_inv[:].rearrange("q j h -> q (j h)"), o_norm[:].rearrange("q j h -> q (j h)"), 2 * HALF)
                dve.tensor_tensor(o_len[:], o_norm[:], o_inv[:], ALU.mult).then_inc(s["o_len_made"], 1)

            def factor_of(q, hf):
                wait(dve, s["gated"], 4 * (q.n - 1) + 2 * hf)
                dve.wait_ge(s["o_tanh_made"], 2 * (q.n - 1) + hf + 1)
                dve.tensor_tensor(o_factor[:], o_tanh[:], o_inv[:], ALU.mult).then_inc(s["o_factor_made"], 1)

            def gated_output(q, hf):
                wait(dve, s["oT_ps"], 4 * (q.n - 1) + 2 * hf)
                dve.wait_ge(s["gated"], 4 * (q.n - 1) + 2 * hf + 2)
                dve.tensor_tensor(o[:], aggr[:], gate[q.p][:, :, 512 * hf:512 * hf + 512], ALU.mult).then_inc(s["o_made"], 1)

            def take_oT(q, hf):
                dve.wait_ge(s["oT_ps"], 4 * (q.n - 1) + 2 * hf + 2)
                dve.tensor_copy(oT[:, 1, 4 * hf:4 * hf + 4, :], ring[OT_BANK[hf][1]][:].rearrange("q (c t) -> q c t", c=4)).then_inc(s["oT_dve"], 1)

            def combine(front):
                dve.wait_ge(s["x1l_landed"][front.p], 16 * front.k)
                dve.wait_ge(s["yg_landed"][front.p], 16 * 2 * K0 * front.k)
                for k in range(K0):
                    for j in range(2):
                        acc = x1l[front.p] if k == 0 else x2
                        ins = dve.scalar_tensor_tensor(x2[:, j, :], yg[front.p][:, j, k, :], routel[front.p][:, j, k:k + 1], acc[:, j, :], ALU.mult, ALU.add)
                        if k < K0 - 1 or j == 0:
                            n = chain.step(ins)
                    if k < K0 - 1:
                        chain.need(n)
                ins.then_inc(s["x2_made"], 1)
                dve.wait_ge(s["x2_made"], front.n)
                for j in range(2):
                    n = chain.step(dve.bn_stats(stats3[:, j, :], x2[:, j, :]))
                chain.need(n)
                chain.step(dve.bn_aggr(meanvar3[:, 0, :], stats3[:, 0, :]))
                dve.bn_aggr(meanvar3[:, 1, :], stats3[:, 1, :]).then_inc(s["var3"], 1)

            def normalise3(front):
                dve.wait_ge(s["var3"], front.n)
                dve.wait_ge(s["rstd3"], front.n)
                chain.step(dve.tensor_scalar(xn3[:, 0, :], x2[:, 0, :], meanvar3[:, 0, 0:1], rstd3[:, 0:1], ALU.subtract, ALU.mult))
                dve.tensor_scalar(xn3[:, 1, :], x2[:, 1, :], meanvar3[:, 1, 0:1], rstd3[:, 1:2], ALU.subtract, ALU.mult).then_inc(s["xn3_made"], 1)

            def split_terms(front):
                dve.wait_ge(s["high_made"], front.n)
                t3 = lambda x: terms[:, :, :, x, :].rearrange("q j h d -> q (j h) d")
                n = chain.step(dve.tensor_tensor(t3(1), qk[:].rearrange("q j h d -> q (j h) d"), t3(0), ALU.subtract))
                chain.need(n)
                chain.step(dve.tensor_copy(terms[:, :, HEADS:, 2:4, :].rearrange("q j h m d -> q j h (m d)"), terms[:, :, HEADS:, 0:2, :].rearrange("q j h m d -> q j h (m d)")))
                chain.step(dve.tensor_copy(terms[:, :, 0:HEADS, 2, :], terms[:, :, 0:HEADS, 1, :]))
                n = chain.step(dve.tensor_copy(terms[:, :, 0:HEADS, 3, :], terms[:, :, 0:HEADS, 0, :]))
                chain.need(n)
                dve.sem_inc(s["terms_made"], 1)

            def half(fetch, front, att, tail):
                if att:
                    chain.step(dve.tensor_copy(x2_kept[att.p][:], x2[:]))
                    if front:
                        chain.need(chain.count)
                for g in range(PAIRS):
                    if g == 0 and tail:
                        square(tail, PAIRS - 1)
                    if g > 0 and att and g - 1 not in POOL_PAIRS:
                        square(att, g - 1)
                    if front and g == 0:
                        combine(front)
                        normalise3(front)
                    if tail and g == 1:
                        length_of(tail, 1)
                    if front and g == 1:
                        for j in range(2):
                            m = 2 * (front.n - 1) + j + 1
                            dve.wait_ge(s["qk_ps"], m)
                            dve.tensor_copy(qk[:, j, :, :], ring[1 - j][:].rearrange("q (h d) -> q h d", d=DK)).then_inc(s["qk_copied"], 1)
                            dve.wait_ge(s["qk_squared"], m)
                            dve.tensor_reduce(qk_norm[:, j, :], squares[j][:].rearrange("q (h d) -> q h d", d=DK), AX, ALU.add).then_inc(s["sq_reduced"], 1)
                    if tail and g == 2:
                        factor_of(tail, 1)
                    if front and g in (2, 3):
                        for h in range(2):
                            m = 4 * (front.n - 1) + 2 * (g - 2) + h + 1
                            if g == 2 and h == 0:
                                wait(dve, s["attn_read"], PAIRS * (front.n - 2))
                            dve.wait_ge(s["v_ps3"], m)
                            dve.tensor_copy(v[front.p][:, g - 2, 512 * h:512 * h + 512], ring[1 - h][:]).then_inc(s["v_copied"], 1)
                            dve.wait_ge(s["v_squared"], m)
                            dve.tensor_reduce(v_norm[:, g - 2, HALF * h:HALF * h + HALF], squares[h][:].rearrange("q (h d) -> q h d", d=DV), AX, ALU.add).then_inc(s["sq_reduced"], 1)
                    if front and g == 3:
                        dve.wait_ge(s["qk_copied"], 2 * front.n)
                        dve.wait_ge(s["sq_reduced"], 6 * (front.n - 1) + 2)
                        inverse_root(qk_inv[:].rearrange("q j h -> q (j h)"), qk_norm[:].rearrange("q j h -> q (j h)"), 4 * HEADS)
                        qk3 = qk[:].rearrange("q j h d -> q (j h) d")
                        dve.tensor_tensor(qk3, qk3, qk_inv[:].rearrange("q j h -> q (j h)").unsqueeze(2).to_broadcast([P, 4 * HEADS, DK]), ALU.mult).then_inc(s["qk_scaled"], 1)
                        dve.wait_ge(s["sq_reduced"], 6 * front.n)
                        inverse_root(v_inv[:].rearrange("q j h -> q (j h)"), v_norm[:].rearrange("q j h -> q (j h)"), 2 * HEADS, s["v_inv_made"])
                    if tail and g == 3:
                        gated_output(tail, 1)
                    if front and g in (4, 5):
                        for h in range(2):
                            m = 4 * (front.n - 1) + 2 * (g - 4) + h + 1
                            wait(dve, s["gate_made"], 2 * (front.n - 1) + (g - 4))
                            dve.wait_ge(s["g_tanh"], m)
                            dve.scalar_tensor_tensor(silu_g[:, 512 * h:512 * h + 512], tanh_g[h][:], 1.0, ring[G_BANK[g - 4][h]][:], ALU.add, ALU.mult).then_inc(s["silu_made"], 1)
                    if front and g == 5:
                        split_terms(front)
                    if tail and g == 4:
                        take_oT(tail, 1)
                    if att and g == 5:
                        length_of(att, 0)
                    if tail and g == 6:
                        wait(dve, s["x3_stored"][tail.p], 16 * (tail.k - 1))
                        dve.wait_ge(s["y3_ps"], tail.n)
                        dve.tensor_tensor(x3[tail.p][:], x2_kept[tail.p][:], ring[1][:, 0:2 * D].rearrange("q (j d) -> q j d", j=2), ALU.add).then_inc(s["x3_made"], 1)
                    if att and g == 6:
                        factor_of(att, 0)
                    if front and g in (6, 7):
                        c = g - 6
                        dve.wait_ge(s["terms_ps"], 4 * (front.n - 1) + 2 * c + 2)
                        dve.tensor_copy(kT[front.p][:, 4 * c:4 * c + 4, :].rearrange("q a t -> q (a t)"), ring[1].bitcast(F16)).then_inc(s["qkT_dve"], 1)
                    if att and g == 7:
                        gated_output(att, 0)
                        take_oT(att, 0)
                chain.restart()

            pipeline(dve, half)
            dve.drain().then_inc(s["phases"], 1)
            dve.wait_ge(s["phases"], 10)
            dve.wait_ge(s["cleared"], 1)
            dve.wait_ge(weights_in, 16 * N_WEIGHT_DMA)
            dve.wait_ge(s["set4"], 8)
            n = chain.step(dve.tensor_copy(token_f[:], token_start[:]))
            chain.need(n)
            chain.restart()

            def moments(x, stats_x, meanvar_x, done):
                for j in range(2):
                    n = chain.step(dve.bn_stats(stats_x[:, j, :], x[:, j, 0:D]))
                chain.need(n)
                chain.step(dve.bn_aggr(meanvar_x[:, 0, :], stats_x[:, 0, :]))
                dve.bn_aggr(meanvar_x[:, 1, :], stats_x[:, 1, :]).then_inc(s[done], 1)

            def normed(y, x, meanvar_x, rstd_x, done):
                chain.step(dve.tensor_scalar(y[:, 0, :], x[:, 0, 0:D], meanvar_x[:, 0, 0:1], rstd_x[:, 0:1], ALU.subtract, ALU.mult))
                dve.tensor_scalar(y[:, 1, :], x[:, 1, 0:D], meanvar_x[:, 1, 0:1], rstd_x[:, 1:2], ALU.subtract, ALU.mult).then_inc(s[done], 1)

            def take_maxima(front, r):
                gp, jp, j = r // 4, r // 2 % 2, r % 2
                dve.wait_ge(s["max_ps"], 8 * (front.n - 1) + r + 1)
                dst = terms4[:, 0, j, :, 6, 0].rearrange("q (g a b c) -> q g a b c", g=2, a=2, b=2)[:, gp, :, jp, :]
                with nc.allow_low_precision(reason="any value near the maximum serves: the sum divides it out"):
                    dve.tensor_reduce(dst, psum[:, 4:6, :].rearrange("q a (b k) -> q a b k", b=2), AX, ALU.max, negate=True).then_inc(s["max_made"], 1)

            def half(fetch, front, att, tail, end):
                for g in range(PAIRS):
                    if front and g == 0:
                        dve.wait_ge(s["x3l_landed"][front.p], 16 * front.k)
                        wait(dve, s["x3n_made"], front.n - 1)
                        moments(x3l[front.p], stats4, meanvar4, "var4")
                        dve.wait_ge(s["var4"], front.n)
                        dve.wait_ge(s["rstd4"], front.n)
                        normed(xn4, x3l[front.p], meanvar4, rstd4, "xn4_made")
                        wait(dve, s["pv_made"], HEADS * (front.n - 2))
                        for j in range(2):
                            b = ring[1 - j]
                            dve.wait_ge(s["qkv_ps"], 2 * (front.n - 1) + j + 1)
                            chain.step(dve.tensor_tensor(v4[front.p][:, j, :, 0:DH], b[:, 2 * D:3 * D].rearrange("q (h d) -> q h d", d=DH),
                                                         b_qkv[:, 2 * D:3 * D].rearrange("q (h d) -> q h d", d=DH), ALU.add))
                            dve.tensor_tensor(qk4[:, :, j, :], b[:, 0:2 * D].rearrange("q (w d) -> q w d", w=2), b_qkv[:, 0:2 * D].rearrange("q (w d) -> q w d", w=2), ALU.add).then_inc(s["qkv_out"], 1)
                    if tail and g == 1:
                        dve.wait_ge(s["pv_made"], HEADS * tail.n)
                        sums = bank[3][:, 0:2 * HEADS * (DH + 1)].rearrange("q (j h d) -> q (j h) d", j=2, d=DH + 1)
                        wait(dve, s["o4T_ps"], tail.n - 1)
                        n = chain.step(dve.reciprocal(rsum[:].rearrange("q j h -> q (j h)"), sums[:, :, DH]))
                        chain.need(n)
                        dve.tensor_tensor(o4[:].rearrange("q j (h d) -> q (j h) d", d=DH), sums[:, :, 0:DH],
                                          rsum[:].rearrange("q j h -> q (j h)").unsqueeze(2).to_broadcast([P, 2 * HEADS, DH]), ALU.mult).then_inc(s["o4_made"], 1)
                    if end and g == 1:
                        dve.wait_ge(s["logit1_ps"], end.n)
                        dve.tensor_tensor(logit[:], ring[1][:, 0:2 * E1].rearrange("q (j e) -> q j e", j=2), gate1_b[:].unsqueeze(1).to_broadcast([P, 2, E1]), ALU.add).then_inc(s["logit1_sum"], 1)
                        dve.wait_ge(s["logit1_sum"], end.n)
                        dve.sem_inc(s["logit1_out"], 1)
                    if front and g == 1:
                        flat = terms4[:].rearrange("q w j h m d -> q (w j h) m d")
                        qk_flat = qk4[:].rearrange("q w j (h d) -> q (w j h) d", d=DH)
                        dve.wait_ge(s["high4_made"], front.n)
                        dve.tensor_tensor(qk4[:], qk4[:], high4[:], ALU.subtract).then_inc(s["rest4_made"], 1)
                        dve.wait_ge(s["high_ps"], front.n)
                        chain.step(dve.tensor_tensor(
                            q_highT[:], ring[0].bitcast(BF16)[:, 0:SEQ].unsqueeze(1).to_broadcast([P, 4, SEQ]), head_mask[:].unsqueeze(2).to_broadcast([P, 4, SEQ]), ALU.mult))
                        dve.tensor_copy(k_highT[:], ring[0].bitcast(BF16)[:, SEQ:2 * SEQ]).then_inc(s["high_out"], 1)
                        tq = terms4[:, 0, :, :, :, :].rearrange("q j h m d -> q (j h) m d")
                        tk = terms4[:, 1, :, :, :, :].rearrange("q j h m d -> q (j h) m d")
                        half_n = 2 * HEADS
                        dve.wait_ge(s["mid4_made"], front.n)
                        high = high4[:].rearrange("q w j (h d) -> q w (j h) d", d=DH)
                        for w, dst in ((0, tq[:, :, 1:4:2, :]), (1, tk[:, :, 2:6:3, :])):
                            chain.step(dve.tensor_copy(dst, high[:, w, :, :].unsqueeze(2).to_broadcast([P, half_n, 2, DH])))
                        chain.step(dve.tensor_copy(tq[:, :, 2, :], tq[:, :, 4, :]))
                        chain.step(dve.tensor_copy(tk[:, :, 1, :], tk[:, :, 4, :]))
                        chain.step(dve.tensor_tensor(tq[:, :, 5, :], qk_flat[:, 0:half_n, :], tq[:, :, 4, :], ALU.subtract))
                        n = chain.step(dve.tensor_tensor(tk[:, :, 3, :], qk_flat[:, half_n:, :], tk[:, :, 4, :], ALU.subtract))
                        chain.need(n)
                        dve.sem_inc(s["terms4_made"], 1)
                    if end and g == 1:
                        for j in range(2):
                            n = chain.step(dve.max(top_b[:, j, :], logit[:, j, :]))
                        chain.need(n)
                        for j in range(2):
                            n = chain.step(dve.max_index(top_at_b[:, j, :], top_b[:, j, :], logit[:, j, :]))
                        chain.need(n)
                        n = chain.step(dve.tensor_copy(chosen_b[:], top_at_b[:, :, 0]))
                        chain.need(n)
                        dve.tensor_tensor(onehot_b[:], expert_id[:, 0:E1].unsqueeze(1).to_broadcast([P, 2, E1]), chosen_b[:].unsqueeze(2).to_broadcast([P, 2, E1]), ALU.is_equal).then_inc(s["onehot1_made"], 1)
                        dve.wait_ge(s["onehot1_made"], end.n)
                        n = chain.step(dve.tensor_tensor(prior_b[:, 1, :], prior_b[:, 0, :], onehot_b[:, 0, :], ALU.add))
                        chain.need(n)
                        dve.tensor_tensor(prior_b[:, 2, :], prior_b[:, 1, :], onehot_b[:, 1, :], ALU.add).then_inc(s["prior1_made"], 1)
                    if front and g in (2, 3):
                        take_maxima(front, 2 * (g - 2))
                        take_maxima(front, 2 * (g - 2) + 1)
                    if end and g == 3:
                        dve.wait_ge(s["pos1_ps"], end.n)
                        dve.tensor_tensor(picked_b[:], onehot_b[:], ring[1][:, 0:2 * E1].rearrange("q (j e) -> q j e", j=2), ALU.mult).then_inc(s["pos1_out"], 1)
                        dve.wait_ge(s["pos1_out"], end.n)
                        n = chain.step(dve.tensor_reduce(pos_b[:], picked_b[:], AX, ALU.add))
                        chain.step(dve.tensor_copy(prior_b[:, 0, :], prior_b[:, 2, :]))
                        wait(dve, s["token_sent"][end.p], 32 * (end.k - 1))
                        n = chain.step(dve.tensor_copy(token[end.p][:], token_f[:]))
                        chain.need(n)
                        chain.step(dve.tensor_scalar(token_f[:], token_f[:], float(SEQ), None, ALU.add))
                        dve.scalar_tensor_tensor(slot_b[end.p][:], chosen_b[:], float(TOK), pos_b[:], ALU.mult, ALU.add).then_inc(s["slot1_made"], 1)
                    if tail and g == 4:
                        wait(dve, s["sum_made"], tail.n - 2)
                        dve.wait_ge(s["y4_ps"], tail.n)
                        dve.tensor_tensor(x4[tail.p][:], x3_kept[tail.p][:], ring[1][:, 0:2 * D].rearrange("q (j d) -> q j d", j=2), ALU.add).then_inc(s["x4_made"], 1)
                        dve.wait_ge(s["x4_made"], tail.n)
                        moments(x4[tail.p], stats5, meanvar5, "var5")
                    if front and g in (5, 6):
                        take_maxima(front, 2 * (g - 3))
                    if tail and g == 5:
                        dve.wait_ge(s["var5"], tail.n)
                        dve.wait_ge(s["rstd5"], tail.n)
                        wait(dve, s["x4_stored"][tail.p], 16 * (tail.k - 1))
                        normed(x4n[tail.p][:, :, D:2 * D], x4[tail.p], meanvar5, rstd5, "x4n_made")
                    if front and g in (5, 6):
                        take_maxima(front, 2 * (g - 3) + 1)
                if front or tail or end:
                    chain.restart()

            pipeline(dve, half, 5)
            dve.sem_inc(s["all_counted"], 1)
            dve.wait_ge(s["count_ps"], 1)
            n = chain.step(dve.tensor_copy(count[:], bank[7][:, 0:E1]))
            chain.need(n)
            n = chain.step(dve.tensor_tensor(steps[:], count[:].unsqueeze(2).to_broadcast([P, E1, TOK // P]), steps_of[:].unsqueeze(1).to_broadcast([P, E1, TOK // P]), ALU.is_gt))
            chain.need(n)
            n = chain.step(dve.tensor_reduce(blocks_of[:], steps[:], AX, ALU.add))
            chain.need(n)
            n = chain.step(dve.tensor_copy(blocks_to[:], blocks_of[:]))
            chain.need(n)
            for e in range(1, E1):
                n = chain.step(dve.tensor_tensor(blocks_to[:, e:e + 1], blocks_to[:, e:e + 1], blocks_to[:, e - 1:e], ALU.add))
                chain.need(n)
            n = chain.step(dve.tensor_tensor(passed[:], block_id[:].unsqueeze(2).to_broadcast([P, BLOCKS, E1]), blocks_to[:].unsqueeze(1).to_broadcast([P, BLOCKS, E1]), ALU.is_ge))
            chain.need(n)
            n = chain.step(dve.tensor_reduce(block_expert[:], passed[:], AX, ALU.add))
            n = chain.step(dve.tensor_tensor(passed_blocks[:], passed[:], blocks_of[:].unsqueeze(1).to_broadcast([P, BLOCKS, E1]), ALU.mult))
            chain.need(n)
            n = chain.step(dve.tensor_reduce(block_start[:], passed_blocks[:], AX, ALU.add))
            chain.need(n)
            n = chain.step(dve.tensor_tensor(block_row[:], block_id[:], block_start[:], ALU.subtract))
            chain.need(n)
            n = chain.step(dve.tensor_scalar(block_row[:], block_row[:], float(P), None, ALU.mult))
            chain.need(n)
            n = chain.step(dve.scalar_tensor_tensor(block_row[:], block_expert[:], float(TOK), block_row[:], ALU.mult, ALU.add))
            chain.need(n)
            chain.step(dve.tensor_scalar(block_row_i[:], block_row[:], float(NO_ROWS), None, ALU.min))
            n = chain.step(dve.tensor_scalar(block_expert_i[:], block_expert[:], float(E1 - 1), None, ALU.min))
            chain.need(n)
            dve.sem_inc(s["plan_made"], 1)
            chain.restart()
            def turn(i):
                for p in range(2):
                    dve.wait_ge(s["wa_landed"][p], 64 * (i + 1))
                    dve.wait_ge(s["mid_ps"], 4 * i + 2 * p + 2)
                    chain.step(dve.tensor_scalar(mid[p][:, 2, :], bank[4 * p + 2][:, 0:P], ba[p][:, 2:3], 0.0, ALU.add, ALU.max))
                    dve.tensor_scalar(mid[p][:, 3, :], bank[4 * p + 2][:, P:2 * P], ba[p][:, 3:4], 0.0, ALU.add, ALU.max).then_inc(s["mid_dve"], 1)
                for p in range(2):
                    wait(dve, s["res_sent"][p], 16 * i)
                    dve.wait_ge(s["res_ps"], 2 * i + p + 1)
                    dve.tensor_tensor(res[p][:], got[p][:, 0:D], bank[4 * p + 3][:, 0:D], ALU.add).then_inc(s["res_made"], 1)
                chain.restart()

            repeat(dve, BLOCKS // 2, turn)


_OUT = ((BATCH, SEQ, D), "float32")


def lay_out(inputs):
    import numpy as np

    def get(name):
        return np.asarray(inputs[name])

    eye = np.eye(P, dtype=np.float32)
    return {
        "x": get("L0_attn_x").reshape(TOK, D),
        "eye": eye,
        "upper": np.triu(np.ones((P, P), np.float32), 1),
        "ones": np.ones((P, P), np.float32),
        "ids": np.tile(np.arange(E0, dtype=np.float32), (P, 1)),
        "w_rkvo": np.stack([get("L0_attn_" + n).T for n in ("Wk", "Wv", "Wr", "Wo")], axis=1),
        "time_decay": get("L0_attn_time_decay").reshape(P, 1),
        "time_first": get("L0_attn_time_first").reshape(P, 1),
        "time_mix": get("L0_attn_time_mix").reshape(P, 1),
        "bias0": get("L0_ffn_bias"),
        "gate0_w": get("L0_ffn_gate_w").T,
        "sw13": np.stack([get("L0_ffn_sw1").T, get("L0_ffn_sw3").T], axis=1),
        "sw2": get("L0_ffn_sw2").T,
        "w1": get("L0_ffn_W1").transpose(1, 0, 2),
        "w3": get("L0_ffn_W3").transpose(1, 0, 2),
        "w_qk": np.concatenate([x.reshape(D, HEADS, DK + DV)[:, :, :DK].reshape(D, -1) for x in (get("L1_attn_Wqg"), get("L1_attn_Wkv"))], axis=1),
        "w_v": get("L1_attn_Wkv").reshape(D, HEADS, DK + DV)[:, :, DK:].reshape(D, -1),
        "w_g": get("L1_attn_Wqg").reshape(D, HEADS, DK + DV)[:, :, DK:].reshape(D, -1),
        "w_out": get("L1_attn_Wout").reshape(PAIRS, P, D).transpose(1, 0, 2),
        "w_qkv": np.concatenate([get("L1_ffn_" + n) for n in ("wq", "wk", "wv")], axis=1),
        "b_qkv": np.concatenate([get("L1_ffn_" + n) for n in ("bq", "bk", "bv")]),
        "w_o": get("L1_ffn_wo"),
        "b_o": get("L1_ffn_bo"),
        "gate1_w": get("L1_ffn_gate_w"),
        "gate1_b": get("L1_ffn_gate_b"),
        "norms": np.stack([get("L1_ffn_" + n) for n in ("ln1_g", "ln1_b", "ln2_g", "ln2_b")], axis=1),
        "head_mask": (np.arange(P)[:, None] // DH % 4 == np.arange(4)[None, :]).astype(np.float32),
        "token_start": (np.arange(P)[:, None] + P * np.arange(2)[None, :]).astype(np.float32),
        "steps_of": (P * np.arange(TOK // P)).astype(np.float32),
        "block_id": np.arange(BLOCKS, dtype=np.float32),
        "wa": get("L1_ffn_w1"),
        "wb": get("L1_ffn_w2"),
        "ba": get("L1_ffn_b1").reshape(E1, CHUNKS, P).transpose(0, 2, 1),
        "bb": get("L1_ffn_b2"),
        "w2": get("L0_ffn_W2").reshape(E0 * I0, D),
    }


def kernel(**inputs):
    import numpy as np
    import concourse.bacc as bacc
    from concourse import mybir as my
    from concourse.bass_utils import run_bass_kernel_spmd

    nc = bacc.Bacc("TRN2", target_bir_lowering=False, num_devices=1)
    arrays, aps = {}, {}
    for name, value in lay_out(inputs).items():
        value = np.ascontiguousarray(value)
        arrays["in_" + name] = value
        aps[name] = nc.dram_tensor("in_" + name, value.shape, my.dt.from_np(value.dtype), kind="ExternalInput").ap()
    out = nc.dram_tensor("out_0", (TOK, D), my.dt.float32, kind="ExternalOutput").ap()
    build_program(nc, aps, out)
    result = run_bass_kernel_spmd(nc, [arrays], core_ids=[0])
    return result.results[0]["out_0"].reshape(_OUT[0])
```

```python
from contextlib import ExitStack

import concourse.bass as bass
from concourse import mybir

F32 = mybir.dt.float32
BF16 = mybir.dt.bfloat16
F16 = mybir.dt.float16
U32 = mybir.dt.uint32
I32 = mybir.dt.int32
ALU = mybir.AluOpType
ACT = mybir.ActivationFunctionType
AX = mybir.AxisListType.X

P = 128
D = 128
BATCH, SEQ = 16, 256
TOK = BATCH * SEQ
LN_EPS = 1e-5

HEADS, DK, DV = 16, 16, 64
HALF = HEADS // 2
PAIRS = HEADS // 2
TERMS = 4

DH = 8
COLS = 32
TERMS1 = 8
SCALE = float(DH) ** -0.5
E1, F1 = 8, 512
CHUNKS = F1 // P
BLOCKS = TOK // P + E1
AHEAD = 8
NO_ROWS = E1 * TOK

E0, K0, CAP, I0 = 32, 4, 128, 64
SLOTS0 = E0 * CAP


class Chain:

    def __init__(self, engine, semaphore):
        self.engine, self.semaphore, self.count = engine, semaphore, 0

    def step(self, instruction):
        self.count += 1
        instruction.then_inc(self.semaphore, 1)
        return self.count

    def need(self, count):
        self.engine.wait_ge(self.semaphore, count)

    def restart(self):
        self.engine.wait_ge(self.semaphore, self.count)
        self.engine.sem_clear(self.semaphore)
        self.count = 0


class Seq:

    def __init__(self, turn, place):
        self.n, self.p, self.k = 2 * turn + place + 1, place % 2, turn + place // 2 + 1


def pipeline(eng, half, stages=4):
    def step(turn, at):
        work = [Seq(turn, at - lag) if not isinstance(turn, int) or 0 <= at - lag < BATCH else None
                for lag in range(stages)]
        half(*work)

    lead = stages - 1
    turns = (BATCH - lead) // 2
    for at in range(lead + 2):
        step(0, at)
    with eng.Fori(1, turns) as turn:
        step(turn, lead)
        step(turn, lead + 1)
    for at in range(lead + 2 * turns, BATCH + lead):
        step(0, at)


def repeat(eng, turns, turn):
    turn(0)
    with eng.Fori(1, turns) as i:
        turn(i)


def wait(eng, semaphore, value):
    if not isinstance(value, int) or value > 0:
        eng.wait_ge(semaphore, value)


def rows(ap, first, n, tiles):
    return ap[bass.ds(first, n)].rearrange("(j q) d -> q j d", q=P)


def build_program(nc, a, out):
    with ExitStack() as ctx:
        scope = [ctx]

        def sb(name, shape, dt=F32):
            return scope[-1].enter_context(nc.sbuf_tensor(name, shape, dt))

        def two(name, shape, dt=F32):
            return [sb(f"{name}{p}", shape, dt) for p in range(2)]

        sem_scope = [ctx]

        def sem(name):
            return sem_scope[-1].enter_context(nc.semaphore(name))

        def sems(name):
            return [sem(f"{name}{p}") for p in range(2)]

        def dram(name, shape, dt=F32):
            return nc.dram_tensor(name, shape, dt, kind="Internal").ap()

        psum = ctx.enter_context(nc.psum_tensor("psum", [P, 8, 512], F32))
        bank = [psum[:, n, :] for n in range(8)]

        x1_dram = dram("x1_dram", (TOK, D))
        route_dram = dram("route_dram", (TOK, 2 * K0))
        xe_dram = dram("xe_dram", (SLOTS0, D))
        ye_dram = dram("ye_dram", (SLOTS0, D))
        x3_dram = dram("x3_dram", (TOK, D))
        x4n_dram = dram("x4n_dram", (TOK, 2 * D))
        token_dram = dram("token_dram", (NO_ROWS + P, 1), U32)

        ident = sb("ident", [P, P])
        before = sb("before", [P, P], BF16)
        ones = sb("ones", [P, P], BF16)
        expert_id = sb("expert_id", [P, E0])
        zero_rows = sb("zero_rows", [P, 4, D])
        minus_half = sb("minus_half", [P, 16])
        w_rkvo = sb("w_rkvo", [P, 4, D])
        decay_in = sb("decay_in", [P, 1])
        decay_exp = sb("decay_exp", [P, 1])
        decay = sb("decay", [P, 1])
        first_in = sb("first_in", [P, 1])
        first_w = sb("first_w", [P, 1])
        mix = sb("mix", [P, 1])
        one_less_mix = sb("one_less_mix", [P, 1])
        gate0_w = sb("gate0_w", [P, E0])
        bias0 = sb("bias0", [P, E0])
        sw13 = sb("sw13", [P, 2, I0])
        sw2 = sb("sw2", [P, D])

        consts_in = sem("consts_in")
        casts_in = sem("casts_in")
        made = sem("made")
        weights_in = sem("weights_in")
        decay_ready = sem("decay_ready")
        xe_zeroed = sem("xe_zeroed")
        N_CONST_DMA, N_CAST_DMA, N_MADE, N_WEIGHT_DMA = 7, 8, 9, 16

        def constants_ready(eng):
            eng.wait_ge(consts_in, 16 * N_CONST_DMA)
            eng.wait_ge(casts_in, 16 * N_CAST_DMA)
            eng.wait_ge(made, N_MADE)
            eng.wait_ge(decay_ready, 3)

        ident16 = sb("ident16", [P, P], F16)
        ident_b = sb("ident_b", [P, P], BF16)
        w_qk = sb("w_qk", [P, 2 * HEADS * DK])
        w_v = sb("w_v", [P, HEADS * DV])
        w_g = sb("w_g", [P, HEADS * DV])
        w_out = sb("w_out", [P, PAIRS, D])
        w_qkv = sb("w_qkv", [P, 3 * D])
        b_qkv = sb("b_qkv", [P, 3 * D])
        w_o = sb("w_o", [P, D])
        b_o = sb("b_o", [P, D])
        gate1_w = sb("gate1_w", [P, E1])
        gate1_b = sb("gate1_b", [P, E1])
        norms = sb("norms", [P, 4])
        head_mask = sb("head_mask", [P, 4])
        token_start = sb("token_start", [P, 2])
        steps_of = sb("steps_of", [P, TOK // P])
        block_id = sb("block_id", [P, BLOCKS])
        ones_row = sb("ones_row", [1, P])

        scope.append(ctx.enter_context(ExitStack()))
        U1 = 512
        J1 = U1 // P
        x_in = two("x_in", [P, J1, D])
        stats = two("stats", [P, J1, 6])
        meanvar = two("meanvar", [P, J1, 2])
        veps = two("veps", [P, J1])
        rstd = two("rstd", [P, J1])
        xn = two("xn", [P, J1, D])
        xT = two("xT", [P, 2, SEQ + 1])
        shifted = two("shifted", [P, 2, SEQ])
        xm = two("xm", [P, 2, SEQ])
        ek = two("ek", [P, 2, SEQ])
        kv = two("kv", [P, 2, SEQ])
        tanh_r = two("tanh_r", [P, U1])
        sum_kv = two("sum_kv", [P, 2, SEQ + 1])
        sum_k = two("sum_k", [P, 2, SEQ + 1])
        num = two("num", [P, 2, SEQ])
        den = two("den", [P, 2, SEQ])
        rden = two("rden", [P, 2, SEQ])
        rw = two("rw", [P, U1])
        x1 = two("x1", [P, J1, D])
        x1s = two("x1s", [P, J1, D])
        xn2 = two("xn2", [P, J1, D])
        rows_out = two("rows_out", [P, J1, D])
        x2T = two("x2T", [P, U1])
        tanh_l = two("tanh_l", [P, J1, E0])
        score = two("score", [P, J1, E0])
        biased = two("biased", [P, J1, E0])
        top = two("top", [P, J1, 8])
        top_at = two("top_at", [P, J1, 8], U32)
        chosen = two("chosen", [P, J1 * K0])
        onehot = two("onehot", [P, J1, K0, E0])
        taken = two("taken", [P, J1, E0], BF16)
        prior = sb("prior", [P, 2 * J1 + 1, E0], BF16)
        picked = two("picked", [P, J1, K0, E0])
        pos = two("pos", [P, J1 * K0])
        weight = two("weight", [P, J1, K0])
        wsum = two("wsum", [P, J1])
        fits = two("fits", [P, J1 * K0])
        slot = two("slot", [P, J1 * K0])
        route = two("route", [P, J1, 2 * K0])
        tanh_a = two("tanh_a", [P, 2 * P])
        half_h = two("half_h", [P, 2 * P])
        hid = two("hid", [P, 2 * P])

        s = {}
        for name in ("scattered", "w_landed", "w2_landed"):
            s[name] = sems(name)
        sem_scope.append(ctx.enter_context(ExitStack()))
        for name in "x_landed x1_stored route_stored xe_landed ye_stored".split():
            s[name] = sems(name)
        for name in ("var1 rstd1 xn_made xnT_ps xT_made xm_made k_ps v_ps r_ps kmin ek_made tanh_r_made "
                     "rw_made y_ps x1_made var2 rstd2 xn2_made rows_out_made x2T_ps x2T_made logit_ps ab_ps tanh_l_made tanh_a_made "
                     "taken_made prior_made pos_ps slots_read route_made hid_made ysh_ps x1s_made "
                     "xeT_ps xeT_made e_ab_ps e_tanh_made e_hid_made ye_ps ye_made").split():
            s[name] = sem(name)
        early = [x for name, value in s.items() if name not in ("scattered", "w_landed", "w2_landed")
                 for x in (value if isinstance(value, list) else [value])]
        sem_scope.pop().close()
        dve_chain = sem("dve_chain")
        pool_chain = sem("pool_chain")
        pool_turn = sem("pool_turn")
        phase1_units = TOK // U1
        T1 = phase1_units // 2

        pairs = E0 // 2
        T2 = pairs // 2
        xe = two("xe", [P, 2, D])
        w13 = two("w13", [P, 2, 2, I0])
        w2 = two("w2", [P, D])
        xeT = two("xeT", [P, 2 * P])
        e_tanh = two("e_tanh", [P, P])
        e_half = two("e_half", [P, P])
        e_hid = two("e_hid", [P, P])
        ye = two("ye", [P, 2, D])

        scope.pop().close()
        scope.append(ctx.enter_context(ExitStack()))
        x1l = two("x1l", [P, 2, D])
        routel = two("routel", [P, 2, 2 * K0])
        yg = two("yg", [P, 2, K0, D])
        x2 = two("x2", [P, 2, D])
        x2_kept = two("x2_kept", [P, 2, D])
        stats3 = sb("stats3", [P, 2, 6])
        meanvar3 = sb("meanvar3", [P, 2, 2])
        veps3 = sb("veps3", [P, 2])
        rstd3 = sb("rstd3", [P, 2])
        xn3 = sb("xn3", [P, 2, D])
        x3T = sb("x3T", [P, SEQ])
        qk = sb("qk", [P, 2, 2 * HEADS, DK])
        squares = two("squares", [P, 512])
        norm3 = sb("norm3", [P, 6 * HEADS])
        qk_norm = norm3[:, 0:4 * HEADS].rearrange("q (j h) -> q j h", j=2)
        v_norm = norm3[:, 4 * HEADS:].rearrange("q (j h) -> q j h", j=2)
        o_norm = sb("o_norm", [P, 2 * HALF])
        o_len = sb("o_len", [P, 2 * HALF])
        o_tanh = sb("o_tanh", [P, 2 * HALF])
        o_factor = sb("o_factor", [P, 2 * HALF])
        guess = sb("guess", [P, 6 * HEADS])
        newton = sb("newton", [P, 6 * HEADS])
        inv3 = sb("inv3", [P, 6 * HEADS])
        o_inv = sb("o_inv", [P, 2 * HALF])
        o_max = sb("o_max", [P, 2 * HALF])
        terms = sb("terms", [P, 2, 2 * HEADS, TERMS, DK], F16)
        qT = two("qT", [P, PAIRS, SEQ], F16)
        kT = two("kT", [P, PAIRS, SEQ], F16)
        v = two("v", [P, 2, HEADS * DV])
        tanh_g = two("tanh_g", [P, 512])
        silu_g = two("silu_g", [P, HEADS * DV])
        gate = two("gate", [P, 2, HEADS * DV])
        RING = 4
        attn = [sb(f"attn{n}", [P, 2, 512]) for n in range(RING)]
        aggr = sb("aggr", [P, 2, 512])
        aggr_sq = sb("aggr_sq", [P, 2, 512])
        o = sb("o", [P, 2, 512])
        oT = sb("oT", [P, 2, PAIRS, P])
        x3 = two("x3", [P, 2, D])
        sem_scope.append(ctx.enter_context(ExitStack()))
        again = "var3 rstd3 xn3_made x3T_ps x3T_made qk_ps v_ps3 g_ps".split()
        for name in again:
            s[name] = sem(name)
        middle = [s[name] for name in again]
        sem_scope.pop().close()
        for name in ("x1l_landed", "routel_landed", "yg_landed", "x3_stored"):
            s[name] = sems(name)
        for name in ("x2_made qk_squared qk_copied v_squared v_copied "
                     "sq_reduced g_tanh silu_made gate_made qk_scaled high_made terms_made terms_ps qkT_act qkT_dve inv_made v_made "
                     "score_ps relu_made attn_made attn_made_pool attn_read aggr_out aggr_sq_made o_norm_made o_len_made o_tanh_made "
                     "o_factor_made gated o_made oT_ps oT_act oT_dve y3_ps x3_made yg_cleared phases").split():
            s[name] = sem(name)
        ring = [bank[6], bank[7]]
        OT_BANK = ((0, 1), (1, 0))
        G_BANK = ((1, 0), (1, 0))
        POOL_PAIRS = (2, 3, 6)

        scope.pop().close()
        x3l = two("x3l", [P, 2, D])
        x3_kept = two("x3_kept", [P, 2, D])
        stats4 = sb("stats4", [P, 2, 6])
        meanvar4 = sb("meanvar4", [P, 2, 2])
        veps4 = sb("veps4", [P, 2])
        rstd4 = sb("rstd4", [P, 2])
        rstd4_in = sb("rstd4_in", [P, 2])
        rstd4_norm = sb("rstd4_norm", [P, 2])
        x3n = two("x3n", [P, 2, D])
        xn4 = sb("xn4", [P, 2, D])
        h4T = sb("h4T", [P, SEQ])
        qk4 = sb("qk4", [P, 2, 2, D])
        v4 = two("v4", [P, 2, HEADS, COLS])
        pvT = two("pvT", [P, 2 * SEQ])
        terms4 = sb("terms4", [P, 2, 2, HEADS, TERMS1, DH], BF16)
        high4 = sb("high4", [P, 2, 2, D], BF16)
        k_highT = sb("k_highT", [P, SEQ], BF16)
        q_highT = sb("q_highT", [P, 4, SEQ], BF16)
        qT4 = two("qT4", [P, PAIRS, SEQ], BF16)
        kT4 = two("kT4", [P, PAIRS, SEQ], BF16)
        prob = [sb(f"prob{n}", [P, 2 * SEQ]) for n in range(4)]
        rsum = sb("rsum", [P, 2, HALF])
        o4 = sb("o4", [P, 2, D])
        o4T = sb("o4T", [P, SEQ])
        stats5 = sb("stats5", [P, 2, 6])
        meanvar5 = sb("meanvar5", [P, 2, 2])
        veps5 = sb("veps5", [P, 2])
        rstd5 = sb("rstd5", [P, 2])
        x3_plain = two("x3_plain", [P, 2, D])
        x4 = two("x4", [P, 2, D])
        x4n = two("x4n", [P, 2, 2 * D])
        h5T = sb("h5T", [P, SEQ])
        logit = sb("logit", [P, 2, E1])
        top_b = sb("top_b", [P, 2, 8])
        top_at_b = sb("top_at_b", [P, 2, 8], U32)
        chosen_b = sb("chosen_b", [P, 2])
        onehot_b = sb("onehot_b", [P, 2, E1], BF16)
        prior_b = sb("prior_b", [P, 3, E1], BF16)
        picked_b = sb("picked_b", [P, 2, E1])
        pos_b = sb("pos_b", [P, 2])
        slot_b = two("slot_b", [P, 2], U32)
        token = two("token", [P, 2], U32)
        token_f = sb("token_f", [P, 2])
        no_token = sb("no_token", [P, E1 * TOK // P + 1], U32)
        for name in ("x3l_landed", "x4_stored", "token_sent"):
            s[name] = sems(name)
        for name in ("kept_made var4 rstd4 xn4_made x4T_ps h4T_made qkv_ps qkv_out high4_made rest4_made mid4_made terms4_made "
                     "high_ps high_out max_ps max_made k4_ps k4_out q4_ps q4_out score4_ps exp_made pv_made pvT_out pv_turned o4_made o4T_ps "
                     "o4T_made y4_ps rstd4_in x3n_made x4_made sum_made plain_made var5 rstd5 x4n_made x5T_ps h5T_made logit1_ps logit1_sum logit1_out onehot1_made prior1_made pos1_ps pos1_out "
                     "slot1_made set4 table_cleared").split():
            s[name] = sem(name)
        count = sb("count", [P, E1])
        steps = sb("steps", [P, E1, TOK // P])
        blocks_of = sb("blocks_of", [P, E1])
        blocks_to = sb("blocks_to", [P, E1])
        passed = sb("passed", [P, BLOCKS, E1])
        passed_blocks = sb("passed_blocks", [P, BLOCKS, E1])
        block_expert = sb("block_expert", [P, BLOCKS])
        block_start = sb("block_start", [P, BLOCKS])
        block_row = sb("block_row", [P, BLOCKS])
        block_expert_i = sb("block_expert_i", [P, BLOCKS], I32)
        own_row = sb("own_row", [P, BLOCKS])
        block_at = sb("block_at", [P, 1])
        block_at_i = sb("block_at_i", [P, 1], U32)
        block_tokens = sb("block_tokens", [P, P], U32)
        block_tokens_f = sb("block_tokens_f", [P, P])
        rows_of = sb("rows_of", [P, BLOCKS], U32)
        gather_at = [sb(f"gather_at{n}", [P, 1], U32) for n in range(AHEAD)]
        scatter_at = [sb(f"scatter_at{n}", [P, 1], U32) for n in range(AHEAD)]
        got = [sb(f"got{n}", [P, 2 * D]) for n in range(AHEAD)]
        wa = sb("wa", [P, E1, F1])
        wb = sb("wb", [P, E1 * CHUNKS, D])
        wa_now = two("wa_now", [P, F1])
        ba = sb("ba", [P, E1 * CHUNKS])
        bb = sb("bb", [1, E1 * D])
        g5T = two("g5T", [P, P])
        mid = two("mid", [P, CHUNKS, P])
        res = [sb(f"res{n}", [P, D]) for n in range(AHEAD)]
        for name in ("got_landed", "res_sent"):
            s[name] = [sem(f"{name}{n}") for n in range(AHEAD)]
        for name in ("all_counted count_ps plan_made experts_in tokens_landed tokens_out tokens_ps rows_made wa_made at_made "
                     "g5T_ps g5T_made mid_ps mid_act mid_dve res_ps res_made cleared").split():
            s[name] = sem(name)

        block = ctx.enter_context(nc.Block())

        @block.sync
        def _(sp):
            for p in range(2):
                sp.dma_start(x_in[p][:], rows(a["x"], p * U1, U1, J1)).then_inc(s["x_landed"][p], 16)
            for dst, src in ((ident[:], a["eye"]), (w_rkvo[:], a["w_rkvo"]), (decay_in[:], a["time_decay"]),
                             (first_in[:], a["time_first"]), (mix[:], a["time_mix"]), (expert_id[:], a["ids"]),
                             (bias0[:], a["bias0"].partition_broadcast(P))):
                sp.dma_start(dst, src).then_inc(consts_in, 16)
            sp.wait_ge(made, N_MADE)
            for n in range(SLOTS0 // U1):
                sp.dma_start(rows(xe_dram, n * U1, U1, J1), zero_rows[:]).then_inc(xe_zeroed, 16)

            for dst, src in ((w_qk[:], a["w_qk"]), (w_v[:], a["w_v"]), (w_g[:], a["w_g"]), (w_out[:], a["w_out"]),
                             (w_qkv[:], a["w_qkv"]), (b_qkv[:], a["b_qkv"].partition_broadcast(P)), (w_o[:], a["w_o"]),
                             (b_o[:], a["b_o"].partition_broadcast(P)), (gate1_w[:], a["gate1_w"]),
                             (gate1_b[:], a["gate1_b"].partition_broadcast(P)), (norms[:], a["norms"]), (head_mask[:], a["head_mask"]),
                             (token_start[:], a["token_start"]), (steps_of[:], a["steps_of"].partition_broadcast(P)),
                             (block_id[:], a["block_id"].partition_broadcast(P)), (ones_row[:], a["ones"][0:1, :])):
                sp.dma_start(dst, src).then_inc(weights_in, 16)

            def load_unit(i, p):
                sp.dma_start(x_in[p][:], rows(a["x"], (2 * i + p) * U1, U1, J1)).then_inc(s["x_landed"][p], 16)

            def turn(i, last=False):
                if not last:
                    for p in range(2):
                        sp.wait_ge(s["x1_made"], 2 * i + p + 1)
                        load_unit(i + 1, p)
                for p in range(2):
                    sp.wait_ge(s["route_made"], 2 * i + p + 1)
                    sp.dma_start(rows(route_dram, (2 * i + p) * U1, U1, J1), route[p][:]).then_inc(s["route_stored"][p], 16)
                for p in range(2):
                    sp.wait_ge(s["x1s_made"], 2 * i + p + 1)
                    sp.dma_start(rows(x1_dram, (2 * i + p) * U1, U1, J1), x1s[p][:]).then_inc(s["x1_stored"][p], 16)

            with sp.Fori(0, T1 - 1) as i:
                turn(i)
            turn(T1 - 1, last=True)

            for p in range(2):
                sp.wait_ge(s["scattered"][p], 16 * J1 * K0 * T1)
            def load_slots(i, p):
                sp.dma_start(xe[p][:], rows(xe_dram, (2 * i + p) * 2 * CAP, 2 * CAP, 2)).then_inc(s["xe_landed"][p], 16)

            def turn(i, last=False):
                if not last:
                    for p in range(2):
                        sp.wait_ge(s["xeT_ps"], 2 * i + p + 1)
                        load_slots(i + 1, p)
                for p in range(2):
                    sp.wait_ge(s["ye_made"], 2 * i + p + 1)
                    sp.dma_start(rows(ye_dram, (2 * i + p) * 2 * CAP, 2 * CAP, 2), ye[p][:]).then_inc(s["ye_stored"][p], 16)

            for p in range(2):
                load_slots(0, p)
            with sp.Fori(0, T2 - 1) as i:
                turn(i)
            turn(T2 - 1, last=True)

            for p in range(2):
                sp.wait_ge(s["x1_stored"][p], 16 * T1)
                sp.wait_ge(s["route_stored"][p], 16 * T1)
                sp.wait_ge(s["ye_stored"][p], 16 * T2)
            sp.sem_inc(s["phases"], 1)
            sp.wait_ge(s["phases"], 5)
            for semaphore in early:
                sp.sem_clear(semaphore)
            sp.sem_inc(s["cleared"], 1)

            def half(fetch, front, att, tail):
                if fetch:
                    wait(sp, s["x2_made"], fetch.n - 2)
                    sp.dma_start(x1l[fetch.p][:], rows(x1_dram, (fetch.n - 1) * SEQ, SEQ, 2)).then_inc(s["x1l_landed"][fetch.p], 16)
                    sp.dma_start(routel[fetch.p][:], rows(route_dram, (fetch.n - 1) * SEQ, SEQ, 2)).then_inc(s["routel_landed"][fetch.p], 16)
                if tail:
                    sp.wait_ge(s["x3_made"], tail.n)
                    sp.dma_start(rows(x3_dram, (tail.n - 1) * SEQ, SEQ, 2), x3[tail.p][:]).then_inc(s["x3_stored"][tail.p], 16)

            pipeline(sp, half)
            for p in range(2):
                sp.wait_ge(s["x3_stored"][p], 16 * BATCH // 2)
            sp.sem_inc(s["phases"], 1)
            sp.wait_ge(s["phases"], 10)
            for semaphore in middle:
                sp.sem_clear(semaphore)
            sp.sem_inc(s["cleared"], 1)
            def half(fetch, front, att, tail, end):
                if fetch:
                    wait(sp, s["kept_made"], fetch.n - 2)
                    sp.dma_start(x3l[fetch.p][:], rows(x3_dram, (fetch.n - 1) * SEQ, SEQ, 2)).then_inc(s["x3l_landed"][fetch.p], 16)
                if tail:
                    sp.wait_ge(s["x4n_made"], tail.n)
                    sp.wait_ge(s["sum_made"], tail.n)
                    sp.dma_start(rows(x4n_dram, (tail.n - 1) * SEQ, SEQ, 2), x4n[tail.p][:]).then_inc(s["x4_stored"][tail.p], 16)

            pipeline(sp, half, 5)
            for p in range(2):
                sp.wait_ge(s["x4_stored"][p], 16 * BATCH // 2)

        @block.gpsimd
        def _(pool):
            def hold(semaphore, value):
                if not isinstance(value, int) or value > 0:
                    pool.wait_ge(semaphore, value)
                    pool.sem_inc(pool_turn, 1)

            chain = Chain(pool, pool_chain)
            pool.memset(zero_rows[:], 0.0).then_inc(made, 1)
            pool.memset(minus_half[:], -0.5).then_inc(made, 1)
            for p in range(2):
                pool.memset(xT[p][:, :, 0:1], 0.0).then_inc(made, 1)
                pool.memset(sum_kv[p][:, :, 0:1], 0.0).then_inc(made, 1)
                pool.memset(sum_k[p][:, :, 0:1], 0.0).then_inc(made, 1)
                if p == 0:
                    pool.memset(prior[:, 0:1, :], 0.0).then_inc(made, 1)
            for dst, src in ((before[:], a["upper"]), (gate0_w[:], a["gate0_w"]), (sw13[:], a["sw13"]),
                             (sw2[0:I0, :], a["sw2"]), (sw2[I0:P, :], a["sw2"]), (ones[:], a["ones"]),
                             (ident16[:], a["eye"]), (ident_b[:], a["eye"])):
                pool.dma_start(dst, src).then_inc(casts_in, 16)
            last_slot = pool.to_reg(SLOTS0 - 1)
            pool.wait_ge(made, N_MADE)

            def scatter_rows(unit, p):
                pool.wait_ge(xe_zeroed, 16 * (SLOTS0 // U1))
                hold(s["route_made"], unit)
                hold(s["rows_out_made"], unit)
                where = route[p][:].bitcast(U32)
                for j in range(J1):
                    for k in range(K0):
                        pool.indirect_dma_start(
                            xe_dram, bass.IndirectOffsetOnAxis(ap=where[:, j, K0 + k:K0 + k + 1], axis=0),
                            rows_out[p][:, j, :], None, bounds_check=last_slot, oob_is_err=False,
                        ).then_inc(s["scattered"][p], 16)

            def turn(i):
                for n, (var, ready) in enumerate((("var1", "rstd1"), ("var2", "rstd2"))):
                    for p in range(2):
                        hold(s[var], 2 * i + p + 1)
                        m = chain.step(pool.tensor_scalar(veps[p][:], meanvar[p][:, :, 1], 1.0, LN_EPS, ALU.mult, ALU.add))
                        chain.need(m)
                        pool.tensor_tensor(rstd[p][:], veps[p][:], minus_half[:, 0:J1], ALU.pow).then_inc(s[ready], 1)
                    if not isinstance(i, int):
                        scatter_rows(2 * i + n - 1, n)
                chain.restart()

            repeat(pool, T1, turn)
            for p in range(2):
                scatter_rows(2 * T1 + p - 1, p)

            def turn(i):
                for p in range(2):
                    hold(s["e_ab_ps"], 2 * i + p - 1)
                    pool.dma_start(w13[p][:, 0, :, :], a["w1"][:, bass.ds((2 * i + p) * 2, 2), :]).then_inc(s["w_landed"][p], 16)
                    pool.dma_start(w13[p][:, 1, :, :], a["w3"][:, bass.ds((2 * i + p) * 2, 2), :]).then_inc(s["w_landed"][p], 16)
                for p in range(2):
                    hold(s["ye_ps"], 2 * i + p - 1)
                    pool.dma_start(w2[p][:], a["w2"][bass.ds((2 * i + p) * P, P)]).then_inc(s["w2_landed"][p], 16)

            repeat(pool, T2, turn)
            pool.drain().then_inc(s["phases"], 1)
            pool.wait_ge(s["phases"], 5)
            for p in range(2):
                pool.memset(yg[p][:], 0.0).then_inc(s["yg_cleared"], 1)
            pool.wait_ge(s["yg_cleared"], 2)

            def square(att, g):
                hold(s["relu_made"], PAIRS * (att.n - 1) + g + 1)
                r = attn[g % RING]
                pool.tensor_tensor(r[:], r[:], r[:], ALU.mult).then_inc(s["attn_made_pool"], 1)

            def length_of(q, hf):
                hold(s["o_norm_made"], 2 * (q.n - 1) + hf + 1)
                n = chain.step(pool.tensor_scalar(o_max[:], o_norm[:], 1e-24, None, ALU.max))
                chain.need(n)
                n = chain.step(pool.tensor_tensor(o_inv[:], o_max[:], minus_half[:], ALU.pow))
                chain.need(n)
                pool.tensor_tensor(o_len[:], o_norm[:], o_inv[:], ALU.mult).then_inc(s["o_len_made"], 1)

            def scale_gate(q, hf):
                hold(s["gate_made"], 2 * q.n)
                hold(s["o_tanh_made"], 2 * (q.n - 1) + hf + 1)
                pool.tensor_tensor(o_factor[:], o_tanh[:], o_inv[:], ALU.mult).then_inc(s["o_factor_made"], 1)
                hold(s["o_factor_made"], 2 * (q.n - 1) + hf + 1)
                for j in range(2):
                    part = gate[q.p][:, j, 512 * hf:512 * hf + 512].rearrange("q (h d) -> q h d", d=DV)
                    ins = pool.tensor_tensor(part, part, o_factor[:, HALF * j:HALF * j + HALF].unsqueeze(2).to_broadcast([P, HALF, DV]), ALU.mult)
                    ins.then_inc(s["gated"], 1)

            def half(fetch, front, att, tail):
                if fetch:
                    if not isinstance(fetch.n, int) or fetch.n > 2:
                        hold(s["x2_made"], fetch.n - 2)
                    hold(s["routel_landed"][fetch.p], 16 * fetch.k)
                    where = routel[fetch.p][:].bitcast(U32)
                    for j in range(2):
                        for k in range(K0):
                            pool.indirect_dma_start(
                                yg[fetch.p][:, j, k, :], None, ye_dram,
                                bass.IndirectOffsetOnAxis(ap=where[:, j, K0 + k:K0 + k + 1], axis=0),
                                bounds_check=last_slot, oob_is_err=False,
                            ).then_inc(s["yg_landed"][fetch.p], 16)
                if tail:
                    length_of(tail, 1)
                if att:
                    square(att, POOL_PAIRS[0])
                if tail:
                    scale_gate(tail, 1)
                if att:
                    square(att, POOL_PAIRS[1])
                if front:
                    hold(s["inv_made"], front.n)
                    hold(s["v_copied"], 4 * front.n)
                    vv = v[front.p][:].rearrange("q j (h d) -> q (j h) d", d=DV)
                    pool.tensor_tensor(vv, vv, inv3[:, 4 * HEADS:].unsqueeze(2).to_broadcast([P, 2 * HEADS, DV]), ALU.mult).then_inc(s["v_made"], 1)
                if att:
                    length_of(att, 0)
                if fetch:
                    hold(s["var3"], fetch.n)
                    n = chain.step(pool.tensor_scalar(veps3[:], meanvar3[:, :, 1], 1.0, LN_EPS, ALU.mult, ALU.add))
                    chain.need(n)
                    pool.tensor_tensor(rstd3[:], veps3[:], minus_half[:, 0:2], ALU.pow).then_inc(s["rstd3"], 1)
                if att:
                    scale_gate(att, 0)
                if att:
                    square(att, POOL_PAIRS[2])
                chain.restart()

            pipeline(pool, half)
            pool.drain().then_inc(s["phases"], 1)
            pool.wait_ge(s["phases"], 10)
            pool.wait_ge(s["cleared"], 2)
            no_more = pool.to_reg(NO_ROWS - 1)
            last_token = pool.to_reg(TOK - 1)
            pool.memset(no_token[:], TOK).then_inc(s["set4"], 1)
            pool.memset(terms4[:], 0.0).then_inc(s["set4"], 1)
            for p in range(2):
                pool.memset(v4[p][:], 0.0).then_inc(s["set4"], 1)
            for n in range(AHEAD):
                pool.memset(got[n][:], 0.0).then_inc(s["set4"], 1)
            pool.memset(prior_b[:, 0:1, :], 0.0).then_inc(s["set4"], 1)
            pool.wait_ge(s["set4"], 5 + AHEAD)
            pool.memset(terms4[:, 1, :, :, 6, 0:1].rearrange("q j h a -> q (j h) a"), 1.0).then_inc(s["set4"], 1)
            for p in range(2):
                pool.memset(v4[p][:, :, :, DH:DH + 1], 1.0).then_inc(s["set4"], 1)
            pool.wait_ge(s["set4"], 8 + AHEAD)

            def inverse_deviation(var, meanvar_x, veps_x, rstd_x, done, count):
                hold(s[var], count)
                n = chain.step(pool.tensor_scalar(veps_x[:], meanvar_x[:, :, 1], 1.0, LN_EPS, ALU.mult, ALU.add))
                chain.need(n)
                pool.tensor_tensor(rstd_x[:], veps_x[:], minus_half[:, 0:2], ALU.pow).then_inc(s[done], 1)

            def half(fetch, front, att, tail, end):
                if att:
                    if not isinstance(att.n, int) or att.n > 2:
                        hold(s["x4_made"], att.n - 2)
                    if not isinstance(att.n, int) or att.n > 2:
                        hold(s["sum_made"], att.n - 2)
                    pool.tensor_copy(x3_plain[att.p][:], x3l[att.p][:]).then_inc(s["plain_made"], 1)
                    hold(s["x3n_made"], att.n)
                    pool.tensor_tensor(x3_kept[att.p][:], x3n[att.p][:], b_o[:].unsqueeze(1).to_broadcast([P, 2, D]), ALU.add).then_inc(s["kept_made"], 1)
                if tail:
                    inverse_deviation("var5", meanvar5, veps5, rstd5, "rstd5", tail.n)
                if end:
                    hold(s["slot1_made"], end.n)
                    pool.wait_ge(s["table_cleared"], 16)
                    for j in range(2):
                        pool.indirect_dma_start(
                            token_dram, bass.IndirectOffsetOnAxis(ap=slot_b[end.p][:, j:j + 1], axis=0),
                            token[end.p][:, j:j + 1], None, bounds_check=no_more, oob_is_err=False,
                        ).then_inc(s["token_sent"][end.p], 16)
                if tail:
                    if not isinstance(tail.k, int) or tail.k > 1:
                        hold(s["x4_stored"][tail.p], 16 * (tail.k - 1))
                    hold(s["plain_made"], tail.n)
                    pool.tensor_tensor(x4n[tail.p][:, :, 0:D], x4[tail.p][:], x3_plain[tail.p][:], ALU.add).then_inc(s["sum_made"], 1)
                if fetch:
                    inverse_deviation("var4", meanvar4, veps4, rstd4_in, "rstd4_in", fetch.n)
                    hold(s["rstd4_in"], fetch.n)
                    n = chain.step(pool.tensor_tensor(veps4[:], rstd4_in[:], rstd4_in[:], ALU.mult))
                    chain.need(n)
                    n = chain.step(pool.tensor_tensor(veps4[:], veps4[:], meanvar4[:, :, 1], ALU.mult))
                    chain.need(n)
                    n = chain.step(pool.tensor_scalar(veps4[:], veps4[:], 1.0, LN_EPS, ALU.mult, ALU.add))
                    chain.need(n)
                    n = chain.step(pool.tensor_tensor(rstd4_norm[:], veps4[:], minus_half[:, 0:2], ALU.pow))
                    chain.need(n)
                    pool.tensor_tensor(rstd4[:], rstd4_norm[:], rstd4_in[:], ALU.mult).then_inc(s["rstd4"], 1)
                    chain.step(pool.tensor_scalar(x3n[fetch.p][:, 0, :], x3l[fetch.p][:, 0, :], meanvar4[:, 0, 0:1], rstd4_in[:, 0:1], ALU.subtract, ALU.mult))
                    pool.tensor_scalar(x3n[fetch.p][:, 1, :], x3l[fetch.p][:, 1, :], meanvar4[:, 1, 0:1], rstd4_in[:, 1:2], ALU.subtract, ALU.mult).then_inc(s["x3n_made"], 1)
                if fetch or tail:
                    chain.restart()

            pipeline(pool, half, 5)
            for p in range(2):
                pool.wait_ge(s["x4_stored"][p], 16 * BATCH // 2)

            def rows_for(dst, turn, q):
                pool.tensor_copy(dst[q][:], rows_of[:, bass.ds(AHEAD * turn + q, 1)]).then_inc(s["at_made"], 1)

            def gather(turn, q, made):
                if not isinstance(turn, int) or turn > 0:
                    hold(s["got_landed"][q], 16 * turn)
                rows_for(gather_at, turn, q)
                hold(s["at_made"], made)
                pool.indirect_dma_start(
                    got[q][:], None, x4n_dram, bass.IndirectOffsetOnAxis(ap=gather_at[q][:], axis=0),
                    bounds_check=last_token, oob_is_err=False).then_inc(s["got_landed"][q], 16)

            def scatter(turn, q, made):
                hold(s["res_sent"][q], 16 * turn)
                rows_for(scatter_at, turn, q)
                hold(s["at_made"], made)
                hold(s["res_made"], AHEAD * turn + q + 1)
                pool.indirect_dma_start(
                    out, bass.IndirectOffsetOnAxis(ap=scatter_at[q][:], axis=0), res[q][:], None,
                    bounds_check=last_token, oob_is_err=False).then_inc(s["res_sent"][q], 16)

            for p in range(2):
                pool.wait_ge(s["token_sent"][p], 32 * BATCH // 2)
            pool.wait_ge(s["plan_made"], 1)
            pool.indirect_dma_start(
                block_tokens[:], None, token_dram.rearrange("(b q) a -> b (q a)", q=P), bass.IndirectOffsetOnAxis(ap=block_at_i[:], axis=0),
                bounds_check=pool.to_reg(NO_ROWS // P), oob_is_err=False).then_inc(s["tokens_landed"], 16)
            pool.wait_ge(s["rows_made"], 1)
            for q in range(AHEAD):
                gather(0, q, q + 1)

            def turn(i):
                for q in range(AHEAD):
                    scatter(i, q, AHEAD * (2 * i + 1) + 2 * q + 1)
                    gather(i + 1, q, AHEAD * (2 * i + 1) + 2 * q + 2)

            repeat(pool, BLOCKS // AHEAD - 1, turn)
            for q in range(AHEAD):
                scatter(BLOCKS // AHEAD - 1, q, AHEAD * (2 * (BLOCKS // AHEAD) - 1) + q + 1)
            for q in range(AHEAD):
                pool.wait_ge(s["res_sent"][q], 16 * BLOCKS // AHEAD)

        @block.scalar
        def _(act):
            act.wait_ge(consts_in, 16 * N_CONST_DMA)
            act.activation(decay_exp[:], decay_in[:], ACT.Exp).then_inc(decay_ready, 1)
            act.wait_ge(decay_ready, 1)
            act.activation(decay[:], decay_exp[:], ACT.Exp, scale=-1.0).then_inc(decay_ready, 1)
            act.activation(first_w[:], first_in[:], ACT.Exp).then_inc(decay_ready, 1)
            constants_ready(act)

            def turn(i):
                for p in range(2):
                    act.wait_ge(s["xnT_ps"], 2 * i + p + 1)
                    act.activation(xT[p][:, :, 1:], bank[4 * p][:].rearrange("q (a t) -> q a t", a=2), ACT.Copy).then_inc(s["xT_made"], 1)
                for p in range(2):
                    act.wait_ge(s["kmin"], 2 * i + p + 1)
                    act.activation(ek[p][:], ek[p][:], ACT.Exp).then_inc(s["ek_made"], 1)
                    act.wait_ge(s["r_ps"], 2 * i + p + 1)
                    act.activation(tanh_r[p][:], bank[4 * p + 3][:], ACT.Tanh, scale=0.5).then_inc(s["tanh_r_made"], 1)
                for p in range(2):
                    act.wait_ge(s["x2T_ps"], 2 * i + p + 1)
                    act.activation(x2T[p][:], bank[4 * p + 1][:], ACT.Copy).then_inc(s["x2T_made"], 1)
                for p in range(2):
                    act.wait_ge(s["logit_ps"], 2 * i + p + 1)
                    act.activation(tanh_l[p][:], bank[4 * p][:, 0:J1 * E0].rearrange("q (j e) -> q j e", j=J1), ACT.Tanh, scale=0.5).then_inc(s["tanh_l_made"], 1)
                    act.wait_ge(s["ab_ps"], 2 * i + p + 1)
                    act.activation(tanh_a[p][:], bank[4 * p + 2][:, 0:256], ACT.Tanh, scale=0.5).then_inc(s["tanh_a_made"], 1)
                for p in range(2):
                    wait(act, s["scattered"][p], 16 * J1 * K0 * i)
                    act.wait_ge(s["xn2_made"], 2 * i + p + 1)
                    act.activation(rows_out[p][:], xn2[p][:], ACT.Copy).then_inc(s["rows_out_made"], 1)

            repeat(act, T1, turn)

            def turn(i):
                for p in range(2):
                    act.wait_ge(s["xeT_ps"], 2 * i + p + 1)
                    act.activation(xeT[p][:], bank[4 * p][:, 0:256], ACT.Copy).then_inc(s["xeT_made"], 1)
                for p in range(2):
                    act.wait_ge(s["e_ab_ps"], 2 * i + p + 1)
                    act.activation(e_tanh[p][:], bank[4 * p + 1][:, 0:P], ACT.Tanh, scale=0.5).then_inc(s["e_tanh_made"], 1)
                for p in range(2):
                    wait(act, s["ye_stored"][p], 16 * i)
                    act.wait_ge(s["ye_ps"], 2 * i + p + 1)
                    act.activation(ye[p][:, 0, :], bank[4 * p + 2][:, 0:D], ACT.Copy)
                    act.activation(ye[p][:, 1, :], bank[4 * p + 3][:, 0:D], ACT.Copy).then_inc(s["ye_made"], 1)

            repeat(act, T2, turn)

            act.drain().then_inc(s["phases"], 1)
            act.wait_ge(s["phases"], 5)

            def relu(att, g):
                r = attn[g % RING]
                wait(act, s["attn_read"], PAIRS * (att.n - 1) + g + 1 - RING)
                act.wait_ge(s["score_ps"], PAIRS * (att.n - 1) + g + 1)
                act.activation(r[:], psum[:, 2 * (g % 2):2 * (g % 2) + 2, :], ACT.Relu).then_inc(s["relu_made"], 1)

            def square_of(front, k, src):
                wait(act, s["sq_reduced"], 6 * (front.n - 1) + k - 1)
                act.activation(squares[k % 2][:], src, ACT.Square).then_inc(s["qk_squared"] if k < 2 else s["v_squared"], 1)

            def gate_tanh(front, j):
                wait(act, s["o_made"], 2 * (front.n - 2))
                act.wait_ge(s["silu_made"], 4 * (front.n - 1) + 2 * j + 2)
                act.activation(gate[front.p][:, j, :], silu_g[j][:], ACT.Tanh, scale=0.5).then_inc(s["gate_made"], 1)

            def take_aggregate(q, hf):
                wait(act, s["o_made"], 2 * (q.n - 1) + hf)
                act.wait_ge(s["attn_read"], PAIRS * (q.n - 1) + 4 * hf + 4)
                act.activation(aggr[:], psum[:, 4:6, :], ACT.Copy).then_inc(s["aggr_out"], 1)
                act.wait_ge(s["aggr_out"], 2 * (q.n - 1) + hf + 1)
                act.activation(aggr_sq[:], aggr[:], ACT.Square).then_inc(s["aggr_sq_made"], 1)

            def tanh_of_norm(q, hf):
                wait(act, s["o_factor_made"], 2 * (q.n - 1) + hf)
                act.wait_ge(s["o_len_made"], 2 * (q.n - 1) + hf + 1)
                act.activation(o_tanh[:], o_len[:], ACT.Tanh).then_inc(s["o_tanh_made"], 1)

            def take_oT(q, hf):
                act.wait_ge(s["oT_ps"], 4 * (q.n - 1) + 2 * hf + 1)
                act.activation(oT[:, 0, 4 * hf:4 * hf + 4, :], ring[OT_BANK[hf][0]][:].rearrange("q (c t) -> q c t", c=4), ACT.Copy).then_inc(s["oT_act"], 1)

            def half(fetch, front, att, tail):
                for g in range(PAIRS):
                    if att:
                        relu(att, g)
                    if front and g == 0:
                        for j in range(2):
                            act.wait_ge(s["qk_copied"], 2 * (front.n - 1) + j + 1)
                            square_of(front, j, qk[:, j, :, :].rearrange("q h d -> q (h d)"))
                    if tail and g == 0:
                        take_aggregate(tail, 1)
                    if tail and g == 2:
                        tanh_of_norm(tail, 1)
                    if front and g in (1, 2):
                        for h in range(2):
                            act.wait_ge(s["v_copied"], 4 * (front.n - 1) + 2 * (g - 1) + h + 1)
                            square_of(front, 2 + 2 * (g - 1) + h, v[front.p][:, g - 1, 512 * h:512 * h + 512])
                    if front and g in (3, 4):
                        for h in range(2):
                            m = 4 * (front.n - 1) + 2 * (g - 3) + h + 1
                            act.wait_ge(s["g_ps"], m)
                            wait(act, s["silu_made"], m - 2)
                            act.activation(tanh_g[h][:], ring[G_BANK[g - 3][h]][:], ACT.Tanh, scale=0.5).then_inc(s["g_tanh"], 1)
                    if tail and g == 1:
                        take_oT(tail, 0)
                    if front and g == 5:
                        wait(act, s["terms_ps"], 4 * (front.n - 1))
                        act.wait_ge(s["qk_scaled"], front.n)
                        act.activation(terms[:, :, :, 0, :].rearrange("q j h d -> q (j h) d"), qk[:].rearrange("q j h d -> q (j h) d"), ACT.Copy).then_inc(s["high_made"], 1)
                    if tail and g == 5:
                        take_oT(tail, 1)
                    if front and g == 5:
                        gate_tanh(front, 0)
                    if att and g == 5:
                        take_aggregate(att, 0)
                    if front and g == 5:
                        gate_tanh(front, 1)
                    if att and g == 6:
                        tanh_of_norm(att, 0)
                    if front and g in (6, 7):
                        c = g - 6
                        act.wait_ge(s["terms_ps"], 4 * (front.n - 1) + 2 * c + 1)
                        act.activation(qT[front.p][:, 4 * c:4 * c + 4, :].rearrange("q a (j t) -> q a j t", j=2),
                                       ring[0].bitcast(F16).rearrange("q (a j t) -> q a j t", a=4, j=2), ACT.Copy).then_inc(s["qkT_act"], 1)
                    if fetch and g == 7:
                        act.wait_ge(s["x3T_ps"], fetch.n)
                        act.activation(x3T[:], ring[0][:, 0:SEQ], ACT.Copy).then_inc(s["x3T_made"], 1)

            pipeline(act, half)
            act.drain().then_inc(s["phases"], 1)
            act.wait_ge(s["phases"], 10)
            act.wait_ge(s["cleared"], 2)
            act.wait_ge(weights_in, 16 * N_WEIGHT_DMA)
            act.wait_ge(s["set4"], 8 + AHEAD)
            act.dma_start(token_dram.rearrange("(q n) a -> q (n a)", q=P), no_token[:]).then_inc(s["table_cleared"], 16)
            for dst, src in ((wa[:], a["wa"].rearrange("e q f -> q e f")), (wb[:], a["wb"].rearrange("e (c q) d -> q (e c) d", q=P)),
                             (ba[:], a["ba"]), (bb[:], a["bb"])):
                act.dma_start(dst, src).then_inc(s["experts_in"], 16)

            def exp(att, head):
                wait(act, s["pv_made"], HEADS * (att.n - 1) + head + 1 - 4)
                act.wait_ge(s["score4_ps"], HEADS * (att.n - 1) + head + 1)
                act.activation(prob[head % 4][:], bank[head % 3][:], ACT.Exp, scale=SCALE).then_inc(s["exp_made"], 1)

            def take_values(q, hf):
                act.wait_ge(s["pv_made"], HEADS * (q.n - 1) + HALF * hf + HALF)
                wait(act, s["pv_turned"], 2 * (q.n - 2) + hf + 1)
                act.activation(pvT[hf][:], bank[3], ACT.Copy).then_inc(s["pvT_out"], 1)

            def take_terms(front, what, c, x):
                dst = (kT4 if what == "k4" else qT4)[front.p]
                act.wait_ge(s[what + "_ps"], 2 * (front.n - 1) + c + 1)
                act.activation(dst[:, 4 * c:4 * c + 4, :].rearrange("q a t -> q (a t)"), ring[x].bitcast(BF16), ACT.Copy).then_inc(s[what + "_out"], 1)

            def half(fetch, front, att, tail, end):
                flat = terms4[:].rearrange("q w j h m d -> q (w j h) m d")
                qk_flat = qk4[:].rearrange("q w j (h d) -> q (w j h) d", d=DH)
                for g in range(PAIRS):
                    if att:
                        exp(att, 2 * g)
                        exp(att, 2 * g + 1)
                    if tail and g == 0:
                        take_values(tail, 1)
                    if att and g == 4:
                        take_values(att, 0)
                    if front and g == 1:
                        wait(act, s["q4_ps"], 2 * (front.n - 1))
                        act.wait_ge(s["qkv_out"], 2 * front.n)
                        act.activation(high4[:], qk4[:], ACT.Copy).then_inc(s["high4_made"], 1)
                    if front and g == 2:
                        act.wait_ge(s["high4_made"], front.n)
                        act.activation(flat[:, :, 0, :], high4[:].rearrange("q w j (h d) -> q (w j h) d", d=DH), ACT.Copy)
                    if tail and g == 2:
                        act.wait_ge(s["o4T_ps"], tail.n)
                        act.activation(o4T[:], ring[1][:, 0:SEQ], ACT.Copy).then_inc(s["o4T_made"], 1)
                    if front and g == 2:
                        act.wait_ge(s["rest4_made"], front.n)
                        act.activation(flat[:, :, 4, :], qk_flat, ACT.Copy).then_inc(s["mid4_made"], 1)
                    if front and g in (4, 5):
                        take_terms(front, "k4", g - 4, g - 4)
                    if front and g == 6:
                        take_terms(front, "q4", 0, 1)
                    if tail and g == 6:
                        act.wait_ge(s["x5T_ps"], tail.n)
                        act.activation(h5T[:], ring[0][:, 0:SEQ], ACT.Identity, bias=norms[:, 3:4], scale=norms[:, 2:3]).then_inc(s["h5T_made"], 1)
                    if front and g == 7:
                        take_terms(front, "q4", 1, 0)
                    if fetch and g == 7:
                        act.wait_ge(s["x4T_ps"], fetch.n)
                        act.activation(h4T[:], ring[1][:, 0:SEQ], ACT.Identity, bias=norms[:, 1:2], scale=norms[:, 0:1]).then_inc(s["h4T_made"], 1)

            pipeline(act, half, 5)
            act.wait_ge(s["experts_in"], 16 * 4)
            act.wait_ge(s["plan_made"], 1)

            def turned(pair, p):
                act.wait_ge(s["g5T_ps"], 2 * pair + p + 1)
                act.activation(g5T[p][:], bank[4 * p][:, 0:P], ACT.Identity, bias=norms[:, 3:4], scale=norms[:, 2:3]).then_inc(s["g5T_made"], 1)

            def turn(i, last=False):
                for h in range(AHEAD // 2):
                    pair = AHEAD // 2 * i + h
                    for p in range(2):
                        expert = act.value_load(block_expert_i[0:1, bass.ds(2 * pair + p, 1)], min_val=0, max_val=E1 - 1)
                        act.wait_ge(s["mid_ps"], 4 * pair + 2 * p + 1)
                        for c in range(2):
                            ins = act.activation(mid[p][:, c, :], bank[4 * p + 1][:, c * P:(c + 1) * P], ACT.Relu, bias=ba[:, bass.ds(expert * CHUNKS + c, 1)])
                        ins.then_inc(s["mid_act"], 1)
                    if not last or h < AHEAD // 2 - 1:
                        for p in range(2):
                            turned(pair + 1, p)

            for p in range(2):
                turned(0, p)
            with act.Fori(0, BLOCKS // AHEAD - 1) as i:
                turn(i)
            turn(BLOCKS // AHEAD - 1, last=True)

        @block.tensor
        def _(pe):
            constants_ready(pe)

            def turn(i):
                for p in range(2):
                    b = bank[4 * p:4 * p + 4]
                    wait(pe, s["slots_read"], 2 * i)
                    pe.wait_ge(s["xn_made"], 2 * i + p + 1)
                    for j in range(J1):
                        mm = pe.transpose(b[0][:, j * P:(j + 1) * P], xn[p][:, j, :], ident[:])
                    mm.then_inc(s["xnT_ps"], 1)
                for p in range(2):
                    b = bank[4 * p:4 * p + 4]
                    wait(pe, s["x1s_made"], 2 * i)
                    pe.wait_ge(s["xm_made"], 2 * i + p + 1)
                    pe.matmul(b[1][:], w_rkvo[:, 0, :], xm[p][:].rearrange("q a t -> q (a t)"), start=True, stop=True).then_inc(s["k_ps"], 1)
                for p in range(2):
                    for n, name in ((1, "v_ps"), (2, "r_ps")):
                        pe.matmul(bank[4 * p + 1 + n][:], w_rkvo[:, n, :], xm[p][:].rearrange("q a t -> q (a t)"), start=True, stop=True).then_inc(s[name], 1)
                for p in range(2):
                    pe.wait_ge(s["rw_made"], 2 * i + p + 1)
                    for j in range(J1):
                        mm = pe.matmul(bank[4 * p][:, j * P:(j + 1) * P], rw[p][:, j * P:(j + 1) * P], w_rkvo[:, 3, :], start=True, stop=True)
                    mm.then_inc(s["y_ps"], 1)
                for p in range(2):
                    pe.wait_ge(s["xn2_made"], 2 * i + p + 1)
                    for j in range(J1):
                        mm = pe.transpose(bank[4 * p + 1][:, j * P:(j + 1) * P], xn2[p][:, j, :], ident[:])
                    mm.then_inc(s["x2T_ps"], 1)
                for p in range(2):
                    b = bank[4 * p:4 * p + 4]
                    pe.wait_ge(s["x2T_made"], 2 * i + p + 1)
                    for j in range(J1):
                        mm = pe.matmul(b[0][:, j * E0:(j + 1) * E0], x2T[p][:, j * P:(j + 1) * P], gate0_w[:], start=True, stop=True)
                    mm.then_inc(s["logit_ps"], 1)
                    for n in range(2):
                        for h in range(2):
                            mm = pe.matmul(b[2][I0 * h:I0 * h + I0, 256 * n:256 * n + 256], sw13[:, n, :], x2T[p][:, 256 * h:256 * h + 256], start=True, stop=True)
                    mm.then_inc(s["ab_ps"], 1)
                for p in range(2):
                    b = bank[4 * p:4 * p + 4]
                    here = b[0][:, 256:256 + J1 * E0]
                    pe.wait_ge(s["tanh_l_made"], 2 * i + p + 1)
                    pe.wait_ge(s["prior_made"], 2 * i + p + 1)
                    pe.matmul(here, before[:], taken[p][:].rearrange("q j e -> q (j e)"), start=True, stop=False)
                    pe.matmul(here, ones[:], prior[:, J1 * p:J1 * p + J1, :].rearrange("q j e -> q (j e)"), start=False, stop=True).then_inc(s["pos_ps"], 1)
                for p in range(2):
                    b = bank[4 * p:4 * p + 4]
                    pe.wait_ge(s["hid_made"], 2 * i + p + 1)
                    for j in range(J1):
                        h = I0 * (j // 2)
                        mm = pe.matmul(b[3 - j // 2 * 2][:, j * P:(j + 1) * P], hid[p][h:h + I0, (j % 2) * P:(j % 2) * P + P], sw2[h:h + I0, :], start=True, stop=True)
                    mm.then_inc(s["ysh_ps"], 1)

            repeat(pe, T1, turn)

            def turn(i):
                for p in range(2):
                    pe.wait_ge(s["xe_landed"][p], 16 * (i + 1))
                    for e in range(2):
                        mm = pe.transpose(bank[4 * p][:, e * P:(e + 1) * P], xe[p][:, e, :], ident[:])
                    mm.then_inc(s["xeT_ps"], 1)
                for p in range(2):
                    pe.wait_ge(s["w_landed"][p], 32 * (i + 1))
                    pe.wait_ge(s["xeT_made"], 2 * i + p + 1)
                    for n in range(2):
                        for e in range(2):
                            mm = pe.matmul(bank[4 * p + 1][I0 * e:I0 * e + I0, n * P:(n + 1) * P], w13[p][:, n, e, :], xeT[p][:, e * P:(e + 1) * P], start=True, stop=True)
                    mm.then_inc(s["e_ab_ps"], 1)
                for p in range(2):
                    wait(pe, s["ye_made"], 2 * i)
                    pe.wait_ge(s["w2_landed"][p], 16 * (i + 1))
                    pe.wait_ge(s["e_hid_made"], 2 * i + p + 1)
                    for e in range(2):
                        mm = pe.matmul(bank[4 * p + 2 + e][:, 0:D], e_hid[p][I0 * e:I0 * e + I0, :], w2[p][I0 * e:I0 * e + I0, :], start=True, stop=True)
                    mm.then_inc(s["ye_ps"], 1)

            repeat(pe, T2, turn)

            pe.drain().then_inc(s["phases"], 1)
            pe.wait_ge(s["phases"], 5)
            pe.wait_ge(weights_in, 16 * N_WEIGHT_DMA)
            readers = [[], []]

            def fill(x, after, now):
                for semaphore, value in readers[x]:
                    pe.wait_ge(semaphore, value)
                for semaphore, value in now:
                    pe.wait_ge(semaphore, value)
                readers[x] = after
                return ring[x]

            def scores(att, g):
                wait(pe, s["relu_made"], PAIRS * (att.n - 1) + g - 1)
                if g == 0:
                    pe.wait_ge(s["qkT_act"], 2 * att.n)
                    pe.wait_ge(s["qkT_dve"], 2 * att.n)
                for c in range(2):
                    for h in range(2):
                        part = slice(64 * h, 64 * h + 64)
                        mm = pe.matmul(psum[:, 2 * (g % 2) + h, c * SEQ:(c + 1) * SEQ], kT[att.p][part, g, c * P:(c + 1) * P], qT[att.p][part, g, :], start=True, stop=True)
                mm.then_inc(s["score_ps"], 1)

            def aggregate(q, g):
                hf = g // 4
                if g % 4 == 0:
                    wait(pe, s["aggr_out"], 2 * (q.n - 1) + hf)
                if g == 0:
                    pe.wait_ge(s["v_made"], q.n)
                if g in POOL_PAIRS:
                    pe.wait_ge(s["attn_made_pool"], len(POOL_PAIRS) * (q.n - 1) + POOL_PAIRS.index(g) + 1)
                else:
                    pe.wait_ge(s["attn_made"], (PAIRS - len(POOL_PAIRS)) * (q.n - 1) + g - sum(x < g for x in POOL_PAIRS) + 1)
                for j in range(2):
                    for h in range(2):
                        head = 2 * g + h
                        for c in range(2):
                            mm = pe.matmul(psum[:, 4 + j, (head % HALF) * DV:(head % HALF + 1) * DV], attn[g % RING][:, h, c * SEQ + j * P:c * SEQ + (j + 1) * P],
                                           v[q.p][:, c, head * DV:(head + 1) * DV], start=(c == 0), stop=(c == 1))
                mm.then_inc(s["attn_read"], 1)

            def turn_oT(q, hf):
                for j in range(2):
                    x = OT_BANK[hf][j]
                    b = fill(x, [(s["oT_dve" if j else "oT_act"], 2 * (q.n - 1) + hf + 1)], [(s["o_made"], 2 * (q.n - 1) + hf + 1)])
                    for c in range(4):
                        mm = pe.transpose(b[:, c * P:(c + 1) * P], o[:, j, c * P:(c + 1) * P], ident[:])
                    mm.then_inc(s["oT_ps"], 1)

            def half(fetch, front, att, tail):
                if att:
                    readers[0] = [(s["qkT_act"], 2 * att.n)]
                    readers[1] = [(s["qkT_dve"], 2 * att.n)]
                elif tail:
                    readers[0] = readers[1] = []
                if front:
                    readers[0] = [(s["x3T_made"], front.n)]
                for g in range(PAIRS):
                    if att:
                        scores(att, g)
                    if front and g == 0:
                        for j in range(2):
                            m = 2 * (front.n - 1) + j + 1
                            b = fill(1 - j, [(s["qk_copied"], m)], [(s["x3T_made"], front.n)] if j == 0 else [])
                            pe.matmul(b[:], x3T[:, j * P:(j + 1) * P], w_qk[:], start=True, stop=True).then_inc(s["qk_ps"], 1)
                    if tail and g < 2:
                        aggregate(tail, 6 + g)
                    if att and g >= 2:
                        aggregate(att, g - 2)
                    if front and g in (1, 2):
                        for h in range(2):
                            m = 4 * (front.n - 1) + 2 * (g - 1) + h + 1
                            b = fill(1 - h, [(s["v_copied"], m)], [])
                            pe.matmul(b[:], x3T[:, (g - 1) * P:g * P], w_v[:, 512 * h:512 * h + 512], start=True, stop=True).then_inc(s["v_ps3"], 1)
                    if front and g in (3, 4):
                        for h in range(2):
                            m = 4 * (front.n - 1) + 2 * (g - 3) + h + 1
                            b = fill(G_BANK[g - 3][h], [(s["silu_made"], m)], [])
                            pe.matmul(b[:], x3T[:, (g - 3) * P:(g - 2) * P], w_g[:, 512 * h:512 * h + 512], start=True, stop=True).then_inc(s["g_ps"], 1)
                    if tail and g == 1:
                        turn_oT(tail, 0)
                    if tail and g == 5:
                        turn_oT(tail, 1)
                    if tail and g == 6:
                        b = fill(1, [(s["x3_made"], tail.n)], [(s["oT_act"], 2 * tail.n), (s["oT_dve"], 2 * tail.n)])
                        for j in range(2):
                            for c in range(PAIRS):
                                mm = pe.matmul(b[:, j * D:(j + 1) * D], oT[:, j, c, :], w_out[:, c, :], start=(c == 0), stop=(c == PAIRS - 1))
                        mm.then_inc(s["y3_ps"], 1)
                    if front and g in (6, 7):
                        for t in range(2):
                            m = 2 * (front.n - 1) + (g - 6) + 1
                            b = fill(t, [(s["qkT_dve" if t else "qkT_act"], m)], [(s["terms_made"], front.n)] if g == 6 and t == 0 else [])
                            b16 = b.bitcast(F16)
                            for a4 in range(4):
                                for j in range(2):
                                    head = HEADS * t + 2 * (4 * (g - 6) + a4)
                                    at = (2 * a4 + j) * P
                                    mm = pe.transpose(b16[:, at:at + P], terms[:, j, head:head + 2, :, :].rearrange("q h m d -> q (h m d)"), ident16[:])
                            mm.then_inc(s["terms_ps"], 1)
                    if fetch and g == 7:
                        b = fill(0, [], [(s["xn3_made"], fetch.n)])
                        for j in range(2):
                            mm = pe.transpose(b[:, j * P:(j + 1) * P], xn3[:, j, :], ident[:])
                        mm.then_inc(s["x3T_ps"], 1)

            pipeline(pe, half)
            pe.drain().then_inc(s["phases"], 1)
            pe.wait_ge(s["phases"], 10)
            pe.wait_ge(s["cleared"], 2)
            pe.wait_ge(s["set4"], 8 + AHEAD)
            readers = [[], []]
            MAXIMA_AT = (3, 4, 5, 6)
            LAST_USER = (15, 13, 14)

            def fill4(x, after, now):
                for semaphore, value in readers[x] + now:
                    pe.wait_ge(semaphore, value)
                readers[x] = after
                return ring[x]

            def scores4(att, head):
                before_it = head - 3 if head >= 3 else LAST_USER[head] - HEADS
                wait(pe, s["exp_made"], HEADS * (att.n - 1) + before_it + 1)
                if head % 8 == 0:
                    pe.wait_ge(s["k4_out"], 2 * (att.n - 1) + head // 8 + 1)
                    pe.wait_ge(s["q4_out"], 2 * (att.n - 1) + head // 8 + 1)
                part = slice(64 * (head % 2), 64 * (head % 2) + 64)
                for c in range(2):
                    mm = pe.matmul(bank[head % 3][:, c * SEQ:(c + 1) * SEQ], kT4[att.p][part, head // 2, c * P:(c + 1) * P], qT4[att.p][part, head // 2, :], start=True, stop=True)
                mm.then_inc(s["score4_ps"], 1)

            def values4(q, head):
                if head % HALF == 0:
                    wait(pe, s["pvT_out"], 2 * (q.n - 1) + head // HALF)
                pe.wait_ge(s["exp_made"], HEADS * (q.n - 1) + head + 1)
                part, t = slice(COLS * (head % 4), COLS * (head % 4) + COLS), head // 4 % 2
                for c in range(2):
                    mm = pe.matmul(bank[3][part, t * SEQ:(t + 1) * SEQ], v4[q.p][:, c, head, :], prob[head % 4][:, c * SEQ:(c + 1) * SEQ], start=(c == 0), stop=(c == 1))
                mm.then_inc(s["pv_made"], 1)

            def turn_values(q, hf, x):
                m = 2 * (q.n - 1) + hf + 1
                b = fill4(x, [(s["o4_made"], m)], [(s["pvT_out"], m)])
                for j in range(2):
                    for t in range(2):
                        mm = pe.transpose(b[:, (2 * j + t) * P:(2 * j + t + 1) * P], pvT[hf][:, t * SEQ + j * P:t * SEQ + (j + 1) * P], ident[:])
                mm.then_inc(s["pv_turned"], 1)

            def maxima(front, r):
                gp, jp, j, a2 = r // 8, r // 4 % 2, r // 2 % 2, r % 2
                wait(pe, s["max_made"], 16 * (front.n - 1) + r - 1)
                if r == 0:
                    pe.wait_ge(s["high_out"], front.n)
                part = slice(32 * (2 * gp + a2), 32 * (2 * gp + a2) + 32)
                for b2 in range(2):
                    mm = pe.matmul(bank[4 + a2][:, b2 * SEQ:(b2 + 1) * SEQ], q_highT[part, 2 * jp + b2, j * P:(j + 1) * P], k_highT[part, :], start=True, stop=True)
                mm.then_inc(s["max_ps"], 1)

            def turn_terms(front, what, c, x, after):
                b16 = fill4(x, [(s[what + "_out"], 2 * (front.n - 1) + c + 1)], after).bitcast(BF16)
                for a4 in range(4):
                    for j in range(2):
                        head = 2 * (4 * c + a4)
                        at = (2 * a4 + j) * P
                        mm = pe.transpose(b16[:, at:at + P], terms4[:, 1 if what == "k4" else 0, j, head:head + 2, :, :].rearrange("q h m d -> q (h m d)"), ident_b[:])
                mm.then_inc(s[what + "_ps"], 1)

            def half(fetch, front, att, tail, end):
                if att:
                    readers[0] = [(s["q4_out"], 2 * att.n)]
                    readers[1] = [(s["q4_out"], 2 * att.n - 1)]
                elif end:
                    readers[0] = [(s["h5T_made"], end.n)]
                if front:
                    readers[1] = [(s["h4T_made"], front.n)]
                for g in range(PAIRS):
                    if att:
                        scores4(att, 2 * g)
                    if front and g in MAXIMA_AT:
                        maxima(front, 4 * (g - 3))
                    if att:
                        scores4(att, 2 * g + 1)
                    if front and g in MAXIMA_AT:
                        maxima(front, 4 * (g - 3) + 1)
                    if front and g == 2:
                        b16 = fill4(0, [(s["high_out"], front.n)], [(s["high4_made"], front.n)]).bitcast(BF16)
                        for w in range(2):
                            for j in range(2):
                                mm = pe.transpose(b16[:, (2 * w + j) * P:(2 * w + j + 1) * P], high4[:, w, j, :], ident_b[:])
                        mm.then_inc(s["high_ps"], 1)
                    if front and g == 7:
                        turn_terms(front, "q4", 1, 0, [(s["max_made"], 16 * front.n)])
                    if front and g == 0:
                        for j in range(2):
                            b = fill4(1 - j, [(s["qkv_out"], 2 * (front.n - 1) + j + 1)], [(s["h4T_made"], front.n)] if j == 0 else [])
                            pe.matmul(b[:, 0:3 * D], h4T[:, j * P:(j + 1) * P], w_qkv[:], start=True, stop=True).then_inc(s["qkv_ps"], 1)
                    if tail and g == 0:
                        values4(tail, HEADS - 2)
                        values4(tail, HEADS - 1)
                    if end and g == 1:
                        b = fill4(1, [(s["logit1_out"], end.n)], [(s["h5T_made"], end.n)])
                        for j in range(2):
                            mm = pe.matmul(b[:, j * E1:(j + 1) * E1], h5T[:, j * P:(j + 1) * P], gate1_w[:], start=True, stop=True)
                        mm.then_inc(s["logit1_ps"], 1)
                    if att and g >= 1:
                        values4(att, 2 * g - 2)
                        values4(att, 2 * g - 1)
                    if front and g in MAXIMA_AT:
                        maxima(front, 4 * (g - 3) + 2)
                    if tail and g == 1:
                        turn_values(tail, 1, 1)
                    if tail and g == 2:
                        b = fill4(1, [(s["o4T_made"], tail.n)], [(s["o4_made"], 2 * tail.n)])
                        for j in range(2):
                            mm = pe.transpose(b[:, j * P:(j + 1) * P], o4[:, j, :], ident[:])
                        mm.then_inc(s["o4T_ps"], 1)
                    if end and g == 3:
                        b = fill4(0, [(s["pos1_out"], end.n)], [(s["onehot1_made"], end.n), (s["prior1_made"], end.n)])
                        pe.matmul(b[:, 0:2 * E1], before[:], onehot_b[:].rearrange("q j e -> q (j e)"), start=True, stop=False)
                        pe.matmul(b[:, 0:2 * E1], ones[:], prior_b[:, 0:2, :].rearrange("q j e -> q (j e)"), start=False, stop=True).then_inc(s["pos1_ps"], 1)
                    if tail and g == 3:
                        b = fill4(1, [(s["x4_made"], tail.n)], [(s["o4T_made"], tail.n)])
                        for j in range(2):
                            mm = pe.matmul(b[:, j * D:(j + 1) * D], o4T[:, j * P:(j + 1) * P], w_o[:], start=True, stop=True)
                        mm.then_inc(s["y4_ps"], 1)
                    if front and g in (4, 5):
                        turn_terms(front, "k4", g - 4, g - 4, [(s["terms4_made"], front.n)] if g == 4 else [])
                    if att and g == 5:
                        turn_values(att, 0, 0)
                    if front and g == 6:
                        turn_terms(front, "q4", 0, 1, [(s["max_made"], 16 * (front.n - 1) + 8)])
                    if front and g in MAXIMA_AT:
                        maxima(front, 4 * (g - 3) + 3)
                    if tail and g == 6:
                        b = fill4(0, [(s["h5T_made"], tail.n)], [(s["x4n_made"], tail.n)])
                        for j in range(2):
                            mm = pe.transpose(b[:, j * P:(j + 1) * P], x4n[tail.p][:, j, D:2 * D], ident[:])
                        mm.then_inc(s["x5T_ps"], 1)
                    if fetch and g == 7:
                        b = fill4(1, [], [(s["xn4_made"], fetch.n)])
                        for j in range(2):
                            mm = pe.transpose(b[:, j * P:(j + 1) * P], xn4[:, j, :], ident[:])
                        mm.then_inc(s["x4T_ps"], 1)

            pipeline(pe, half, 5)
            pe.wait_ge(s["all_counted"], 1)
            pe.matmul(bank[7][:, 0:E1], ones[:], prior_b[:, 0, :], start=True, stop=True).then_inc(s["count_ps"], 1)
            pe.wait_ge(s["tokens_out"], 1)
            pe.transpose(bank[7][:, 0:P], block_tokens_f[:], ident[:]).then_inc(s["tokens_ps"], 1)
            pe.wait_ge(s["rows_made"], 1)
            pe.wait_ge(s["experts_in"], 16 * 4)

            def turn_rows(turn, q):
                pe.wait_ge(s["got_landed"][q], 16 * (turn + 1))
                pe.transpose(bank[4 * (q % 2)][:, 0:P], got[q][:, D:2 * D], ident[:]).then_inc(s["g5T_ps"], 1)

            def turn(i, last=False):
                for h in range(AHEAD // 2):
                    pair = AHEAD // 2 * i + h
                    expert = [pe.value_load(block_expert_i[0:1, bass.ds(2 * pair + p, 1)], min_val=0, max_val=E1 - 1) for p in range(2)]
                    for p in range(2):
                        pe.wait_ge(s["wa_made"], 2 * pair + p + 1)
                        pe.wait_ge(s["g5T_made"], 2 * pair + p + 1)
                        for c in range(CHUNKS):
                            mm = pe.matmul(bank[4 * p + 1 + c // 2][:, (c % 2) * P:(c % 2 + 1) * P],
                                           wa_now[p][:, c * P:(c + 1) * P], g5T[p][:], start=True, stop=True)
                            if c % 2 == 1:
                                mm.then_inc(s["mid_ps"], 1)
                    if not last or h < AHEAD // 2 - 1:
                        for p in range(2):
                            q = (2 * h + 2 + p) % AHEAD
                            turn_rows(i + (1 if h == AHEAD // 2 - 1 else 0), q)
                    for p in range(2):
                        pe.wait_ge(s["mid_act"], 2 * pair + p + 1)
                        pe.wait_ge(s["mid_dve"], 2 * pair + p + 1)
                        wait(pe, s["res_made"], 2 * pair)
                        for c in range(CHUNKS):
                            pe.matmul(bank[4 * p + 3][:, 0:D], mid[p][:, c, :], wb[:, bass.ds(expert[p] * CHUNKS + c, 1), :].rearrange("q c d -> q (c d)"), start=(c == 0), stop=False)
                        pe.matmul(bank[4 * p + 3][:, 0:D], ones_row[:], bb[:, bass.ds(expert[p] * D, D)], start=False, stop=True).then_inc(s["res_ps"], 1)

            for q in range(2):
                turn_rows(0, q)
            turn(0)
            with pe.Fori(1, BLOCKS // AHEAD - 1) as i:
                turn(i)
            turn(BLOCKS // AHEAD - 1, last=True)

        @block.vector
        def _(dve):
            chain = Chain(dve, dve_chain)
            dve.wait_ge(consts_in, 16 * N_CONST_DMA)
            dve.wait_ge(made, N_MADE)
            dve.wait_ge(decay_ready, 3)
            n = chain.step(dve.tensor_scalar(one_less_mix[:], mix[:], -1.0, 1.0, ALU.mult, ALU.add))
            chain.need(n)
            chain.restart()

            def statistics(x, p, signal):
                for j in range(J1):
                    n = chain.step(dve.bn_stats(stats[p][:, j, :], x[:, j, :]))
                chain.need(n)
                for j in range(J1):
                    ins = dve.bn_aggr(meanvar[p][:, j, :], stats[p][:, j, :])
                    if j < J1 - 1:
                        chain.step(ins)
                ins.then_inc(signal, 1)

            def normalise(x, y, p, signal):
                for j in range(J1):
                    ins = dve.tensor_scalar(y[:, j, :], x[:, j, :], meanvar[p][:, j, 0:1], rstd[p][:, j:j + 1], ALU.subtract, ALU.mult)
                    if j < J1 - 1:
                        chain.step(ins)
                ins.then_inc(signal, 1)

            def turn(i):
                for p in range(2):
                    dve.wait_ge(s["x_landed"][p], 16 * (i + 1))
                    statistics(x_in[p], p, s["var1"])
                for p in range(2):
                    dve.wait_ge(s["var1"], 2 * i + p + 1)
                    dve.wait_ge(s["rstd1"], 2 * i + p + 1)
                    normalise(x_in[p], xn[p], p, s["xn_made"])
                for p in range(2):
                    dve.wait_ge(s["xT_made"], 2 * i + p + 1)
                    n = chain.step(dve.tensor_scalar(shifted[p][:], xT[p][:, :, 0:SEQ], one_less_mix[:], None, ALU.mult))
                    chain.need(n)
                    dve.scalar_tensor_tensor(xm[p][:], xT[p][:, :, 1:], mix[:], shifted[p][:], ALU.mult, ALU.add).then_inc(s["xm_made"], 1)
                for p in range(2):
                    dve.wait_ge(s["k_ps"], 2 * i + p + 1)
                    dve.tensor_scalar(ek[p][:], bank[4 * p + 1][:].rearrange("q (a t) -> q a t", a=2), 60.0, None, ALU.min).then_inc(s["kmin"], 1)
                for p in range(2):
                    dve.wait_ge(s["v_ps"], 2 * i + p + 1)
                    dve.wait_ge(s["ek_made"], 2 * i + p + 1)
                    n = chain.step(dve.tensor_tensor(kv[p][:], ek[p][:], bank[4 * p + 2][:].rearrange("q (a t) -> q a t", a=2), ALU.mult))
                    for a2 in range(2):
                        chain.step(dve.tensor_tensor_scan(sum_k[p][:, a2, 1:], decay[:].to_broadcast([P, SEQ]), ek[p][:, a2, :], 0.0, ALU.mult, ALU.add))
                    chain.need(n)
                    for a2 in range(2):
                        n = chain.step(dve.tensor_tensor_scan(sum_kv[p][:, a2, 1:], decay[:].to_broadcast([P, SEQ]), kv[p][:, a2, :], 0.0, ALU.mult, ALU.add))
                    chain.need(n)
                    n1 = chain.step(dve.scalar_tensor_tensor(den[p][:], ek[p][:], first_w[:], sum_k[p][:, :, 0:SEQ], ALU.mult, ALU.add))
                    n2 = chain.step(dve.scalar_tensor_tensor(num[p][:], kv[p][:], first_w[:], sum_kv[p][:, :, 0:SEQ], ALU.mult, ALU.add))
                    chain.need(n1)
                    n = chain.step(dve.tensor_scalar(den[p][:], den[p][:], 1e-16, None, ALU.add))
                    chain.need(n)
                    n = chain.step(dve.reciprocal(rden[p][:], den[p][:]))
                    chain.need(n)
                    n = chain.step(dve.scalar_tensor_tensor(num[p][:], num[p][:], 0.5, rden[p][:], ALU.mult, ALU.mult))
                    chain.need(n)
                    dve.wait_ge(s["tanh_r_made"], 2 * i + p + 1)
                    dve.scalar_tensor_tensor(rw[p][:], tanh_r[p][:], 1.0, num[p][:].rearrange("q a t -> q (a t)"), ALU.add, ALU.mult).then_inc(s["rw_made"], 1)
                for p in range(2):
                    dve.wait_ge(s["y_ps"], 2 * i + p + 1)
                    dve.tensor_tensor(x1[p][:], x_in[p][:], bank[4 * p][:].rearrange("q (j d) -> q j d", j=J1), ALU.add).then_inc(s["x1_made"], 1)
                    dve.wait_ge(s["x1_made"], 2 * i + p + 1)
                    statistics(x1[p], p, s["var2"])
                for p in range(2):
                    wait(dve, s["rows_out_made"], 2 * i + p - 1)
                    dve.wait_ge(s["var2"], 2 * i + p + 1)
                    dve.wait_ge(s["rstd2"], 2 * i + p + 1)
                    normalise(x1[p], xn2[p], p, s["xn2_made"])
                for p in range(2):
                    dve.wait_ge(s["tanh_l_made"], 2 * i + p + 1)
                    n = chain.step(dve.tensor_scalar(score[p][:], tanh_l[p][:], 0.5, 0.5, ALU.mult, ALU.add))
                    chain.need(n)
                    n = chain.step(dve.tensor_tensor(biased[p][:], score[p][:], bias0[:].unsqueeze(1).to_broadcast([P, J1, E0]), ALU.add))
                    chain.need(n)
                    for j in range(J1):
                        n = chain.step(dve.max(top[p][:, j, :], biased[p][:, j, :]))
                    chain.need(n)
                    for j in range(J1):
                        n = chain.step(dve.max_index(top_at[p][:, j, :], top[p][:, j, :], biased[p][:, j, :]))
                    chain.need(n)
                    n = chain.step(dve.tensor_copy(chosen[p][:].rearrange("q (j k) -> q j k", j=J1), top_at[p][:, :, 0:K0]))
                    chain.need(n)
                    n = chain.step(dve.tensor_tensor(
                        onehot[p][:].rearrange("q j k e -> q (j k) e"), expert_id[:].unsqueeze(1).to_broadcast([P, J1 * K0, E0]),
                        chosen[p][:].unsqueeze(2).to_broadcast([P, J1 * K0, E0]), ALU.is_equal))
                    chain.need(n)
                    with nc.allow_low_precision(reason="ones and zeros, exact in bfloat16"):
                        dve.tensor_reduce(taken[p][:], onehot[p][:].rearrange("q j k e -> q j e k"), AX, ALU.add).then_inc(s["taken_made"], 1)
                    dve.wait_ge(s["taken_made"], 2 * i + p + 1)
                    if p == 0:
                        wait(dve, s["pos_ps"], 2 * i)
                    for j in range(J1):
                        ins = dve.tensor_tensor(prior[:, J1 * p + j + 1, :], prior[:, J1 * p + j, :], taken[p][:, j, :], ALU.add)
                        if j < J1 - 1:
                            n = chain.step(ins)
                            chain.need(n)
                    ins.then_inc(s["prior_made"], 1)
                    dve.wait_ge(s["prior_made"], 2 * i + p + 1)
                    n = chain.step(dve.tensor_tensor(picked[p][:], onehot[p][:], score[p][:].unsqueeze(2).to_broadcast([P, J1, K0, E0]), ALU.mult))
                    chain.need(n)
                    n = chain.step(dve.tensor_reduce(weight[p][:], picked[p][:], AX, ALU.add))
                    chain.need(n)
                    n = chain.step(dve.tensor_reduce(wsum[p][:], weight[p][:], AX, ALU.add))
                    chain.need(n)
                    n = chain.step(dve.tensor_scalar(wsum[p][:], wsum[p][:], 1e-12, None, ALU.max))
                    chain.need(n)
                    n = chain.step(dve.reciprocal(wsum[p][:], wsum[p][:]))
                    chain.need(n)
                    n = chain.step(dve.tensor_tensor(weight[p][:], weight[p][:], wsum[p][:].unsqueeze(2).to_broadcast([P, J1, K0]), ALU.mult))
                    chain.need(n)
                    dve.wait_ge(s["pos_ps"], 2 * i + p + 1)
                    n = chain.step(dve.tensor_tensor(
                        picked[p][:], onehot[p][:],
                        bank[4 * p][:, 256:256 + J1 * E0].rearrange("q (j e) -> q j e", j=J1).unsqueeze(2).to_broadcast([P, J1, K0, E0]), ALU.mult))
                    chain.need(n)
                    dve.tensor_reduce(pos[p][:].rearrange("q (j k) -> q j k", j=J1), picked[p][:], AX, ALU.add).then_inc(s["slots_read"], 1)
                    dve.wait_ge(s["slots_read"], 2 * i + p + 1)
                    n = chain.step(dve.tensor_scalar(fits[p][:], pos[p][:], float(CAP), None, ALU.is_lt))
                    n = chain.step(dve.scalar_tensor_tensor(slot[p][:], chosen[p][:], float(CAP), pos[p][:], ALU.mult, ALU.add))
                    chain.need(n)
                    wait(dve, s["scattered"][p], 16 * J1 * K0 * i)
                    wait(dve, s["route_stored"][p], 16 * i)
                    chain.step(dve.tensor_tensor(route[p][:, :, 0:K0], weight[p][:], fits[p][:].rearrange("q (j k) -> q j k", j=J1), ALU.mult))
                    n = chain.step(dve.scalar_tensor_tensor(slot[p][:], slot[p][:], -float(SLOTS0), fits[p][:], ALU.add, ALU.mult))
                    chain.need(n)
                    dve.tensor_scalar(route[p][:].bitcast(U32)[:, :, K0:2 * K0], slot[p][:].rearrange("q (j k) -> q j k", j=J1), float(SLOTS0), None, ALU.add).then_inc(s["route_made"], 1)
                for p in range(2):
                    dve.wait_ge(s["ab_ps"], 2 * i + p + 1)
                    dve.wait_ge(s["tanh_a_made"], 2 * i + p + 1)
                    n = chain.step(dve.scalar_tensor_tensor(half_h[p][:], tanh_a[p][:], 1.0, bank[4 * p + 2][:, 0:256], ALU.add, ALU.mult))
                    chain.need(n)
                    dve.scalar_tensor_tensor(hid[p][:], half_h[p][:], 0.5, bank[4 * p + 2][:, 256:512], ALU.mult, ALU.mult).then_inc(s["hid_made"], 1)
                for p in range(2):
                    dve.wait_ge(s["ysh_ps"], 2 * i + p + 1)
                    wait(dve, s["x1_stored"][p], 16 * i)
                    for h, b in ((0, bank[4 * p + 3]), (1, bank[4 * p + 1])):
                        half = slice(2 * h, 2 * h + 2)
                        ins = dve.tensor_tensor(x1s[p][:, half, :], x1[p][:, half, :], b[:, 256 * h:256 * h + 256].rearrange("q (j d) -> q j d", j=2), ALU.add)
                        if h == 0:
                            chain.step(ins)
                    ins.then_inc(s["x1s_made"], 1)
                for p in range(2):
                    dve.wait_ge(s["pos_ps"], 2 * i + p + 1)
                chain.step(dve.tensor_copy(prior[:, 0, :], prior[:, 2 * J1, :]))
                chain.restart()

            repeat(dve, T1, turn)

            def turn(i):
                for p in range(2):
                    b = bank[4 * p + 1]
                    dve.wait_ge(s["e_ab_ps"], 2 * i + p + 1)
                    dve.wait_ge(s["e_tanh_made"], 2 * i + p + 1)
                    n = chain.step(dve.scalar_tensor_tensor(e_half[p][:], e_tanh[p][:], 1.0, b[:, 0:P], ALU.add, ALU.mult))
                    chain.need(n)
                    dve.scalar_tensor_tensor(e_hid[p][:], e_half[p][:], 0.5, b[:, P:2 * P], ALU.mult, ALU.mult).then_inc(s["e_hid_made"], 1)
                chain.restart()

            repeat(dve, T2, turn)
            dve.drain().then_inc(s["phases"], 1)
            dve.wait_ge(s["phases"], 5)

            def inverse_root(dst, squared, columns, signal=None):
                y, t = dst, newton[:, 0:columns]
                n = chain.step(dve.tensor_scalar(squared, squared, 1e-24, None, ALU.max))
                chain.need(n)
                n = chain.step(dve.tensor_scalar(guess[:, 0:columns].bitcast(U32), squared.bitcast(U32), 1, None, ALU.logical_shift_right))
                chain.need(n)
                n = chain.step(dve.tensor_scalar(y.bitcast(U32), guess[:, 0:columns].bitcast(U32), -1.0, float(0x5F3759DF), ALU.mult, ALU.add))
                chain.need(n)
                for turn in range(3):
                    n = chain.step(dve.tensor_tensor(t, y, y, ALU.mult))
                    chain.need(n)
                    n = chain.step(dve.scalar_tensor_tensor(t, t, -0.5, squared, ALU.mult, ALU.mult))
                    chain.need(n)
                    ins = dve.scalar_tensor_tensor(y, t, 1.5, y, ALU.add, ALU.mult)
                    if turn == 2 and signal:
                        ins.then_inc(signal, 1)
                    else:
                        n = chain.step(ins)
                        chain.need(n)

            def square(q, g):
                dve.wait_ge(s["relu_made"], PAIRS * (q.n - 1) + g + 1)
                r = attn[g % RING]
                dve.tensor_tensor(r[:], r[:], r[:], ALU.mult).then_inc(s["attn_made"], 1)

            def norm_of(q, hf):
                wait(dve, s["o_len_made"], 2 * (q.n - 1) + hf)
                dve.wait_ge(s["aggr_sq_made"], 2 * (q.n - 1) + hf + 1)
                dve.tensor_reduce(o_norm[:], aggr_sq[:].rearrange("q j (h d) -> q (j h) d", d=DV), AX, ALU.add).then_inc(s["o_norm_made"], 1)

            def gated_output(q, hf):
                wait(dve, s["oT_ps"], 4 * (q.n - 1) + 2 * hf)
                dve.wait_ge(s["gated"], 4 * (q.n - 1) + 2 * hf + 2)
                dve.tensor_tensor(o[:], aggr[:], gate[q.p][:, :, 512 * hf:512 * hf + 512], ALU.mult).then_inc(s["o_made"], 1)

            def take_oT(q, hf):
                dve.wait_ge(s["oT_ps"], 4 * (q.n - 1) + 2 * hf + 2)
                dve.tensor_copy(oT[:, 1, 4 * hf:4 * hf + 4, :], ring[OT_BANK[hf][1]][:].rearrange("q (c t) -> q c t", c=4)).then_inc(s["oT_dve"], 1)

            def combine(front):
                dve.wait_ge(s["x1l_landed"][front.p], 16 * front.k)
                dve.wait_ge(s["yg_landed"][front.p], 16 * 2 * K0 * front.k)
                for k in range(K0):
                    for j in range(2):
                        acc = x1l[front.p] if k == 0 else x2[front.p]
                        ins = dve.scalar_tensor_tensor(x2[front.p][:, j, :], yg[front.p][:, j, k, :], routel[front.p][:, j, k:k + 1], acc[:, j, :], ALU.mult, ALU.add)
                        if k < K0 - 1 or j == 0:
                            n = chain.step(ins)
                    if k < K0 - 1:
                        chain.need(n)
                ins.then_inc(s["x2_made"], 1)
                dve.wait_ge(s["x2_made"], front.n)
                for j in range(2):
                    n = chain.step(dve.bn_stats(stats3[:, j, :], x2[front.p][:, j, :]))
                chain.need(n)
                chain.step(dve.bn_aggr(meanvar3[:, 0, :], stats3[:, 0, :]))
                dve.bn_aggr(meanvar3[:, 1, :], stats3[:, 1, :]).then_inc(s["var3"], 1)

            def normalise3(front):
                dve.wait_ge(s["var3"], front.n)
                dve.wait_ge(s["rstd3"], front.n)
                chain.step(dve.tensor_scalar(xn3[:, 0, :], x2[front.p][:, 0, :], meanvar3[:, 0, 0:1], rstd3[:, 0:1], ALU.subtract, ALU.mult))
                dve.tensor_scalar(xn3[:, 1, :], x2[front.p][:, 1, :], meanvar3[:, 1, 0:1], rstd3[:, 1:2], ALU.subtract, ALU.mult).then_inc(s["xn3_made"], 1)

            def qk_sum(front, j):
                dve.wait_ge(s["qk_squared"], 2 * (front.n - 1) + j + 1)
                dve.tensor_reduce(qk_norm[:, j, :], squares[j][:].rearrange("q (h d) -> q h d", d=DK), AX, ALU.add).then_inc(s["sq_reduced"], 1)

            def v_sum(front, k):
                dve.wait_ge(s["v_squared"], 4 * (front.n - 1) + k + 1)
                dve.tensor_reduce(v_norm[:, k // 2, HALF * (k % 2):HALF * (k % 2) + HALF], squares[k % 2][:].rearrange("q (h d) -> q h d", d=DV), AX, ALU.add).then_inc(s["sq_reduced"], 1)

            def split_terms(front):
                dve.wait_ge(s["high_made"], front.n)
                t3 = lambda x: terms[:, :, :, x, :].rearrange("q j h d -> q (j h) d")
                n = chain.step(dve.tensor_tensor(t3(1), qk[:].rearrange("q j h d -> q (j h) d"), t3(0), ALU.subtract))
                chain.need(n)
                chain.step(dve.tensor_copy(terms[:, :, HEADS:, 2:4, :].rearrange("q j h m d -> q j h (m d)"), terms[:, :, HEADS:, 0:2, :].rearrange("q j h m d -> q j h (m d)")))
                chain.step(dve.tensor_copy(terms[:, :, 0:HEADS, 2, :], terms[:, :, 0:HEADS, 1, :]))
                n = chain.step(dve.tensor_copy(terms[:, :, 0:HEADS, 3, :], terms[:, :, 0:HEADS, 0, :]))
                chain.need(n)
                dve.sem_inc(s["terms_made"], 1)

            def half(fetch, front, att, tail):
                for g in range(PAIRS):
                    if g == 0 and tail:
                        square(tail, PAIRS - 1)
                    if g > 0 and att and g - 1 not in POOL_PAIRS:
                        square(att, g - 1)
                    if front and g == 0:
                        for j in range(2):
                            m = 2 * (front.n - 1) + j + 1
                            dve.wait_ge(s["qk_ps"], m)
                            dve.tensor_copy(qk[:, j, :, :], ring[1 - j][:].rearrange("q (h d) -> q h d", d=DK)).then_inc(s["qk_copied"], 1)
                    if front and g in (1, 2):
                        for h in range(2):
                            k = 2 * (g - 1) + h
                            if k == 0:
                                wait(dve, s["attn_read"], PAIRS * (front.n - 2))
                            if k < 2:
                                qk_sum(front, k)
                            else:
                                v_sum(front, k - 2)
                            dve.wait_ge(s["v_ps3"], 4 * (front.n - 1) + k + 1)
                            dve.tensor_copy(v[front.p][:, g - 1, 512 * h:512 * h + 512], ring[1 - h][:]).then_inc(s["v_copied"], 1)
                    if att and g == 1:
                        wait(dve, s["x3_made"], att.n - 2)
                        chain.step(dve.tensor_copy(x2_kept[att.p][:], x2[att.p][:]))
                    if tail and g == 1:
                        norm_of(tail, 1)
                    if tail and g == 1:
                        take_oT(tail, 0)
                    if front and g == 3:
                        v_sum(front, 2)
                        v_sum(front, 3)
                    if tail and g == 4:
                        gated_output(tail, 1)
                    if front and g in (3, 4):
                        for h in range(2):
                            m = 4 * (front.n - 1) + 2 * (g - 3) + h + 1
                            wait(dve, s["gate_made"], 2 * (front.n - 2) + g - 2)
                            dve.wait_ge(s["g_tanh"], m)
                            dve.scalar_tensor_tensor(silu_g[g - 3][:, 512 * h:512 * h + 512], tanh_g[h][:], 1.0, ring[G_BANK[g - 3][h]][:], ALU.add, ALU.mult).then_inc(s["silu_made"], 1)
                    if front and g == 3:
                        dve.wait_ge(s["sq_reduced"], 6 * front.n)
                        inverse_root(inv3[:], norm3[:], 6 * HEADS, s["inv_made"])
                        qk3 = qk[:].rearrange("q j h d -> q (j h) d")
                        dve.wait_ge(s["inv_made"], front.n)
                        dve.tensor_tensor(qk3, qk3, inv3[:, 0:4 * HEADS].unsqueeze(2).to_broadcast([P, 4 * HEADS, DK]), ALU.mult).then_inc(s["qk_scaled"], 1)
                    if front and g == 5:
                        split_terms(front)
                    if tail and g == 5:
                        take_oT(tail, 1)
                    if att and g == 5:
                        norm_of(att, 0)
                    if fetch and g == 5:
                        combine(fetch)
                    if tail and g == 6:
                        wait(dve, s["x3_stored"][tail.p], 16 * (tail.k - 1))
                        dve.wait_ge(s["y3_ps"], tail.n)
                        dve.tensor_tensor(x3[tail.p][:], x2_kept[tail.p][:], ring[1][:, 0:2 * D].rearrange("q (j d) -> q j d", j=2), ALU.add).then_inc(s["x3_made"], 1)
                    if front and g in (6, 7):
                        c = g - 6
                        dve.wait_ge(s["terms_ps"], 4 * (front.n - 1) + 2 * c + 2)
                        dve.tensor_copy(kT[front.p][:, 4 * c:4 * c + 4, :].rearrange("q a t -> q (a t)"), ring[1].bitcast(F16)).then_inc(s["qkT_dve"], 1)
                    if fetch and g == 6:
                        normalise3(fetch)
                    if att and g == 7:
                        gated_output(att, 0)
                chain.restart()

            pipeline(dve, half)
            dve.drain().then_inc(s["phases"], 1)
            dve.wait_ge(s["phases"], 10)
            dve.wait_ge(s["cleared"], 2)
            dve.wait_ge(weights_in, 16 * N_WEIGHT_DMA)
            dve.wait_ge(s["set4"], 8 + AHEAD)
            n = chain.step(dve.tensor_copy(token_f[:], token_start[:]))
            chain.need(n)
            chain.restart()

            def moments(x, stats_x, meanvar_x, done):
                for j in range(2):
                    n = chain.step(dve.bn_stats(stats_x[:, j, :], x[:, j, 0:D]))
                chain.need(n)
                chain.step(dve.bn_aggr(meanvar_x[:, 0, :], stats_x[:, 0, :]))
                dve.bn_aggr(meanvar_x[:, 1, :], stats_x[:, 1, :]).then_inc(s[done], 1)

            def normed(y, x, meanvar_x, rstd_x, done):
                chain.step(dve.tensor_scalar(y[:, 0, :], x[:, 0, 0:D], meanvar_x[:, 0, 0:1], rstd_x[:, 0:1], ALU.subtract, ALU.mult))
                dve.tensor_scalar(y[:, 1, :], x[:, 1, 0:D], meanvar_x[:, 1, 0:1], rstd_x[:, 1:2], ALU.subtract, ALU.mult).then_inc(s[done], 1)

            def divide_by_sums(q, hf, x):
                m = 2 * (q.n - 1) + hf + 1
                dve.wait_ge(s["pv_turned"], m)
                sums = ring[x].rearrange("q (j h d) -> q j h d", j=2, d=COLS)
                wait(dve, s["o4T_ps"], q.n - 1)
                n = chain.step(dve.reciprocal(rsum[:], sums[:, :, :, DH]))
                chain.need(n)
                dve.tensor_tensor(o4[:, :, D // 2 * hf:D // 2 * (hf + 1)].rearrange("q j (h d) -> q j h d", d=DH), sums[:, :, :, 0:DH],
                                  rsum[:].unsqueeze(3).to_broadcast([P, 2, HALF, DH]), ALU.mult).then_inc(s["o4_made"], 1)

            def take_maxima(front, r):
                gp, jp, j, a2 = r // 8, r // 4 % 2, r // 2 % 2, r % 2
                dve.wait_ge(s["max_ps"], 16 * (front.n - 1) + r + 1)
                head = HALF * gp + 4 * a2 + 2 * jp
                with nc.allow_low_precision(reason="any value near the maximum serves: the sum divides it out"):
                    dve.tensor_reduce(terms4[:, 0, j, head:head + 2, 6, 0], bank[4 + a2].rearrange("q (b k) -> q b k", b=2), AX, ALU.max, negate=True).then_inc(s["max_made"], 1)

            def half(fetch, front, att, tail, end):
                for g in range(PAIRS):
                    if front and g == 0:
                        wait(dve, s["pv_made"], HEADS * (front.n - 2))
                        for j in range(2):
                            b = ring[1 - j]
                            dve.wait_ge(s["qkv_ps"], 2 * (front.n - 1) + j + 1)
                            chain.step(dve.tensor_tensor(v4[front.p][:, j, :, 0:DH], b[:, 2 * D:3 * D].rearrange("q (h d) -> q h d", d=DH),
                                                         b_qkv[:, 2 * D:3 * D].rearrange("q (h d) -> q h d", d=DH), ALU.add))
                            dve.tensor_tensor(qk4[:, :, j, :], b[:, 0:2 * D].rearrange("q (w d) -> q w d", w=2), b_qkv[:, 0:2 * D].rearrange("q (w d) -> q w d", w=2), ALU.add).then_inc(s["qkv_out"], 1)
                    if end and g == 1:
                        dve.wait_ge(s["logit1_ps"], end.n)
                        dve.tensor_tensor(logit[:], ring[1][:, 0:2 * E1].rearrange("q (j e) -> q j e", j=2), gate1_b[:].unsqueeze(1).to_broadcast([P, 2, E1]), ALU.add).then_inc(s["logit1_sum"], 1)
                        dve.wait_ge(s["logit1_sum"], end.n)
                        dve.sem_inc(s["logit1_out"], 1)
                    if front and g == 1:
                        dve.wait_ge(s["high4_made"], front.n)
                        dve.tensor_tensor(qk4[:], qk4[:], high4[:], ALU.subtract).then_inc(s["rest4_made"], 1)
                    if tail and g == 2:
                        divide_by_sums(tail, 1, 1)
                    if front and g == 2:
                        flat = terms4[:].rearrange("q w j h m d -> q (w j h) m d")
                        qk_flat = qk4[:].rearrange("q w j (h d) -> q (w j h) d", d=DH)
                        dve.wait_ge(s["high_ps"], front.n)
                        chain.step(dve.tensor_tensor(
                            q_highT[:], ring[0].bitcast(BF16)[:, 0:SEQ].unsqueeze(1).to_broadcast([P, 4, SEQ]), head_mask[:].unsqueeze(2).to_broadcast([P, 4, SEQ]), ALU.mult))
                        dve.tensor_copy(k_highT[:], ring[0].bitcast(BF16)[:, SEQ:2 * SEQ]).then_inc(s["high_out"], 1)
                    if end and g == 2:
                        for j in range(2):
                            n = chain.step(dve.max(top_b[:, j, :], logit[:, j, :]))
                        chain.need(n)
                        for j in range(2):
                            n = chain.step(dve.max_index(top_at_b[:, j, :], top_b[:, j, :], logit[:, j, :]))
                        chain.need(n)
                        n = chain.step(dve.tensor_copy(chosen_b[:], top_at_b[:, :, 0]))
                        chain.need(n)
                        dve.tensor_tensor(onehot_b[:], expert_id[:, 0:E1].unsqueeze(1).to_broadcast([P, 2, E1]), chosen_b[:].unsqueeze(2).to_broadcast([P, 2, E1]), ALU.is_equal).then_inc(s["onehot1_made"], 1)
                        dve.wait_ge(s["onehot1_made"], end.n)
                        n = chain.step(dve.tensor_tensor(prior_b[:, 1, :], prior_b[:, 0, :], onehot_b[:, 0, :], ALU.add))
                        chain.need(n)
                        dve.tensor_tensor(prior_b[:, 2, :], prior_b[:, 1, :], onehot_b[:, 1, :], ALU.add).then_inc(s["prior1_made"], 1)
                    if front and g == 2:
                        tq = terms4[:, 0, :, :, :, :].rearrange("q j h m d -> q (j h) m d")
                        tk = terms4[:, 1, :, :, :, :].rearrange("q j h m d -> q (j h) m d")
                        half_n = 2 * HEADS
                        dve.wait_ge(s["mid4_made"], front.n)
                        high = high4[:].rearrange("q w j (h d) -> q w (j h) d", d=DH)
                        for w, dst in ((0, tq[:, :, 1:4:2, :]), (1, tk[:, :, 2:6:3, :])):
                            chain.step(dve.tensor_copy(dst, high[:, w, :, :].unsqueeze(2).to_broadcast([P, half_n, 2, DH])))
                        chain.step(dve.tensor_copy(tq[:, :, 2, :], tq[:, :, 4, :]))
                        chain.step(dve.tensor_copy(tk[:, :, 1, :], tk[:, :, 4, :]))
                        chain.step(dve.tensor_tensor(tq[:, :, 5, :], qk_flat[:, 0:half_n, :], tq[:, :, 4, :], ALU.subtract))
                        n = chain.step(dve.tensor_tensor(tk[:, :, 3, :], qk_flat[:, half_n:, :], tk[:, :, 4, :], ALU.subtract))
                        chain.need(n)
                        dve.sem_inc(s["terms4_made"], 1)
                    if front and g in (3, 4, 5, 6):
                        for r in range(4):
                            take_maxima(front, 4 * (g - 3) + r)
                    if tail and g == 3:
                        wait(dve, s["sum_made"], tail.n - 2)
                        dve.wait_ge(s["y4_ps"], tail.n)
                        dve.tensor_tensor(x4[tail.p][:], x3_kept[tail.p][:], ring[1][:, 0:2 * D].rearrange("q (j d) -> q j d", j=2), ALU.add).then_inc(s["x4_made"], 1)
                        dve.wait_ge(s["x4_made"], tail.n)
                        moments(x4[tail.p], stats5, meanvar5, "var5")
                    if end and g == 3:
                        dve.wait_ge(s["pos1_ps"], end.n)
                        dve.tensor_tensor(picked_b[:], onehot_b[:], ring[0][:, 0:2 * E1].rearrange("q (j e) -> q j e", j=2), ALU.mult).then_inc(s["pos1_out"], 1)
                        dve.wait_ge(s["pos1_out"], end.n)
                        n = chain.step(dve.tensor_reduce(pos_b[:], picked_b[:], AX, ALU.add))
                        chain.step(dve.tensor_copy(prior_b[:, 0, :], prior_b[:, 2, :]))
                        wait(dve, s["token_sent"][end.p], 32 * (end.k - 1))
                        n = chain.step(dve.tensor_copy(token[end.p][:], token_f[:]))
                        chain.need(n)
                        chain.step(dve.tensor_scalar(token_f[:], token_f[:], float(SEQ), None, ALU.add))
                        dve.scalar_tensor_tensor(slot_b[end.p][:], chosen_b[:], float(TOK), pos_b[:], ALU.mult, ALU.add).then_inc(s["slot1_made"], 1)
                    if fetch and g == 4:
                        wait(dve, s["x3n_made"], fetch.n - 1)
                        dve.wait_ge(s["x3l_landed"][fetch.p], 16 * fetch.k)
                        moments(x3l[fetch.p], stats4, meanvar4, "var4")
                    if att and g == 5:
                        divide_by_sums(att, 0, 0)
                    if tail and g == 5:
                        dve.wait_ge(s["var5"], tail.n)
                        dve.wait_ge(s["rstd5"], tail.n)
                        wait(dve, s["x4_stored"][tail.p], 16 * (tail.k - 1))
                        normed(x4n[tail.p][:, :, D:2 * D], x4[tail.p], meanvar5, rstd5, "x4n_made")
                    if fetch and g == 6:
                        dve.wait_ge(s["var4"], fetch.n)
                        dve.wait_ge(s["rstd4"], fetch.n)
                        wait(dve, s["x4T_ps"], fetch.n - 1)
                        normed(xn4, x3l[fetch.p], meanvar4, rstd4, "xn4_made")
                if fetch or front or tail or end:
                    chain.restart()

            pipeline(dve, half, 5)
            dve.sem_inc(s["all_counted"], 1)
            dve.wait_ge(s["count_ps"], 1)
            n = chain.step(dve.tensor_copy(count[:], bank[7][:, 0:E1]))
            chain.need(n)
            n = chain.step(dve.tensor_tensor(steps[:], count[:].unsqueeze(2).to_broadcast([P, E1, TOK // P]), steps_of[:].unsqueeze(1).to_broadcast([P, E1, TOK // P]), ALU.is_gt))
            chain.need(n)
            n = chain.step(dve.tensor_reduce(blocks_of[:], steps[:], AX, ALU.add))
            chain.need(n)
            n = chain.step(dve.tensor_copy(blocks_to[:], blocks_of[:]))
            chain.need(n)
            for e in range(1, E1):
                n = chain.step(dve.tensor_tensor(blocks_to[:, e:e + 1], blocks_to[:, e:e + 1], blocks_to[:, e - 1:e], ALU.add))
                chain.need(n)
            n = chain.step(dve.tensor_tensor(passed[:], block_id[:].unsqueeze(2).to_broadcast([P, BLOCKS, E1]), blocks_to[:].unsqueeze(1).to_broadcast([P, BLOCKS, E1]), ALU.is_ge))
            chain.need(n)
            n = chain.step(dve.tensor_reduce(block_expert[:], passed[:], AX, ALU.add))
            n = chain.step(dve.tensor_tensor(passed_blocks[:], passed[:], blocks_of[:].unsqueeze(1).to_broadcast([P, BLOCKS, E1]), ALU.mult))
            chain.need(n)
            n = chain.step(dve.tensor_reduce(block_start[:], passed_blocks[:], AX, ALU.add))
            chain.need(n)
            n = chain.step(dve.tensor_tensor(block_row[:], block_id[:], block_start[:], ALU.subtract))
            chain.need(n)
            n = chain.step(dve.tensor_scalar(block_row[:], block_row[:], float(P), None, ALU.mult))
            chain.need(n)
            n = chain.step(dve.scalar_tensor_tensor(block_row[:], block_expert[:], float(TOK), block_row[:], ALU.mult, ALU.add))
            chain.need(n)
            n = chain.step(dve.tensor_scalar(block_row[:], block_row[:], float(NO_ROWS), None, ALU.min))
            chain.step(dve.tensor_scalar(block_expert_i[:], block_expert[:], float(E1 - 1), None, ALU.min))
            chain.need(n)
            n = chain.step(dve.tensor_tensor(own_row[:], block_row[:], ident[:, 0:BLOCKS], ALU.mult))
            chain.need(n)
            n = chain.step(dve.tensor_reduce(block_at[:], own_row[:], AX, ALU.add))
            chain.need(n)
            n = chain.step(dve.tensor_scalar(block_at_i[:], block_at[:], 1.0 / P, None, ALU.mult))
            chain.need(n)
            dve.sem_inc(s["plan_made"], 1)
            dve.wait_ge(s["tokens_landed"], 16)
            dve.tensor_copy(block_tokens_f[:], block_tokens[:]).then_inc(s["tokens_out"], 1)
            dve.wait_ge(s["tokens_ps"], 1)
            dve.tensor_copy(rows_of[:], bank[7][:, 0:BLOCKS]).then_inc(s["rows_made"], 1)
            dve.wait_ge(s["experts_in"], 16 * 4)
            chain.restart()

            def place_weights(pair, p):
                expert = dve.value_load(block_expert_i[0:1, bass.ds(2 * pair + p, 1)], min_val=0, max_val=E1 - 1)
                dve.tensor_copy(wa_now[p][:], wa[:, bass.ds(expert, 1), :].rearrange("q e f -> q (e f)")).then_inc(s["wa_made"], 1)

            def turn(i, last=False):
                for h in range(AHEAD // 2):
                    pair = AHEAD // 2 * i + h
                    for p in range(2):
                        expert = dve.value_load(block_expert_i[0:1, bass.ds(2 * pair + p, 1)], min_val=0, max_val=E1 - 1)
                        dve.wait_ge(s["mid_ps"], 4 * pair + 2 * p + 2)
                        for c in (2, 3):
                            ins = dve.tensor_scalar(mid[p][:, c, :], bank[4 * p + 2][:, (c - 2) * P:(c - 1) * P], ba[:, bass.ds(expert * CHUNKS + c, 1)], 0.0, ALU.add, ALU.max)
                        ins.then_inc(s["mid_dve"], 1)
                        if not last or h < AHEAD // 2 - 1:
                            place_weights(pair + 1, p)
                    for p in range(2):
                        q = 2 * h + p
                        wait(dve, s["res_sent"][q], 16 * i)
                        dve.wait_ge(s["res_ps"], 2 * pair + p + 1)
                        dve.tensor_tensor(res[q][:], got[q][:, 0:D], bank[4 * p + 3][:, 0:D], ALU.add).then_inc(s["res_made"], 1)

            for p in range(2):
                place_weights(0, p)
            turn(0)
            with dve.Fori(1, BLOCKS // AHEAD - 1) as i:
                turn(i)
            turn(BLOCKS // AHEAD - 1, last=True)


_OUT = ((BATCH, SEQ, D), "float32")


def lay_out(inputs):
    import numpy as np

    def get(name):
        return np.asarray(inputs[name])

    eye = np.eye(P, dtype=np.float32)
    return {
        "x": get("L0_attn_x").reshape(TOK, D),
        "eye": eye,
        "upper": np.triu(np.ones((P, P), np.float32), 1),
        "ones": np.ones((P, P), np.float32),
        "ids": np.tile(np.arange(E0, dtype=np.float32), (P, 1)),
        "w_rkvo": np.stack([get("L0_attn_" + n).T for n in ("Wk", "Wv", "Wr", "Wo")], axis=1),
        "time_decay": get("L0_attn_time_decay").reshape(P, 1),
        "time_first": get("L0_attn_time_first").reshape(P, 1),
        "time_mix": get("L0_attn_time_mix").reshape(P, 1),
        "bias0": get("L0_ffn_bias"),
        "gate0_w": get("L0_ffn_gate_w").T,
        "sw13": np.stack([get("L0_ffn_sw1").T, get("L0_ffn_sw3").T], axis=1),
        "sw2": get("L0_ffn_sw2").T,
        "w1": get("L0_ffn_W1").transpose(1, 0, 2),
        "w3": get("L0_ffn_W3").transpose(1, 0, 2),
        "w_qk": np.concatenate([x.reshape(D, HEADS, DK + DV)[:, :, :DK].reshape(D, -1) for x in (get("L1_attn_Wqg"), get("L1_attn_Wkv"))], axis=1),
        "w_v": get("L1_attn_Wkv").reshape(D, HEADS, DK + DV)[:, :, DK:].reshape(D, -1),
        "w_g": get("L1_attn_Wqg").reshape(D, HEADS, DK + DV)[:, :, DK:].reshape(D, -1),
        "w_out": get("L1_attn_Wout").reshape(PAIRS, P, D).transpose(1, 0, 2),
        "w_qkv": np.concatenate([get("L1_ffn_" + n) for n in ("wq", "wk", "wv")], axis=1),
        "b_qkv": np.concatenate([get("L1_ffn_" + n) for n in ("bq", "bk", "bv")]),
        "w_o": get("L1_ffn_wo"),
        "b_o": get("L1_ffn_bo"),
        "gate1_w": get("L1_ffn_gate_w"),
        "gate1_b": get("L1_ffn_gate_b"),
        "norms": np.stack([get("L1_ffn_" + n) for n in ("ln1_g", "ln1_b", "ln2_g", "ln2_b")], axis=1),
        "head_mask": (np.arange(P)[:, None] // DH % 4 == np.arange(4)[None, :]).astype(np.float32),
        "token_start": (np.arange(P)[:, None] + P * np.arange(2)[None, :]).astype(np.float32),
        "steps_of": (P * np.arange(TOK // P)).astype(np.float32),
        "block_id": np.arange(BLOCKS, dtype=np.float32),
        "wa": get("L1_ffn_w1"),
        "wb": get("L1_ffn_w2"),
        "ba": get("L1_ffn_b1").reshape(E1 * CHUNKS, P).T,
        "bb": get("L1_ffn_b2").reshape(1, E1 * D),
        "w2": get("L0_ffn_W2").reshape(E0 * I0, D),
    }


def kernel(**inputs):
    import numpy as np
    import concourse.bacc as bacc
    from concourse import mybir as my
    from concourse.bass_utils import run_bass_kernel_spmd

    nc = bacc.Bacc("TRN2", target_bir_lowering=False, num_devices=1)
    arrays, aps = {}, {}
    for name, value in lay_out(inputs).items():
        value = np.ascontiguousarray(value)
        arrays["in_" + name] = value
        aps[name] = nc.dram_tensor("in_" + name, value.shape, my.dt.from_np(value.dtype), kind="ExternalInput").ap()
    out = nc.dram_tensor("out_0", (TOK, D), my.dt.float32, kind="ExternalOutput").ap()
    build_program(nc, aps, out)
    result = run_bass_kernel_spmd(nc, [arrays], core_ids=[0])
    return result.results[0]["out_0"].reshape(_OUT[0])
```
